# Optimizing a Trainium2 kernel written in Bass

```python
import numpy as np
import jax
import jax.numpy as jnp

def _softmax(x, axis=-1):
    return jax.nn.softmax(x, axis=axis)

def _gelu(x):
    return jax.nn.gelu(x, approximate=True)

def _silu(x):
    return jax.nn.silu(x)

def _sigmoid(x):
    return jax.nn.sigmoid(x)

def _layernorm(x, axis=-1, eps=1e-05):
    m = jnp.mean(x, axis=axis, keepdims=True)
    v = jnp.var(x, axis=axis, keepdims=True)
    return (x - m) / jnp.sqrt(v + eps)

def _scatter_add(tgt, idx, src, axis=0):
    return tgt.at[idx].add(src)

def _segment_sum(src, seg, n):
    return jax.ops.segment_sum(src, seg, n)
kernel_name = 'mk_audio_tower_d2_tok_audfeat512_r4_1bb3fd'

def setup_inputs(seed: int=0):
    np.random.seed(seed)
    _w = jnp.asarray

    def _rec_inputs():
        import jax
        import jax.numpy as jnp
        _rk = jax.random.key(seed)
        x = -0.000356955 + 1 * jax.random.normal(jax.random.fold_in(_rk, 1), (64, 196, 96), jnp.float32)
        return x
    x = _rec_inputs()

    def _L0_tok_setup():
        import jax, jax.numpy as jnp
        import numpy as np
        import itertools
        B, RES, RES_, STRIDE = (64, 14, 7, 2)
        N, N_ = (RES * RES, RES_ * RES_)
        IN_DIM, OUT_DIM = (96, 128)
        H, KD, AR = (12, 32, 2)
        D = AR * KD
        DH = D * H
        NH_KD = KD * H
        KV_H = DH + NH_KD
        EPS = 1e-05

        def _bias_idxs():
            points = list(itertools.product(range(RES), range(RES)))
            points_ = list(itertools.product(range(RES_), range(RES_)))
            offsets, idxs = ({}, [])
            for p1 in points_:
                for p2 in points:
                    off = (abs(p1[0] * STRIDE - p2[0]), abs(p1[1] * STRIDE - p2[1]))
                    if off not in offsets:
                        offsets[off] = len(offsets)
                    idxs.append(offsets[off])
            return (np.array(idxs, dtype=np.int32).reshape(N_, N), len(offsets))

        def linear_bn(x, w, gamma, beta, mean, var):
            s = gamma / jnp.sqrt(var + EPS)
            return jnp.matmul(x, w.T) * s + (beta - mean * s)
        key = jax.random.key(seed)
        ks = jax.random.split(key, 12)
        idxs_np, n_off = _bias_idxs()

        def bn_params(k, dim):
            k1, k2, k3, k4 = jax.random.split(k, 4)
            return (jax.random.normal(k1, (dim,)) * 0.1 + 1.0, jax.random.normal(k2, (dim,)) * 0.1, jax.random.normal(k3, (dim,)) * 0.1, jax.random.uniform(k4, (dim,), minval=0.5, maxval=1.5))
        kv_g, kv_b, kv_m, kv_v = bn_params(ks[1], KV_H)
        q_g, q_b, q_m, q_v = bn_params(ks[3], NH_KD)
        pr_g, pr_b, pr_m, pr_v = bn_params(ks[5], OUT_DIM)
        return {'x': jax.random.normal(ks[0], (B, N, IN_DIM), dtype=jnp.float32), 'kv_w': jax.random.normal(ks[6], (KV_H, IN_DIM), dtype=jnp.float32) * IN_DIM ** (-0.5), 'kv_g': kv_g, 'kv_b': kv_b, 'kv_m': kv_m, 'kv_v': kv_v, 'q_w': jax.random.normal(ks[7], (NH_KD, IN_DIM), dtype=jnp.float32) * IN_DIM ** (-0.5), 'q_g': q_g, 'q_b': q_b, 'q_m': q_m, 'q_v': q_v, 'proj_w': jax.random.normal(ks[8], (OUT_DIM, DH), dtype=jnp.float32) * DH ** (-0.5), 'proj_g': pr_g, 'proj_b': pr_b, 'proj_m': pr_m, 'proj_v': pr_v, 'attention_biases': jax.random.normal(ks[9], (H, n_off), dtype=jnp.float32) * 0.02, 'bias_idxs': jnp.asarray(idxs_np)}
    _L0_tok_all = _L0_tok_setup()
    _L0_tok_in = {k: v for k, v in _L0_tok_all.items() if k in ('kv_w', 'kv_g', 'kv_b', 'kv_m', 'kv_v', 'q_w', 'q_g', 'q_b', 'q_m', 'q_v', 'proj_w', 'proj_g', 'proj_b', 'proj_m', 'proj_v', 'attention_biases', 'bias_idxs')}
    del _L0_tok_all

    def _L0_attn_setup():
        import jax, jax.numpy as jnp
        import numpy as np
        D_MODEL = 128
        NUM_HEADS = 8
        D_HEAD = 64
        BATCH = 2
        SEQ = 512
        NEG_BIG = 10000000000.0
        key = jax.random.key(seed)
        k1, k2, k3, k4, k5 = jax.random.split(key, 5)
        scale = D_MODEL ** (-0.5)
        return {'x': jax.random.normal(k1, (BATCH, SEQ, D_MODEL), dtype=jnp.float32), 'W_Q': jax.random.normal(k2, (NUM_HEADS, D_HEAD, D_MODEL), dtype=jnp.float32) * scale, 'W_K': jax.random.normal(k3, (NUM_HEADS, D_HEAD, D_MODEL), dtype=jnp.float32) * scale, 'W_V': jax.random.normal(k4, (NUM_HEADS, D_HEAD, D_MODEL), dtype=jnp.float32) * scale, 'W_O': jax.random.normal(k5, (D_MODEL, D_HEAD * NUM_HEADS), dtype=jnp.float32) * scale}
    _L0_attn_all = _L0_attn_setup()
    _L0_attn_in = {k: v for k, v in _L0_attn_all.items() if k in ('W_Q', 'W_K', 'W_V', 'W_O')}
    del _L0_attn_all

    def _L0_ffn_setup():
        import jax, jax.numpy as jnp
        import numpy as np
        B, S, H, E, F = (4, 512, 128, 8, 128)
        key = jax.random.key(seed)
        k = jax.random.split(key, 7)
        x = jax.random.normal(k[0], (B, S, H), dtype=jnp.float32)
        Wr = jax.random.normal(k[1], (H, E), dtype=jnp.float32) / np.sqrt(H)
        br = jnp.zeros((E,), dtype=jnp.float32)
        W1 = jax.random.normal(k[2], (E, H, F), dtype=jnp.float32) / np.sqrt(H)
        b1 = jnp.zeros((E, F), dtype=jnp.float32)
        W2 = jax.random.normal(k[3], (E, F, H), dtype=jnp.float32) / np.sqrt(F)
        b2 = jnp.zeros((E, H), dtype=jnp.float32)
        return {'x': x, 'Wr': Wr, 'br': br, 'W1': W1, 'b1': b1, 'W2': W2, 'b2': b2}
    _L0_ffn_all = _L0_ffn_setup()
    _L0_ffn_in = {k: v for k, v in _L0_ffn_all.items() if k in ('Wr', 'br', 'W1', 'b1', 'W2', 'b2')}
    del _L0_ffn_all

    def _L1_attn_setup():
        import jax, jax.numpy as jnp
        import numpy as np
        H, HEADS, LAYERS = (128, 4, 3)
        HD = H // HEADS
        FFN = 4 * H
        B, S = (4, 512)
        EPS = 1e-05
        SCALE_BASE = 512.0
        GAMMAS = (1.0 - np.exp(np.linspace(np.log(1.0 / 32.0), np.log(1.0 / 512.0), HEADS))).astype(np.float32)

        def _xpos(x, downscale):
            L, d = (x.shape[-2], x.shape[-1])
            half = d // 2
            s = (jnp.arange(half, dtype=jnp.float32) + 0.4 * d) / (1.4 * d)
            pos = jnp.arange(L, dtype=jnp.float32)
            scale = s[None, :] ** (pos[:, None] / SCALE_BASE)
            inv_freq = 1.0 / 10000.0 ** (jnp.arange(half, dtype=jnp.float32) / half)
            ang = pos[:, None] * inv_freq[None, :]
            if downscale:
                scale = 1.0 / scale
            sin_s = jnp.repeat(jnp.sin(ang) * scale, 2, axis=-1)
            cos_s = jnp.repeat(jnp.cos(ang) * scale, 2, axis=-1)
            x1, x2 = (x[..., 0::2], x[..., 1::2])
            rot = jnp.stack([-x2, x1], axis=-1).reshape(x.shape)
            return x * cos_s + rot * sin_s

        def _layernorm(x, w, b):
            m = x.mean(-1, keepdims=True)
            v = ((x - m) ** 2).mean(-1, keepdims=True)
            return (x - m) / jnp.sqrt(v + EPS) * w + b

        def _decay_mask(L):
            n = jnp.arange(L)
            nm = n[:, None] - n[None, :]
            g = jnp.asarray(GAMMAS)
            return jnp.where((nm >= 0)[None], g[:, None, None] ** jnp.maximum(nm, 0)[None], 0.0)

        def _msr(X, WQ, WK, WV, WG, WO, gnw, gnb, D):
            Q = _xpos(jnp.einsum('bsh,nhd->bnsd', X, WQ), False)
            K = _xpos(jnp.einsum('bsh,nhd->bnsd', X, WK), True)
            V = jnp.einsum('bsh,nhd->bnsd', X, WV)
            A = jnp.einsum('bnsd,bntd->bnst', Q, K) * D[None]
            Y = jnp.einsum('bnst,bntd->bnsd', A, V)
            Y = jnp.transpose(Y, (0, 2, 1, 3))
            m = Y.mean(-1, keepdims=True)
            v = ((Y - m) ** 2).mean(-1, keepdims=True)
            Yn = ((Y - m) / jnp.sqrt(v + EPS)).reshape(X.shape[0], X.shape[1], H) * gnw + gnb
            G = X @ WG
            return G * jax.nn.sigmoid(G) * Yn @ WO

        def _reference_tuple_inner(X, WQ, WK, WV, WG, WO, gn_w, gn_b, ln1_w, ln1_b, ln2_w, ln2_b, ffn_w1, ffn_b1, ffn_w2, ffn_b2):
            D = _decay_mask(X.shape[1])
            for l in range(LAYERS):
                Y = _msr(_layernorm(X, ln1_w[l], ln1_b[l]), WQ[l], WK[l], WV[l], WG[l], WO[l], gn_w[l], gn_b[l], D) + X
                Hn = _layernorm(Y, ln2_w[l], ln2_b[l])
                X = jax.nn.gelu(Hn @ ffn_w1[l] + ffn_b1[l], approximate=False) @ ffn_w2[l] + ffn_b2[l] + Y
            return (X, jnp.einsum('bsh,bth->bst', X, X))
        key = jax.random.key(seed)
        ks = jax.random.split(key, 10)
        rn = lambda k, shape, sc: jax.random.normal(k, shape, jnp.float32) * sc
        return {'X': rn(ks[0], (B, S, H), 1.0), 'WQ': rn(ks[1], (LAYERS, HEADS, H, HD), 1.0 / H), 'WK': rn(ks[2], (LAYERS, HEADS, H, HD), 1.0 / H), 'WV': rn(ks[3], (LAYERS, HEADS, H, HD), 1.0 / H), 'WG': rn(ks[4], (LAYERS, H, H), 1.0 / H), 'WO': rn(ks[5], (LAYERS, H, H), 1.0 / H), 'gn_w': jnp.ones((LAYERS, H), jnp.float32), 'gn_b': jnp.zeros((LAYERS, H), jnp.float32), 'ln1_w': jnp.ones((LAYERS, H), jnp.float32), 'ln1_b': jnp.zeros((LAYERS, H), jnp.float32), 'ln2_w': jnp.ones((LAYERS, H), jnp.float32), 'ln2_b': jnp.zeros((LAYERS, H), jnp.float32), 'ffn_w1': rn(ks[6], (LAYERS, H, FFN), (2.0 / (H + FFN)) ** 0.5), 'ffn_b1': jnp.zeros((LAYERS, FFN), jnp.float32), 'ffn_w2': rn(ks[7], (LAYERS, FFN, H), (2.0 / (H + FFN)) ** 0.5), 'ffn_b2': jnp.zeros((LAYERS, H), jnp.float32)}
    _L1_attn_all = _L1_attn_setup()
    _L1_attn_in = {k: v for k, v in _L1_attn_all.items() if k in ('WQ', 'WK', 'WV', 'WG', 'WO', 'gn_w', 'gn_b', 'ln1_w', 'ln1_b', 'ln2_w', 'ln2_b', 'ffn_w1', 'ffn_b1', 'ffn_w2', 'ffn_b2')}
    del _L1_attn_all

    def _L1_ffn_setup():
        import jax, jax.numpy as jnp
        import numpy as np
        E = 64
        K = 2
        CAP = 128
        H = 128
        FFN = 512
        B, S = (8, 1024)
        key = jax.random.key(seed)
        ks = jax.random.split(key, 6)
        hidden_states = jax.random.normal(ks[0], (B, S, H), dtype=jnp.float32)
        router_w = jax.random.normal(ks[1], (E, H), dtype=jnp.float32) * (0.01 / np.sqrt(H))
        w1 = jax.random.normal(ks[2], (FFN, H), dtype=jnp.float32) * (1.0 / np.sqrt(H))
        b1 = jnp.zeros((FFN,), dtype=jnp.float32)
        w2 = jax.random.normal(ks[3], (H, FFN), dtype=jnp.float32) * (1.0 / np.sqrt(FFN))
        b2 = jnp.zeros((H,), dtype=jnp.float32)
        return {'hidden_states': hidden_states, 'router_w': router_w, 'w1': w1, 'b1': b1, 'w2': w2, 'b2': b2}
    _L1_ffn_all = _L1_ffn_setup()
    _L1_ffn_in = {k: v for k, v in _L1_ffn_all.items() if k in ('router_w', 'w1', 'b1', 'w2', 'b2')}
    del _L1_ffn_all
    return {'x': x, 'L0_tok_kv_w': _L0_tok_in['kv_w'], 'L0_tok_kv_g': _L0_tok_in['kv_g'], 'L0_tok_kv_b': _L0_tok_in['kv_b'], 'L0_tok_kv_m': _L0_tok_in['kv_m'], 'L0_tok_kv_v': _L0_tok_in['kv_v'], 'L0_tok_q_w': _L0_tok_in['q_w'], 'L0_tok_q_g': _L0_tok_in['q_g'], 'L0_tok_q_b': _L0_tok_in['q_b'], 'L0_tok_q_m': _L0_tok_in['q_m'], 'L0_tok_q_v': _L0_tok_in['q_v'], 'L0_tok_proj_w': _L0_tok_in['proj_w'], 'L0_tok_proj_g': _L0_tok_in['proj_g'], 'L0_tok_proj_b': _L0_tok_in['proj_b'], 'L0_tok_proj_m': _L0_tok_in['proj_m'], 'L0_tok_proj_v': _L0_tok_in['proj_v'], 'L0_tok_attention_biases': _L0_tok_in['attention_biases'], 'L0_tok_bias_idxs': _L0_tok_in['bias_idxs'], 'L0_attn_W_Q': _L0_attn_in['W_Q'], 'L0_attn_W_K': _L0_attn_in['W_K'], 'L0_attn_W_V': _L0_attn_in['W_V'], 'L0_attn_W_O': _L0_attn_in['W_O'], 'L0_ffn_Wr': _L0_ffn_in['Wr'], 'L0_ffn_br': _L0_ffn_in['br'], 'L0_ffn_W1': _L0_ffn_in['W1'], 'L0_ffn_b1': _L0_ffn_in['b1'], 'L0_ffn_W2': _L0_ffn_in['W2'], 'L0_ffn_b2': _L0_ffn_in['b2'], 'L1_attn_WQ': _L1_attn_in['WQ'], 'L1_attn_WK': _L1_attn_in['WK'], 'L1_attn_WV': _L1_attn_in['WV'], 'L1_attn_WG': _L1_attn_in['WG'], 'L1_attn_WO': _L1_attn_in['WO'], 'L1_attn_gn_w': _L1_attn_in['gn_w'], 'L1_attn_gn_b': _L1_attn_in['gn_b'], 'L1_attn_ln1_w': _L1_attn_in['ln1_w'], 'L1_attn_ln1_b': _L1_attn_in['ln1_b'], 'L1_attn_ln2_w': _L1_attn_in['ln2_w'], 'L1_attn_ln2_b': _L1_attn_in['ln2_b'], 'L1_attn_ffn_w1': _L1_attn_in['ffn_w1'], 'L1_attn_ffn_b1': _L1_attn_in['ffn_b1'], 'L1_attn_ffn_w2': _L1_attn_in['ffn_w2'], 'L1_attn_ffn_b2': _L1_attn_in['ffn_b2'], 'L1_ffn_router_w': _L1_ffn_in['router_w'], 'L1_ffn_w1': _L1_ffn_in['w1'], 'L1_ffn_b1': _L1_ffn_in['b1'], 'L1_ffn_w2': _L1_ffn_in['w2'], 'L1_ffn_b2': _L1_ffn_in['b2']}

def reference(x, L0_tok_kv_w, L0_tok_kv_g, L0_tok_kv_b, L0_tok_kv_m, L0_tok_kv_v, L0_tok_q_w, L0_tok_q_g, L0_tok_q_b, L0_tok_q_m, L0_tok_q_v, L0_tok_proj_w, L0_tok_proj_g, L0_tok_proj_b, L0_tok_proj_m, L0_tok_proj_v, L0_tok_attention_biases, L0_tok_bias_idxs, L0_attn_W_Q, L0_attn_W_K, L0_attn_W_V, L0_attn_W_O, L0_ffn_Wr, L0_ffn_br, L0_ffn_W1, L0_ffn_b1, L0_ffn_W2, L0_ffn_b2, L1_attn_WQ, L1_attn_WK, L1_attn_WV, L1_attn_WG, L1_attn_WO, L1_attn_gn_w, L1_attn_gn_b, L1_attn_ln1_w, L1_attn_ln1_b, L1_attn_ln2_w, L1_attn_ln2_b, L1_attn_ffn_w1, L1_attn_ffn_b1, L1_attn_ffn_w2, L1_attn_ffn_b2, L1_ffn_router_w, L1_ffn_w1, L1_ffn_b1, L1_ffn_w2, L1_ffn_b2):
    import jax
    import jax.numpy as jnp

    def _L0_tok_ref(x, kv_w, kv_g, kv_b, kv_m, kv_v, q_w, q_g, q_b, q_m, q_v, proj_w, proj_g, proj_b, proj_m, proj_v, attention_biases, bias_idxs):
        import jax, jax.numpy as jnp
        import numpy as np
        import itertools
        B, RES, RES_, STRIDE = (64, 14, 7, 2)
        N, N_ = (RES * RES, RES_ * RES_)
        IN_DIM, OUT_DIM = (96, 128)
        H, KD, AR = (12, 32, 2)
        D = AR * KD
        DH = D * H
        NH_KD = KD * H
        KV_H = DH + NH_KD
        EPS = 1e-05

        def _bias_idxs():
            points = list(itertools.product(range(RES), range(RES)))
            points_ = list(itertools.product(range(RES_), range(RES_)))
            offsets, idxs = ({}, [])
            for p1 in points_:
                for p2 in points:
                    off = (abs(p1[0] * STRIDE - p2[0]), abs(p1[1] * STRIDE - p2[1]))
                    if off not in offsets:
                        offsets[off] = len(offsets)
                    idxs.append(offsets[off])
            return (np.array(idxs, dtype=np.int32).reshape(N_, N), len(offsets))

        def linear_bn(x, w, gamma, beta, mean, var):
            s = gamma / jnp.sqrt(var + EPS)
            return jnp.matmul(x, w.T) * s + (beta - mean * s)
        Bsz = x.shape[0]
        scale = KD ** (-0.5)
        kv = linear_bn(x, kv_w, kv_g, kv_b, kv_m, kv_v).reshape(Bsz, N, H, KD + D)
        k, v = (kv[..., :KD], kv[..., KD:])
        xs = x.reshape(Bsz, RES, RES, IN_DIM)[:, ::STRIDE, ::STRIDE].reshape(Bsz, N_, IN_DIM)
        q = linear_bn(xs, q_w, q_g, q_b, q_m, q_v).reshape(Bsz, N_, H, KD)
        bias = attention_biases[:, bias_idxs]
        attn = jnp.einsum('bqhd,bkhd->bhqk', q, k) * scale + bias
        attn = jax.nn.softmax(attn, axis=-1)
        out = jnp.einsum('bhqk,bkhd->bqhd', attn, v).reshape(Bsz, N_, DH)
        out = jax.nn.hard_swish(out)
        return linear_bn(out, proj_w, proj_g, proj_b, proj_m, proj_v)

    def _L0_attn_ref(x, W_Q, W_K, W_V, W_O):
        import jax, jax.numpy as jnp
        import numpy as np
        D_MODEL = 128
        NUM_HEADS = 8
        D_HEAD = 64
        BATCH = 2
        SEQ = 512
        NEG_BIG = 10000000000.0
        b, n, d = x.shape
        q = jnp.einsum('ihd,bpd->biph', W_Q, x)
        k = jnp.einsum('ihd,bpd->biph', W_K, x)
        v = jnp.einsum('ihd,bpd->biph', W_V, x)
        scores = jnp.einsum('biph,biqh->biqp', k, q)
        tril = jnp.tril(jnp.ones((n, n), dtype=scores.dtype))
        triu = jnp.triu(jnp.ones((n, n), dtype=scores.dtype))
        masked = scores * tril - NEG_BIG * (1.0 - triu)
        attn = jax.nn.softmax(masked / D_HEAD ** 0.5, axis=-1)
        z = jnp.einsum('biph,biqp->biqh', v, attn)
        z_flat = jnp.transpose(z, (0, 2, 1, 3)).reshape(b, n, -1)
        out = jnp.einsum('df,bqf->bqd', W_O, z_flat)
        return out

    def _L0_ffn_ref(x, Wr, br, W1, b1, W2, b2):
        import jax, jax.numpy as jnp
        import numpy as np
        B, S, H, E, F = (4, 512, 128, 8, 128)
        b, s, h = x.shape
        xt = x.reshape(-1, h)
        logits = xt @ Wr + br
        probs = jax.nn.softmax(logits, axis=-1)
        G = jnp.max(probs, axis=-1)
        idx = jnp.argmax(probs, axis=-1)
        h1 = jax.nn.relu(jnp.einsum('nh,ehf->nef', xt, W1) + b1)
        eo = jnp.einsum('nef,efh->neh', h1, W2) + b2
        Eout = jnp.take_along_axis(eo, idx[:, None, None], axis=1)[:, 0, :]
        y = G[:, None] * Eout
        return y.reshape(b, s, h)

    def _L1_attn_ref(X, WQ, WK, WV, WG, WO, gn_w, gn_b, ln1_w, ln1_b, ln2_w, ln2_b, ffn_w1, ffn_b1, ffn_w2, ffn_b2):
        import jax, jax.numpy as jnp
        import numpy as np
        H, HEADS, LAYERS = (128, 4, 3)
        HD = H // HEADS
        FFN = 4 * H
        B, S = (4, 512)
        EPS = 1e-05
        SCALE_BASE = 512.0
        GAMMAS = (1.0 - np.exp(np.linspace(np.log(1.0 / 32.0), np.log(1.0 / 512.0), HEADS))).astype(np.float32)

        def _xpos(x, downscale):
            L, d = (x.shape[-2], x.shape[-1])
            half = d // 2
            s = (jnp.arange(half, dtype=jnp.float32) + 0.4 * d) / (1.4 * d)
            pos = jnp.arange(L, dtype=jnp.float32)
            scale = s[None, :] ** (pos[:, None] / SCALE_BASE)
            inv_freq = 1.0 / 10000.0 ** (jnp.arange(half, dtype=jnp.float32) / half)
            ang = pos[:, None] * inv_freq[None, :]
            if downscale:
                scale = 1.0 / scale
            sin_s = jnp.repeat(jnp.sin(ang) * scale, 2, axis=-1)
            cos_s = jnp.repeat(jnp.cos(ang) * scale, 2, axis=-1)
            x1, x2 = (x[..., 0::2], x[..., 1::2])
            rot = jnp.stack([-x2, x1], axis=-1).reshape(x.shape)
            return x * cos_s + rot * sin_s

        def _layernorm(x, w, b):
            m = x.mean(-1, keepdims=True)
            v = ((x - m) ** 2).mean(-1, keepdims=True)
            return (x - m) / jnp.sqrt(v + EPS) * w + b

        def _decay_mask(L):
            n = jnp.arange(L)
            nm = n[:, None] - n[None, :]
            g = jnp.asarray(GAMMAS)
            return jnp.where((nm >= 0)[None], g[:, None, None] ** jnp.maximum(nm, 0)[None], 0.0)

        def _msr(X, WQ, WK, WV, WG, WO, gnw, gnb, D):
            Q = _xpos(jnp.einsum('bsh,nhd->bnsd', X, WQ), False)
            K = _xpos(jnp.einsum('bsh,nhd->bnsd', X, WK), True)
            V = jnp.einsum('bsh,nhd->bnsd', X, WV)
            A = jnp.einsum('bnsd,bntd->bnst', Q, K) * D[None]
            Y = jnp.einsum('bnst,bntd->bnsd', A, V)
            Y = jnp.transpose(Y, (0, 2, 1, 3))
            m = Y.mean(-1, keepdims=True)
            v = ((Y - m) ** 2).mean(-1, keepdims=True)
            Yn = ((Y - m) / jnp.sqrt(v + EPS)).reshape(X.shape[0], X.shape[1], H) * gnw + gnb
            G = X @ WG
            return G * jax.nn.sigmoid(G) * Yn @ WO

        def _reference_tuple_inner(X, WQ, WK, WV, WG, WO, gn_w, gn_b, ln1_w, ln1_b, ln2_w, ln2_b, ffn_w1, ffn_b1, ffn_w2, ffn_b2):
            D = _decay_mask(X.shape[1])
            for l in range(LAYERS):
                Y = _msr(_layernorm(X, ln1_w[l], ln1_b[l]), WQ[l], WK[l], WV[l], WG[l], WO[l], gn_w[l], gn_b[l], D) + X
                Hn = _layernorm(Y, ln2_w[l], ln2_b[l])
                X = jax.nn.gelu(Hn @ ffn_w1[l] + ffn_b1[l], approximate=False) @ ffn_w2[l] + ffn_b2[l] + Y
            return (X, jnp.einsum('bsh,bth->bst', X, X))
        return _reference_tuple_inner(X, WQ, WK, WV, WG, WO, gn_w, gn_b, ln1_w, ln1_b, ln2_w, ln2_b, ffn_w1, ffn_b1, ffn_w2, ffn_b2)[0]

    def _L1_ffn_ref(hidden_states, router_w, w1, b1, w2, b2):
        import jax, jax.numpy as jnp
        import numpy as np
        E = 64
        K = 2
        CAP = 128
        H = 128
        FFN = 512
        B, S = (8, 1024)
        orig_shape = hidden_states.shape
        x = hidden_states.reshape(-1, orig_shape[-1])
        T = x.shape[0]
        N = T * K
        logits = jnp.einsum('th,eh->te', x, router_w)
        probs_full = jax.nn.softmax(logits, axis=-1)
        probs, idx = jax.lax.top_k(probs_full, K)
        flat_e = idx.reshape(-1)
        flat_p = probs.reshape(-1)
        order = jnp.argsort(flat_e, stable=True)
        sorted_e = flat_e[order]
        counts = jnp.zeros((E,), jnp.int32).at[flat_e].add(1)
        offsets = jnp.concatenate([jnp.zeros((1,), jnp.int32), jnp.cumsum(counts)[:-1]])
        pos = jnp.arange(N, dtype=jnp.int32) - offsets[sorted_e]
        keep = pos < CAP
        slot = sorted_e * CAP + jnp.minimum(pos, CAP - 1)
        dest = jnp.where(keep, slot, E * CAP)
        tok = order // K
        buf = jnp.zeros((E * CAP + 1, x.shape[-1]), x.dtype).at[dest].set(x[tok])
        buf = buf[:-1]
        h = jax.nn.gelu(jnp.einsum('nh,fh->nf', buf, w1) + b1, approximate=False)
        y = jnp.einsum('nf,hf->nh', h, w2) + b2
        gate = jnp.where(keep, flat_p[order], 0.0)
        contrib = y[jnp.minimum(slot, E * CAP - 1)] * gate[:, None]
        out = jnp.zeros_like(x).at[tok].add(contrib)
        return out.reshape(orig_shape)
    h = _L0_tok_ref(x, L0_tok_kv_w, L0_tok_kv_g, L0_tok_kv_b, L0_tok_kv_m, L0_tok_kv_v, L0_tok_q_w, L0_tok_q_g, L0_tok_q_b, L0_tok_q_m, L0_tok_q_v, L0_tok_proj_w, L0_tok_proj_g, L0_tok_proj_b, L0_tok_proj_m, L0_tok_proj_v, L0_tok_attention_biases, L0_tok_bias_idxs)
    h = h + _L0_attn_ref(_layernorm(h, axis=-1), L0_attn_W_Q, L0_attn_W_K, L0_attn_W_V, L0_attn_W_O)
    h = h + _L0_ffn_ref(_layernorm(h, axis=-1), L0_ffn_Wr, L0_ffn_br, L0_ffn_W1, L0_ffn_b1, L0_ffn_W2, L0_ffn_b2)
    h = h + _L1_attn_ref(_layernorm(h, axis=-1), L1_attn_WQ, L1_attn_WK, L1_attn_WV, L1_attn_WG, L1_attn_WO, L1_attn_gn_w, L1_attn_gn_b, L1_attn_ln1_w, L1_attn_ln1_b, L1_attn_ln2_w, L1_attn_ln2_b, L1_attn_ffn_w1, L1_attn_ffn_b1, L1_attn_ffn_w2, L1_attn_ffn_b2)
    h = h + _L1_ffn_ref(_layernorm(h, axis=-1), L1_ffn_router_w, L1_ffn_w1, L1_ffn_b1, L1_ffn_w2, L1_ffn_b2)
    return h

_drawn_inputs = setup_inputs


def setup_inputs(seed=0):
    import zlib

    import numpy as np

    out = dict(_drawn_inputs(seed))
    spreads = {'L0_ffn_br': (0.0, 0.469),
     'L0_ffn_b1': (0.0, 0.451),
     'L0_ffn_b2': (0.0, 0.3),
     'L1_attn_gn_w': (1.0, 0.6),
     'L1_attn_gn_b': (0.0, 0.8),
     'L1_attn_ln1_w': (1.0, 0.6),
     'L1_attn_ln1_b': (0.0, 0.8),
     'L1_attn_ln2_w': (1.0, 0.2),
     'L1_attn_ln2_b': (0.0, 0.1),
     'L1_attn_ffn_b1': (0.0, 0.1),
     'L1_attn_ffn_b2': (0.0, 0.1),
     'L1_ffn_b1': (0.0, 2.0),
     'L1_ffn_b2': (0.0, 2.0)}
    factors = {'L0_tok_attention_biases': 8.0,
     'L1_attn_WQ': 8.0,
     'L1_attn_WK': 8.0,
     'L1_attn_WV': 8.0,
     'L1_attn_WG': 8.0,
     'L1_attn_WO': 8.0,
     'L1_ffn_router_w': 8.0,
     'L1_ffn_w1': 8.0,
     'L1_ffn_w2': 8.0}
    for name, (base, spread) in spreads.items():
        noise = np.random.default_rng([zlib.crc32(name.encode()), seed]).standard_normal(out[name].shape)
        drawn = base * np.exp(spread * noise) if base else spread * noise
        out[name] = jnp.asarray(drawn.astype(out[name].dtype))
    for name, factor in factors.items():
        out[name] = (out[name] * factor).astype(out[name].dtype)
    return out
```

```python
from contextlib import ExitStack

import concourse.bass as bass
from concourse import mybir
import numpy as np

F32 = mybir.dt.float32
BF16 = mybir.dt.bfloat16
I32 = mybir.dt.int32
ALU = mybir.AluOpType
ACT = mybir.ActivationFunctionType
AX = mybir.AxisListType

B, N, NQ = 64, 196, 49
D_IN, D = 96, 128
H0, KD, VD = 12, 32, 64
HALF = N // 2
TOK = 2 * NQ
TILES = B * NQ // TOK
AUG = D_IN + 1
OFFS = 196
PAIRS = H0 // 2
EPS = 1e-5
LOWEST = -3.0e38
BANK = 512

CONSTS = {}


def _constants():
    p = np.arange(128)
    parts = []

    def put(name, a):
        full = np.zeros((128,) + a.shape[1:], np.float32)
        full[:a.shape[0]] = a
        full = full.reshape(128, -1)
        at = sum(x.shape[1] for x in parts)
        CONSTS[name] = (at, at + full.shape[1])
        parts.append(full)

    put("entry", np.stack([p, p + HALF], 1).astype(np.float32))
    put("ident", np.eye(128, dtype=np.float32))
    t = np.arange(TOK)
    same = (t[:, None] // NQ) == (t[None, :] // NQ)
    put("after", (same & (t[:, None] > t[None, :])).astype(np.float32))
    put("before", (t[:, None] < t[None, :]).astype(np.float32))
    later = (NQ - 1 - t % NQ).astype(np.float32)
    put("later", later[:, None])
    put("floor", np.where(later > 0, 0.0, LOWEST).astype(np.float32)[:, None])
    put("rank8", np.tile(8.0 - np.arange(8), (TOK, 1)))
    put("rank64", np.tile(64.0 - np.arange(64), (TOK, 1)))
    put("sel", np.repeat(np.eye(8)[:, :, None], D, 2))
    heads, hd = 4, 32
    gam = (1.0 - np.exp(np.linspace(np.log(1.0 / 32.0), np.log(1.0 / 512.0), heads))).astype(np.float32)
    nm = t[None, :] - t[:, None]
    dec = np.where((same & (nm >= 0))[:, None, :],
                   gam.astype(np.float64)[None, :, None] ** np.maximum(nm, 0)[:, None, :], 0.0)
    put("decay", dec.astype(np.float32))
    half = hd // 2
    s = (np.arange(half) + 0.4 * hd) / (1.4 * hd)
    pos = np.arange(NQ)
    scale = s[:, None] ** (pos[None, :] / 512.0)
    ang = pos[None, :] / 10000.0 ** (np.arange(half)[:, None] / half)
    for name, sc in (("q", scale), ("k", 1.0 / scale)):
        cos = np.repeat(np.cos(ang) * sc, 2, 0)
        sin = np.repeat(np.sin(ang) * sc, 2, 0)
        sin[0::2] *= -1.0
        put("cos" + name, np.tile(cos, (heads, 1)).astype(np.float32))
        put("sin" + name, np.tile(sin, (heads, 1)).astype(np.float32))
    return np.ascontiguousarray(np.concatenate(parts, 1))


CONST_ARRAY = _constants()


def known(v):
    return isinstance(v, (int, float))


def positive(count):
    return not known(count) or count > 0


def stand(eng, passed):
    eng.sem_inc(passed, 1)


def load_features(sp, io, mem, i, par):
    x = io["xT"].rearrange("d (i q b) k -> i q d b k", q=2, b=4)
    sp.dma_start(mem["xT"][0:D_IN, par, :, :], x[i, par]).then_inc(mem["xT_in"][par], 16)


def load_tokens(sp, io, mem, i, par):
    x = io["x"].rearrange("(i q b) (p t) d -> i q b p t d", q=2, b=4, t=2)
    for b in range(4):
        sp.dma_start(mem["xtok"][:, par, b, :, 0:D_IN], x[i, par, b]).then_inc(mem["xtok_in"][par], 16)


def load_later(sp, io, mem):
    loads = [(mem["w1"]["qkv"][:, j, :], io[f"a_{w}"]) for j, w in enumerate("qkv")]
    loads.append((mem["w1"]["o"][:], io["a_o"].rearrange("(k p) o -> p k o", p=128)))
    w = mem["w2"]
    loads += [(w["wr"][:], io["b_wr"]), (w["br"][:], io["b_br"].unsqueeze(0).to_broadcast([TOK, NE])),
              (w["w1"][:], io["b_w1"]), (w["b1"][:], io["b_b1"]), (w["w2"][:], io["b_w2"]), (w["b2"][:], io["b_b2"])]
    a, c, d = mem["ret_a"], mem["ret_c"], mem["ret_d"]
    loads += [(a[:, :, j * D:(j + 1) * D], io["r_" + n]) for j, n in enumerate(("wq", "wqs", "wk", "wks", "wv", "wg"))]
    loads += [(a[:, :, 6 * D:], io["r_ln1"]), (c[:, :, 0:8], io["r_small"]), (c[:, :, 8:8 + D], io["r_wo"]),
              (c[:, :, 8 + D:], io["r_w1"]), (d[:], io["r_w2"]),
              (mem["ret_b2"][:], io["r_b2"].unsqueeze(0).to_broadcast([TOK, LAYERS, D]))]
    w = mem["w4"]
    loads += [(w["wr"][:], io["c_wr"]), (w["w1"][:], io["c_w1"]), (w["b1"][:], io["c_b1"]), (w["w2"][:], io["c_w2"]),
              (w["b2"][:], io["c_b2"].unsqueeze(0).to_broadcast([TOK, D]))]
    for dst, src in loads:
        sp.dma_start(dst, src).then_inc(mem["later_in"], 16)
    return len(loads)


def setup(nc, ctx, io, mem):
    NCH = 7
    CH = NQ * N // NCH
    BLK = CH // 4
    LOADS = (0, 1, 4, NCH)
    with ExitStack() as here:
        def sb(name, shape, dt=F32):
            return here.enter_context(nc.sbuf_tensor(name, shape, dt))

        def sem(name):
            return here.enter_context(nc.semaphore(name))

        table = sb("table", [HALF, 2, H0])
        rest1 = sb("rest1", [HALF, 2, H0])
        rest2 = sb("rest2", [HALF, 2, H0])
        parts = sb("parts", [HALF, 2, 3, H0], BF16)
        idx = sb("idx", [HALF, NCH, CH], I32)
        onehot = sb("onehot", [HALF, 2, 2, CH], BF16)
        gathered = sb("gathered", [3 * H0, NCH * CH], BF16)
        kw = sb("kw", [KD, H0, AUG])
        qw = sb("qw", [KD, H0, AUG])
        vw = sb("vw", [VD, H0, AUG])
        bn = {k: sb("bn_" + k, shape) for k, shape in
              (("k", [KD, 4, H0]), ("q", [KD, 4, H0]), ("v", [VD, 4, H0]), ("p", [D, 4, 1]))}
        rs = {k: sb("rs_" + k, list(bn[k].shape)[:1] + list(bn[k].shape)[2:]) for k in bn}
        wide_p = sb("wide_p", [D, 2, D])
        epsb = sb("epsb", [D, H0])
        expo = sb("expo", [D, H0])
        scratch = nc.dram_tensor("bias_scratch", (3 * H0, NQ * N), BF16, kind="Internal").ap()

        bank = [here.enter_context(nc.psum_tensor(f"setup_bank{i}", [128, BANK], F32)) for i in range(8)]

        table_in = sem("table_in")
        idx_in = [sem(f"idx_in{n}") for n in range(3)]
        bn_in, w_in = sem("bn_in"), sem("w_in")
        split = sem("split")
        oh_made = sem("oh_made")
        g_mm = sem("g_mm")
        g_copied = sem("g_copied")
        g_out = sem("g_out")
        fills = sem("fills")
        var_eps = sem("var_eps")
        rstd = sem("rstd")
        folded = sem("folded")
        bt_mm = sem("bt_mm")
        done = sem("setup_done")
        bias_in = mem["bias_in"]
        consts, WpT, VT, BT = mem["consts"], mem["WpT"], mem["VT"], mem["BT"]
        ident = mem["c"]("ident")
        entry = mem["c"]("entry", HALF)
        idx_flat = io["idx"].rearrange("a b c -> (a b c)")

        with nc.Block() as block:
            @block.sync
            def _(sp):
                sp.dma_start(table[:], io["ab"].rearrange("(t p) h -> p t h", t=2)).then_inc(table_in, 16)
                sp.dma_start(entry, io["consts"][0:HALF, 0:2]).then_inc(table_in, 16)
                for n, (c, end) in enumerate(zip(LOADS, LOADS[1:])):
                    sp.dma_start(idx[:, c:end, :].rearrange("p n c -> p (n c)"),
                                 idx_flat[c * CH:end * CH].unsqueeze(0).to_broadcast([HALF, (end - c) * CH])
                                 ).then_inc(idx_in[n], 16)
                sp.wait_ge(mem["ones_set"], 1)
                for par in range(2):
                    load_features(sp, io, mem, 0, par)
                    load_tokens(sp, io, mem, 0, par)
                for c, n in ((0, 4), (4, NCH - 4)):
                    sp.wait_ge(g_copied, c + n)
                    sp.dma_start(scratch[:, c * CH:(c + n) * CH], gathered[:, c * CH:(c + n) * CH]
                                 ).then_inc(g_out, 16)
                sp.wait_ge(g_out, 32)
                for par in range(2):
                    sp.dma_start(mem["bias3"][par * NQ:(par + 1) * NQ, :, :],
                                 scratch.rearrange("(s r) (q k) -> r q s k", r=2, q=NQ)[par]
                                 ).then_inc(bias_in, 16)

            @block.scalar
            def _(act):
                act.dma_start(bn["k"][:], io["kv_bn"][0:KD]).then_inc(bn_in, 16)
                act.dma_start(bn["q"][:], io["q_bn"]).then_inc(bn_in, 16)
                act.dma_start(bn["v"][:], io["kv_bn"][KD:KD + VD]).then_inc(bn_in, 16)
                act.dma_start(bn["p"][:], io["proj_bn"].unsqueeze(2)).then_inc(bn_in, 16)
                kv = io["kv_w"].rearrange("(h e) d -> e h d", h=H0)
                act.dma_start(kw[:, :, 0:D_IN], kv[0:KD]).then_inc(w_in, 16)
                act.dma_start(qw[:, :, 0:D_IN], io["q_w"].rearrange("(h e) d -> e h d", h=H0)).then_inc(w_in, 16)
                act.dma_start(vw[:, :, 0:D_IN], kv[KD:KD + VD]).then_inc(w_in, 16)
                act.dma_start(WpT[:], io["projT"].rearrange("(k p) o -> p k o", p=D)).then_inc(w_in, 16)
                act.dma_start(consts[:, 2:], io["consts"][:, 2:]).then_inc(w_in, 16)
                for c in range(NCH):
                    act.wait_ge(g_mm, c + 1)
                    for j in range(4):
                        at = c * CH + j * BLK
                        ins = act.activation(gathered[:, at:at + BLK], bank[(c % 2) * 4 + j][0:3 * H0, 0:BLK],
                                             ACT.Copy)
                    ins.then_inc(g_copied, 1)
                act.wait_ge(bt_mm, 1)
                for j in range(3):
                    act.activation(BT[:, 4 * j:4 * j + 4, :],
                                   bank[j][0:AUG, 0:4 * AUG].rearrange("p (a b) -> p a b", a=4), ACT.Copy)
                for j in range(2):
                    ins = act.activation(VT[0:AUG, 6 * j:6 * j + 6, 0:VD],
                                         bank[3 + j][0:AUG, 0:6 * VD].rearrange("p (a b) -> p a b", a=6), ACT.Copy)
                ins.then_inc(done, 1)

            @block.gpsimd
            def _(pool):
                pool.memset(epsb[:], EPS)
                pool.memset(expo[:], -0.5)
                pool.memset(mem["ones_bf"][:], 1.0)
                pool.memset(mem["half_neg"][:], -0.5)
                pool.memset(mem["eps"][:], EPS)
                pool.memset(mem["half"][:], 0.5)
                pool.memset(mem["xtok"][:], 1.0)
                pool.memset(VT[:], 0.0).then_inc(fills, 1)
                pool.wait_ge(fills, 1)
                pool.memset(VT[D_IN:AUG, :, VD:VD + 1], 1.0).then_inc(fills, 1)
                pool.wait_ge(fills, 2)
                pool.memset(mem["xT"][D_IN:AUG, :, :, :], 1.0).then_inc(mem["ones_set"], 1)
                pool.wait_ge(mem["ones_set"], 1)
                pool.wait_ge(bn_in, 16 * 4)
                for k in "kqvp":
                    v = bn[k][:, 3, :]
                    e, w = v.shape
                    ins = pool.tensor_tensor(rs[k][:], v, epsb[0:e, 0:w], ALU.add)
                ins.then_inc(var_eps, 1)
                pool.wait_ge(var_eps, 1)
                for k in "kqvp":
                    e, w = rs[k].shape
                    ins = pool.tensor_tensor(rs[k][:], rs[k][:], expo[0:e, 0:w], ALU.pow)
                ins.then_inc(rstd, 1)

            @block.vector
            def _(dve):
                steps = [0]

                def link(ins):
                    steps[0] += 1
                    ins.then_inc(split, 1)
                    dve.wait_ge(split, steps[0])

                dve.wait_ge(table_in, 32)
                link(dve.tensor_copy(parts[:, :, 0], table[:]))
                link(dve.tensor_tensor(rest1[:], table[:], parts[:, :, 0], ALU.subtract))
                link(dve.tensor_copy(parts[:, :, 1], rest1[:]))
                link(dve.tensor_tensor(rest2[:], rest1[:], parts[:, :, 1], ALU.subtract))
                link(dve.tensor_copy(parts[:, :, 2], rest2[:]))
                for c in range(NCH):
                    if c in LOADS:
                        dve.wait_ge(idx_in[LOADS.index(c)], 16)
                    if c >= 2:
                        dve.wait_ge(g_mm, c - 1)
                    for t in range(2):
                        dve.tensor_scalar(onehot[:, c % 2, t, :], idx[:, c, :], entry[:, t:t + 1], None,
                                          ALU.is_equal).then_inc(oh_made, 1)
                dve.wait_ge(rstd, 1)
                dve.wait_ge(w_in, 16 * 5)
                for k, w in (("k", kw), ("q", qw), ("v", vw), ("p", None)):
                    link(dve.tensor_tensor(rs[k][:], rs[k][:], bn[k][:, 0, :], ALU.mult))
                    link(dve.tensor_tensor(bn[k][:, 2, :], bn[k][:, 2, :], rs[k][:], ALU.mult))
                    link(dve.tensor_tensor(bn[k][:, 1, :], bn[k][:, 1, :], bn[k][:, 2, :], ALU.subtract))
                    if k == "q":
                        link(dve.tensor_scalar(rs[k][:], rs[k][:], KD ** -0.5, None, ALU.mult))
                        link(dve.tensor_scalar(bn[k][:, 1, :], bn[k][:, 1, :], KD ** -0.5, None, ALU.mult))
                    if w is not None:
                        e = w.shape[0]
                        link(dve.tensor_tensor(w[:, :, 0:D_IN], w[:, :, 0:D_IN],
                                               rs[k][:].unsqueeze(2).to_broadcast([e, H0, D_IN]), ALU.mult))
                        dve.tensor_copy(w[:, :, D_IN:AUG], bn[k][:, 1, :].unsqueeze(2)).then_inc(folded, 1)
                    else:
                        dve.tensor_copy(wide_p[:, 0], rs[k][:].to_broadcast([D, D]))
                        dve.tensor_copy(wide_p[:, 1], bn[k][:, 1].to_broadcast([D, D])).then_inc(folded, 1)
                dve.tensor_copy(mem["before_bf"][:], mem["c"]("before", TOK))
                dve.tensor_copy(mem["sel_bf"][:].rearrange("p e f -> p (e f)"), mem["c"]("sel", 8))
                dve.wait_ge(bt_mm, 1)
                dve.tensor_copy(mem["proj_c"][:], bank[5][0:TOK, D:2 * D])
                dve.tensor_tensor(WpT[:], WpT[:], bank[5][:, 0:D].unsqueeze(1).to_broadcast([D, 6, D]), ALU.mult)

            @block.tensor
            def _(pe):
                for c in range(NCH):
                    pe.wait_ge(oh_made, 2 * (c + 1))
                    if c >= 2:
                        pe.wait_ge(g_copied, c - 1)
                    for j in range(4):
                        for m in range(2):
                            ins = pe.matmul(bank[(c % 2) * 4 + j][0:3 * H0, 0:BLK],
                                            parts[:, m].rearrange("p s h -> p (s h)"),
                                            onehot[:, c % 2, m, j * BLK:(j + 1) * BLK],
                                            start=(m == 0), stop=(m == 1))
                    ins.then_inc(g_mm, 1)
                pe.wait_ge(folded, 2)
                pe.wait_ge(g_copied, NCH)
                for h in range(H0):
                    pe.matmul(bank[h // 4][0:AUG, (h % 4) * AUG:(h % 4 + 1) * AUG], qw[:, h, :], kw[:, h, :],
                              start=True, stop=True)
                pe.wait_ge(folded, 4)
                for h in range(H0):
                    pe.transpose(bank[3 + h // 6][0:AUG, (h % 6) * VD:(h % 6 + 1) * VD], vw[:, h, :],
                                 ident[0:VD, 0:VD])
                for j in range(2):
                    ins = pe.transpose(bank[5][:, j * D:(j + 1) * D], wide_p[:, j], ident)
                ins.then_inc(bt_mm, 1)


def token_attention(nc, ctx, io, mem):
    QUADS = B // 4
    with ExitStack() as here:
        def sb(name, shape, dt=F32):
            return here.enter_context(nc.sbuf_tensor(name, shape, dt))

        def sem(name):
            return here.enter_context(nc.semaphore(name))

        xtok, xT = mem["xtok"], mem["xT"]
        QT = sb("QT", [AUG, 2, 4, H0 * NQ])
        T = sb("T", [TOK, 2, PAIRS, N])
        mx = sb("mx", [TOK, 2, PAIRS])
        E = sb("E", [HALF, 2, 2, H0 * NQ])
        EX = sb("EX", [AUG, 2, H0, TOK])
        rc = sb("rc", [TOK, 2, H0])
        O = sb("O", [TOK, 2, H0 * VD])
        R = sb("R", [TOK, 2, H0 * VD])
        HS = sb("HS", [TOK, 2, H0 * VD])
        HST = sb("HST", [128, 6, TOK])
        psS = here.enter_context(nc.psum_tensor("psS", [128, 3, BANK], F32))
        psT = here.enter_context(nc.psum_tensor("psT", [128, 2, BANK], F32))
        psX = here.enter_context(nc.psum_tensor("psX", [128, 2, BANK], F32))
        psM = here.enter_context(nc.psum_tensor("psM", [128, BANK], F32))

        xtok_in, xT_in = mem["xtok_in"], mem["xT_in"]
        q_mm, q_copied = sem("q_mm"), sem("q_copied")
        s_mm, s_added = sem("s_mm"), sem("s_added")
        shifted = sem("shifted")
        t_mm, exped = sem("t_mm"), sem("exped")
        x_mm = [sem("x_mm0"), sem("x_mm1")]
        x_copied = [sem("x_copied0"), sem("x_copied1")]
        v_mm, v_inverse, v_scaled = sem("v_mm"), sem("v_inverse"), sem("v_scaled")
        relued, swished = sem("relued"), sem("swished")
        bias_made = sem("bias_made")
        hst_mm, hst_copied = sem("hst_mm"), sem("hst_copied")
        p_mm, p_added = sem("p_mm"), sem("p_added")

        ident = mem["c"]("ident")
        bias, BT, VT, WpT = mem["bias"], mem["BT"], mem["VT"], mem["WpT"]
        h = mem["h"][:].rearrange("p (i k) c -> p i k c", k=4)

        def steps(emit):
            for r in range(8):
                emit(0, r)
            with emit.eng.Fori(1, QUADS // 2 - 1) as i:
                for r in range(8):
                    emit(i, r)
            for r in range(8, 20):
                emit(QUADS // 2 - 2, r)

        class Steps:

            def __init__(self, eng, step):
                self.eng, self.step = eng, step

            def __call__(self, i, r):
                if known(i):
                    i, r = i + r // 8, r % 8
                self.step(i, r)

        def live(n, last=B):
            return not known(n) or 0 <= n < last

        with nc.Block() as block:
            @block.sync
            def _(sp):
                later = load_later(sp, io, mem)
                with sp.Fori(1, QUADS // 2) as i:
                    for par in range(2):
                        q = 2 * i + par
                        sp.wait_ge(s_mm, 12 * (q - 1))
                        stand(sp, mem["passed"]["sp"])
                        load_features(sp, io, mem, i, par)
                        sp.wait_ge(x_mm[1], 4 * (q - 1))
                        stand(sp, mem["passed"]["sp"])
                        load_tokens(sp, io, mem, i, par)
                sp.wait_ge(mem["later_in"], 16 * later)

            @block.tensor
            def _(pe):
                def q_chunk(i, par, j):
                    q = 2 * i + par
                    if j == 0:
                        pe.wait_ge(xT_in[par], 16 * (i + 1))
                    if positive(6 * q + j):
                        pe.wait_ge(q_copied, 6 * q + j)
                    src = xT[:, par, :, 0:HALF].rearrange("p b (y x) -> p b y x", x=14)[:, :, 0:7, 0:7]
                    for u in range(2):
                        ins = pe.matmul(psM[0:AUG, u * 4 * NQ:(u + 1) * 4 * NQ], BT[:, 2 * j + u, :], src,
                                        start=True, stop=True)
                    ins.then_inc(q_mm, 1)

                def scores(i, r, n):
                    q, par, b = 2 * i + r // 4, r // 4, r % 4
                    pe.wait_ge(q_copied, 6 * (q + 1))
                    for j in range(3):
                        if positive(3 * (n - 1) + j + 1):
                            pe.wait_ge(s_added, 3 * (n - 1) + j + 1)
                        for u in range(2):
                            at = (2 * j + u) * TOK
                            ins = pe.matmul(psS[0:TOK, j, u * N:(u + 1) * N], QT[:, par, b, at:at + TOK],
                                            xT[:, par, b, :], start=True, stop=True)
                        ins.then_inc(s_mm, 1)

                def turn(n, t, slot):
                    pe.wait_ge(shifted, n + 1)
                    if positive(2 * n + t):
                        pe.wait_ge(exped, 2 * n + t)
                    for j in range(PAIRS):
                        ins = pe.transpose(psT[0:HALF, j // 3, (j % 3) * TOK:(j % 3 + 1) * TOK],
                                           T[:, slot, j, t * HALF:(t + 1) * HALF], ident[0:TOK, 0:TOK])
                    ins.then_inc(t_mm, 1)

                def weigh(n, c, slot, par, b, i, pair_before):
                    if c == 0:
                        pe.wait_ge(xtok_in[par], 64 * (i + 1))
                    pe.wait_ge(exped, 2 * n + 2)
                    if positive(n):
                        pe.wait_ge(x_copied[c], n)
                    if slot == 0:
                        if positive(n - 1 + c):
                            pe.wait_ge(v_scaled, n - 1 + c)
                    for t in range(2):
                        ins = pe.matmul(psX[0:AUG, c, 0:6 * NQ], xtok[:, par, b, t, :],
                                        E[:, slot, t, c * 6 * NQ:(c + 1) * 6 * NQ], start=(t == 0), stop=(t == 1))
                    ins.then_inc(x_mm[c], 1)

                def values(p, slot):
                    for c in range(2):
                        for k in range(2):
                            pe.wait_ge(x_copied[k], 2 * p + 2)
                        for j in range(6):
                            hh = 6 * c + j
                            ins = pe.matmul(psX[0:TOK, c, j * (VD + 1):(j + 1) * (VD + 1)], EX[:, slot, hh, :],
                                            VT[0:AUG, hh, :], start=True, stop=True)
                        ins.then_inc(v_mm, 1)

                def swish_turn(p, c, slot, q_count):
                    if c == 0:
                        pe.wait_ge(swished, p + 1)
                        if positive(q_count):
                            pe.wait_ge(q_copied, q_count)
                        if positive(p):
                            pe.wait_ge(p_added, p)
                    else:
                        pe.wait_ge(hst_copied, 2 * p + 1)
                    for j in range(3):
                        k = 3 * c + j
                        ins = pe.transpose(psM[:, j * TOK:(j + 1) * TOK], HS[:, slot, k * 128:(k + 1) * 128],
                                           ident[0:TOK, 0:TOK])
                    ins.then_inc(hst_mm, 1)

                def project(p, q_count):
                    pe.wait_ge(hst_copied, 2 * p + 2)
                    if positive(q_count):
                        pe.wait_ge(q_copied, q_count)
                    for k in range(6):
                        ins = pe.matmul(psM[0:TOK, 0:D], HST[:, k, :], WpT[:, k, :], start=(k == 0), stop=(k == 5))
                    ins.then_inc(p_mm, 1)

                def step(i, r):
                    n = 8 * i + r
                    q = 2 * i + r // 4
                    ahead = live(q + 1, QUADS)
                    ni, npar = i + (r // 4 + 1) // 2, (r // 4 + 1) % 2
                    made = 6 * (q + 1)

                    def chunk(j):
                        if ahead:
                            if j == 1:
                                if positive(4 * i + r // 2 - 2):
                                    pe.wait_ge(p_added, 4 * i + r // 2 - 2)
                            if j in (0, 5):
                                if positive(2 * (4 * i + (r - 5) // 2) + 2):
                                    pe.wait_ge(hst_copied, 2 * (4 * i + (r - 5) // 2) + 2)
                            q_chunk(ni, npar, j)

                    p = 4 * i + (r - 4) // 2 if r % 2 == 0 else 4 * i + (r - 5) // 2
                    pair = live(p, TILES)
                    slot = (p % 2) if known(p) else ((r - 4) // 2) % 2 if r % 2 == 0 else ((r - 5) // 2) % 2
                    if r % 2 == 0 and pair:
                        values(p, slot)
                    if live(n):
                        scores(i, r, n)
                    if r % 4 == 2:
                        chunk(1)
                    if r % 2 == 1 and pair:
                        swish_turn(p, 0, slot, made + 5 if ahead and r % 4 == 3 else 0)
                    if live(n - 1):
                        turn(n - 1, 0, (r - 1) % 2)
                    if r % 4 == 2:
                        chunk(2)
                    if r % 2 == 1 and pair:
                        swish_turn(p, 1, slot, 0)
                    m = n - 2
                    mi, mr = i + (r - 2) // 8, (r - 2) % 8
                    if live(m):
                        weigh(m, 0, mr % 2, mr // 4, mr % 4, mi, None)
                    if r % 4 > 0:
                        chunk({1: 0, 2: 3, 3: 5}[r % 4])
                    if live(n - 1):
                        turn(n - 1, 1, (r - 1) % 2)
                    if live(m):
                        weigh(m, 1, mr % 2, mr // 4, mr % 4, mi, None)
                    if r % 4 == 2:
                        chunk(4)
                    if r % 2 == 1 and pair:
                        project(p, (made + (1 if r % 4 == 1 else 6)) if ahead else 0)

                for j in range(6):
                    q_chunk(0, 0, j)
                steps(Steps(pe, step))

            @block.vector
            def _(dve):
                def add_max(n, r):
                    slot = r % 2
                    for j in range(PAIRS):
                        if j % 2 == 0:
                            dve.wait_ge(s_mm, 3 * n + j // 2 + 1)
                            stand(dve, mem["passed"]["dve"])
                        ins = dve.tensor_tensor_reduce(
                            T[:, slot, j, :], psS[0:TOK, j // 2, (j % 2) * N:(j % 2 + 1) * N], bias[:, j, :],
                            1.0, LOWEST, ALU.add, ALU.max, mx[:, slot, j:j + 1])
                        if j % 2:
                            ins.then_inc(s_added, 1)

                def shift(n, r):
                    slot = r % 2
                    dve.wait_ge(s_added, 3 * n + 3)
                    dve.tensor_tensor(T[:, slot], T[:, slot],
                                      mx[:, slot].unsqueeze(2).to_broadcast([TOK, PAIRS, N]),
                                      ALU.subtract).then_inc(shifted, 1)

                def copy_x(n, slot, odd):
                    dve.wait_ge(x_mm[0], n + 1)
                    dve.tensor_copy(EX[:, slot, 0:6, odd * NQ:(odd + 1) * NQ],
                                    psX[0:AUG, 0, 0:6 * NQ].rearrange("p (h q) -> p h q", h=6)
                                    ).then_inc(x_copied[0], 1)

                def scale_values(p, slot):
                    for c in range(2):
                        v = psX[0:TOK, c, 0:6 * (VD + 1)].rearrange("p (h e) -> p h e", h=6)
                        dve.wait_ge(v_mm, 2 * p + c + 1)
                        dve.reciprocal(rc[:, slot, 6 * c:6 * c + 6].unsqueeze(2), v[:, :, VD:VD + 1]
                                       ).then_inc(v_inverse, 1)
                        dve.wait_ge(v_inverse, 2 * p + c + 1)
                        dve.tensor_tensor(O[:, slot, c * 6 * VD:(c + 1) * 6 * VD].rearrange("p (h e) -> p h e", h=6),
                                          v[:, :, 0:VD],
                                          rc[:, slot, 6 * c:6 * c + 6].unsqueeze(2).to_broadcast([TOK, 6, VD]),
                                          ALU.mult).then_inc(v_scaled, 1)

                def swish(p, slot):
                    dve.wait_ge(relued, p + 1)
                    dve.scalar_tensor_tensor(HS[:, slot], R[:, slot], 1.0, O[:, slot], ALU.min, ALU.mult
                                             ).then_inc(swished, 1)

                def add_proj(p, i, k):
                    dve.wait_ge(p_mm, p + 1)
                    dve.tensor_tensor(h[:, i + k // 4, k % 4, :], psM[0:TOK, 0:D], mem["proj_c"][:], ALU.add
                                      ).then_inc(p_added, 1)

                def step(i, r):
                    n = 8 * i + r
                    k = (r - 4) // 2 if r % 2 == 0 else (r - 5) // 2
                    p = 4 * i + k
                    pair = live(p, TILES)
                    slot = k % 2
                    if r % 2 == 0 and pair:
                        scale_values(p, slot)
                    if live(n):
                        add_max(n, r)
                    if live(n - 2):
                        copy_x(n - 2, ((r - 2) // 2) % 2, r % 2)
                    if live(n):
                        shift(n, r)
                    if r % 2 == 0 and pair:
                        swish(p, slot)
                    if r % 2 == 1 and pair:
                        add_proj(p, i, k)

                dve.wait_ge(mem["bias_in"], 32)
                part = lambda n: mem["bias3"][:, n * PAIRS:(n + 1) * PAIRS, :]
                dve.tensor_tensor(bias[:], part(0), part(1), ALU.add).then_inc(bias_made, 1)
                dve.wait_ge(bias_made, 1)
                dve.tensor_tensor(bias[:], bias[:], part(2), ALU.add).then_inc(bias_made, 1)
                dve.wait_ge(bias_made, 2)
                steps(Steps(dve, step))

            @block.scalar
            def _(act):
                def copy_q(i, par, j):
                    q = 2 * i + par
                    act.wait_ge(q_mm, 6 * q + j + 1)
                    for u in range(2):
                        hh = 2 * j + u
                        ins = act.activation(QT[:, par, :, hh * NQ:(hh + 1) * NQ],
                                             psM[0:AUG, u * 4 * NQ:(u + 1) * 4 * NQ].rearrange("p (b q) -> p b q", b=4),
                                             ACT.Copy)
                    ins.then_inc(q_copied, 1)

                def exp(n, t, slot):
                    act.wait_ge(t_mm, 2 * n + t + 1)
                    act.activation(E[:, slot, t, :].rearrange("p (c x) -> p c x", c=2), psT[0:HALF, :, 0:6 * NQ],
                                   ACT.Exp).then_inc(exped, 1)

                def copy_x(n, slot, odd):
                    act.wait_ge(x_mm[1], n + 1)
                    act.activation(EX[:, slot, 6:12, odd * NQ:(odd + 1) * NQ],
                                   psX[0:AUG, 1, 0:6 * NQ].rearrange("p (h q) -> p h q", h=6), ACT.Copy
                                   ).then_inc(x_copied[1], 1)

                def relu(p, slot):
                    act.wait_ge(v_scaled, 2 * p + 2)
                    act.activation(R[:, slot], O[:, slot], ACT.Relu, bias=mem["half"][:, 0:1], scale=1.0 / 6.0
                                   ).then_inc(relued, 1)

                def copy_hst(p, c):
                    act.wait_ge(hst_mm, 2 * p + c + 1)
                    act.activation(HST[:, 3 * c:3 * c + 3, :],
                                   psM[:, 0:3 * TOK].rearrange("p (k q) -> p k q", k=3), ACT.Copy
                                   ).then_inc(hst_copied, 1)

                def step(i, r):
                    n = 8 * i + r
                    q = 2 * i + r // 4
                    ahead = live(q + 1, QUADS)
                    ni, npar = i + (r // 4 + 1) // 2, (r // 4 + 1) % 2

                    def chunk(j):
                        if ahead:
                            copy_q(ni, npar, j)

                    k = (r - 4) // 2 if r % 2 == 0 else (r - 5) // 2
                    p = 4 * i + k
                    pair = live(p, TILES)
                    slot = k % 2
                    if r % 4 == 2:
                        chunk(1)
                    if r % 2 == 1 and pair:
                        copy_hst(p, 0)
                    if live(n - 1):
                        exp(n - 1, 0, (r - 1) % 2)
                    if r % 4 == 2:
                        chunk(2)
                    if r % 2 == 1 and pair:
                        copy_hst(p, 1)
                    if r % 2 == 0 and pair:
                        relu(p, slot)
                    if r % 4 > 0:
                        chunk({1: 0, 2: 3, 3: 5}[r % 4])
                    if live(n - 1):
                        exp(n - 1, 1, (r - 1) % 2)
                    if live(n - 2):
                        copy_x(n - 2, ((r - 2) // 2) % 2, r % 2)
                    if r % 4 == 2:
                        chunk(4)

                for j in range(6):
                    copy_q(0, 0, j)
                steps(Steps(act, step))


class Norm:

    def __init__(self, nc, here, name, mem):
        self.mem, self.name = mem, name
        self.stats = here.enter_context(nc.sbuf_tensor(name + "_stats", [TOK, 2, 4, 6], F32))
        self.mv = here.enter_context(nc.sbuf_tensor(name + "_mv", [TOK, 2, 4, 2], F32))
        self.var = here.enter_context(nc.sbuf_tensor(name + "_var", [TOK, 2, 4], F32))
        self.rstd = here.enter_context(nc.sbuf_tensor(name + "_rstd", [TOK, 2, 4], F32))
        self.moments = here.enter_context(nc.semaphore(name + "_moments"))
        self.roots = here.enter_context(nc.semaphore(name + "_roots"))

    def take(self, dve, x, g, slot):
        for k in range(4):
            ins = dve.bn_stats(self.stats[:, slot, k, :], x[:, k, :])
        ins.then_inc(self.moments, 1)
        dve.wait_ge(self.moments, 2 * g + 1)
        stand(dve, self.mem["passed"]["dve"])
        for k in range(4):
            ins = dve.bn_aggr(self.mv[:, slot, k, :], self.stats[:, slot, k, :])
        ins.then_inc(self.moments, 1)

    def root(self, pool, g, slot):
        pool.wait_ge(self.moments, 2 * g + 2)
        pool.tensor_tensor(self.var[:, slot, :].unsqueeze(2), self.mv[:, slot, :, 1:2],
                           self.mem["eps"][0:TOK, 0:4].unsqueeze(2), ALU.add).then_inc(self.roots, 1)
        pool.wait_ge(self.roots, 2 * g + 1)
        pool.tensor_tensor(self.rstd[:, slot, :], self.var[:, slot, :], self.mem["half_neg"][0:TOK, 0:4],
                           ALU.pow).then_inc(self.roots, 1)

    def scale(self, dve, out, x, g, slot, done, last_only=False):
        dve.wait_ge(self.roots, 2 * g + 2)
        stand(dve, self.mem["passed"]["dve"])
        for k in range(4):
            ins = dve.tensor_scalar(out[:, k, :], x[:, k, :], self.mv[:, slot, k, 0:1],
                                    self.rstd[:, slot, k:k + 1], ALU.subtract, ALU.mult)
            if not last_only or k == 3:
                ins.then_inc(done, 1)


def group_view(t, per):
    return t[:].rearrange("p (i r k) c -> p i r k c", r=per, k=4)


def at(view, i, r, per):
    return view[:, i + r // per, r % per]


def skewed(eng, step, groups, lag, per=2, peel=0):
    first = -(-(lag + peel) // per)
    whole = groups // per
    for n in range(first * per):
        step(n // per, n % per)
    with eng.Fori(first, whole) as i:
        for r in range(per):
            step(i, r)
    for n in range(whole * per, groups + lag):
        step(n // per, n % per)


GROUPS = TILES // 4
H1, D1 = 8, 64


def head_attention(nc, ctx, io, mem):
    with ExitStack() as here:
        def sb(name, shape, dt=F32):
            return here.enter_context(nc.sbuf_tensor(name, shape, dt))

        def sem(name):
            return here.enter_context(nc.semaphore(name))

        def bank(name):
            return here.enter_context(nc.psum_tensor(name, [128, BANK], F32))

        W = mem["w1"]
        ln = Norm(nc, here, "ln_a", mem)
        xn = sb("xn", [TOK, 2, 4, D])
        XT = sb("XT", [D, 2, 4, 2 * TOK])
        KS = sb("KS", [TOK, 2, 512])
        VS = sb("VS", [TOK, 2, 4, 2, 512])
        PR = sb("PR", [TOK, 2, 512])
        dots = sb("dots", [TOK, 2, 4, H1])
        top = sb("top", [TOK, 2, 4, H1])
        arg = sb("arg", [TOK, 2, 2, 4, H1])
        wts = sb("wts", [TOK, 2, 2, 4, H1])
        den = sb("den", [TOK, 2, 4, H1])
        coef = sb("coef", [TOK, 2, 2, 4, H1])
        ZA, ZB, Z = sb("ZA", [TOK, 2, 512]), sb("ZB", [TOK, 2, 512]), sb("Z", [TOK, 2, 512])
        ZT = sb("ZT", [128, 2, 4 * TOK])
        ps = [bank(n) for n in ("psQ", "psK", "psV", "psL")]
        psZ, psO = bank("psZ"), bank("psO")
        psX = [bank("psX0"), bank("psX1")]

        normed = sem("normed")
        x_mm, x_copied = sem("a_x_mm"), sem("a_x_copied")
        qkvl_mm, kvl_copied = sem("qkvl_mm"), sem("kvl_copied")
        multiplied, dotted = sem("multiplied"), sem("dotted")
        soft = sem("soft")
        arg_made, wts_made, coef_made = sem("arg_made"), sem("wts_made"), sem("coef_made")
        z_parts, z_made = sem("z_parts"), sem("z_made")
        z_mm, z_copied, o_mm, o_added = sem("z_mm"), sem("z_copied"), sem("o_mm"), sem("o_added")
        h = group_view(mem["h"], 2)
        ident, after = mem["c"]("ident"), mem["c"]("after", TOK)
        live = lambda g: not known(g) or 0 <= g < GROUPS

        def behind(s, r, k, tiles):
            return (s - 3, r - 3, k + 4 - tiles) if k + 4 >= tiles else (s - 4, r - 4, k + 8 - tiles)

        with nc.Block() as block:
            @block.gpsimd
            def _(pool):
                def step(i, r):
                    s = 2 * i + r
                    for k in range(4):
                        g, gr, kz = behind(s, r, k, 5)
                        if live(g):
                            t = 4 * g + kz
                            if positive(t - 1):
                                pool.wait_ge(z_mm, t - 1)
                            pool.wait_ge(z_parts, t + 1)
                            pool.tensor_tensor(Z[:, kz % 2], ZA[:, kz % 2], ZB[:, kz % 2], ALU.add
                                               ).then_inc(z_made, 1)
                        if k == 1 and live(s):
                            ln.root(pool, s, r % 2)

                skewed(pool, step, GROUPS, 4)

            @block.vector
            def _(dve):
                def z_tile(g, slot, k):
                    t = 4 * g + k
                    if k == 0:
                        dve.wait_ge(coef_made, g + 1)
                    if positive(t - 1):
                        dve.wait_ge(z_made, t - 1)
                    for j, out in ((0, ZA), (1, ZB)):
                        ins = dve.tensor_tensor(out[:, k % 2].rearrange("p (h d) -> p h d", h=H1),
                                                VS[:, slot, k, j].rearrange("p (h d) -> p h d", h=H1),
                                                coef[:, slot, j, k].unsqueeze(2).to_broadcast([TOK, H1, D1]),
                                                ALU.mult)
                    ins.then_inc(z_parts, 1)

                def dot(g, slot, k):
                    t = 4 * g + k
                    dve.wait_ge(qkvl_mm, 4 * t + 1)
                    dve.wait_ge(kvl_copied, 3 * t + 1)
                    dve.tensor_tensor(PR[:, k % 2], ps[0][0:TOK, :], KS[:, k % 2], ALU.mult).then_inc(multiplied, 1)
                    dve.wait_ge(multiplied, t + 1)
                    dve.tensor_reduce(dots[:, slot, k, :].unsqueeze(2),
                                      PR[:, k % 2].rearrange("p (h d) -> p h d", h=H1), AX.X, ALU.add
                                      ).then_inc(dotted, 1)

                def softmax_args(g, slot):
                    d = dots[:, slot]
                    dve.wait_ge(dotted, 4 * g + 4)
                    dve.tensor_scalar(top[:, slot], d, D1 ** -0.5, mem["c"]("floor", TOK), ALU.mult, ALU.max
                                      ).then_inc(soft, 1)
                    dve.wait_ge(soft, 3 * g + 1)
                    dve.scalar_tensor_tensor(arg[:, slot, 0], d, D1 ** -0.5, top[:, slot], ALU.mult, ALU.subtract)
                    dve.tensor_scalar(arg[:, slot, 1], top[:, slot], -1.0, 0.0, ALU.mult, ALU.min
                                      ).then_inc(arg_made, 1)

                def softmax_ends(g, slot):
                    dve.wait_ge(wts_made, g + 1)
                    dve.scalar_tensor_tensor(den[:, slot], wts[:, slot, 1], mem["c"]("later", TOK), wts[:, slot, 0],
                                             ALU.mult, ALU.add).then_inc(soft, 1)
                    dve.wait_ge(soft, 3 * g + 2)
                    dve.reciprocal(den[:, slot], den[:, slot]).then_inc(soft, 1)
                    dve.wait_ge(soft, 3 * g + 3)
                    dve.tensor_tensor(coef[:, slot].rearrange("p j k h -> p j (k h)"),
                                      wts[:, slot].rearrange("p j k h -> p j (k h)"),
                                      den[:, slot].rearrange("p k h -> p (k h)").unsqueeze(1)
                                      .to_broadcast([TOK, 2, 4 * H1]), ALU.mult).then_inc(coef_made, 1)

                def step(i, r):
                    s = 2 * i + r
                    for k in range(4):
                        if live(s - 2):
                            dot(s - 2, r % 2, k)
                        if k == 0 and live(s - 3):
                            softmax_ends(s - 3, (r - 3) % 2)
                        g, gr, kz = behind(s, r, k, 5)
                        if live(g):
                            z_tile(g, gr % 2, kz)
                        if k == 1 and live(s):
                            ln.take(dve, at(h, i, r, 2), s, r % 2)
                        if k == 3 and live(s - 2):
                            softmax_args(s - 2, r % 2)
                        if k == 3 and live(s):
                            if positive(4 * (s - 1)):
                                dve.wait_ge(x_mm, 4 * (s - 1))
                            ln.scale(dve, xn[:, r % 2], at(h, i, r, 2), s, r % 2, normed)
                        g, gr, kz = behind(s, r, k, 6)
                        if live(g):
                            dve.wait_ge(o_mm, 4 * g + kz + 1)
                            x = at(h, i, gr, 2)[:, kz, :]
                            dve.tensor_tensor(x, psO[0:TOK, 0:D], x, ALU.add).then_inc(o_added, 1)

                skewed(dve, step, GROUPS, 4)

            @block.scalar
            def _(act):
                def step(i, r):
                    s = 2 * i + r
                    for k in range(4):
                        t = 4 * (s - 2) + k
                        if live(s - 2):
                            if positive(t - 1):
                                act.wait_ge(multiplied, t - 1)
                            act.wait_ge(qkvl_mm, 4 * t + 2)
                            act.activation(KS[:, k % 2], ps[1][0:TOK, :], ACT.Copy).then_inc(kvl_copied, 1)
                        if k == 0 and live(s - 3):
                            act.wait_ge(arg_made, s - 2)
                            act.activation(wts[:, (r - 3) % 2], arg[:, (r - 3) % 2], ACT.Exp).then_inc(wts_made, 1)
                        g, gr, kz = behind(s, r, k, 6)
                        if live(g):
                            act.wait_ge(z_mm, 4 * g + kz + 1)
                            act.activation(ZT[:, kz % 2], psZ[:, 0:4 * TOK], ACT.Copy).then_inc(z_copied, 1)
                        if live(s - 2):
                            for j in range(2):
                                act.wait_ge(qkvl_mm, 4 * t + 3 + j)
                                act.activation(VS[:, r % 2, k, j], ps[2 + j][0:TOK, :], ACT.Copy
                                               ).then_inc(kvl_copied, 1)
                        if live(s - 1):
                            act.wait_ge(x_mm, 4 * (s - 1) + k + 1)
                            act.activation(XT[:, (r - 1) % 2, k, :], psX[k % 2][:, 0:2 * TOK], ACT.Copy
                                           ).then_inc(x_copied, 1)

                skewed(act, step, GROUPS, 4)

            @block.tensor
            def _(pe):
                def project(g, slot, k, j):
                    t = 4 * g + k
                    if j == 0:
                        pe.wait_ge(x_copied, t + 1)
                        if positive(t):
                            pe.wait_ge(multiplied, t)
                    else:
                        if positive(3 * (t - 1) + j):
                            pe.wait_ge(kvl_copied, 3 * (t - 1) + j)
                    src = XT[:, slot, k, TOK:2 * TOK] if j == 3 else XT[:, slot, k, 0:TOK]
                    pe.matmul(ps[j][0:TOK, :], src, W["qkv"][:, min(j, 2), :], start=True, stop=True
                              ).then_inc(qkvl_mm, 1)

                def step(i, r):
                    s = 2 * i + r
                    for k in range(4):
                        gz, gr, kz = behind(s, r, k, 6)
                        g = 4 * gz + kz
                        if live(s - 2):
                            project(s - 2, r % 2, k, 0)
                            project(s - 2, r % 2, k, 1)
                        if live(gz):
                            if positive(g):
                                pe.wait_ge(z_copied, g)
                            pe.wait_ge(z_made, g + 1)
                            for j in range(4):
                                ins = pe.transpose(psZ[:, j * TOK:(j + 1) * TOK], Z[:, kz % 2, j * 128:(j + 1) * 128],
                                                   ident[0:TOK, 0:TOK])
                            ins.then_inc(z_mm, 1)
                        if live(s - 2):
                            project(s - 2, r % 2, k, 2)
                            project(s - 2, r % 2, k, 3)
                        if live(gz):
                            if positive(g):
                                pe.wait_ge(o_added, g)
                            pe.wait_ge(z_copied, g + 1)
                            for j in range(4):
                                ins = pe.matmul(psO[0:TOK, 0:D], ZT[:, kz % 2, j * TOK:(j + 1) * TOK],
                                                W["o"][:, j, :], start=(j == 0), stop=(j == 3))
                            ins.then_inc(o_mm, 1)
                        if live(s - 1):
                            t = 4 * (s - 1) + k
                            if positive(t - 1):
                                pe.wait_ge(x_copied, t - 1)
                            pe.wait_ge(normed, t + 1)
                            pe.transpose(psX[k % 2][:, 0:TOK], xn[:, (r - 1) % 2, k, :], ident[0:TOK, 0:TOK])
                            pe.matmul(psX[k % 2][:, TOK:2 * TOK], xn[:, (r - 1) % 2, k, :], after,
                                      start=True, stop=True).then_inc(x_mm, 1)

                skewed(pe, step, GROUPS, 4)


NE = 8
BIG = 1.0e30


def top1_experts(nc, ctx, io, mem):
    with ExitStack() as here:
        def sb(name, shape, dt=F32):
            return here.enter_context(nc.sbuf_tensor(name, shape, dt))

        def sem(name):
            return here.enter_context(nc.semaphore(name))

        def bank(name):
            return here.enter_context(nc.psum_tensor(name, [128, BANK], F32))

        W = mem["w2"]
        ln = Norm(nc, here, "ln_b", mem)
        xn = sb("b_xn", [TOK, 2, 4, D])
        XT = sb("b_XT", [D, 2, 4 * TOK])
        LG, SH, EX = sb("LG", [TOK, 2, 4, NE]), sb("SH", [TOK, 2, 4, NE]), sb("b_EX", [TOK, 2, 4, NE])
        cand, OH = sb("cand", [TOK, 2, 4, NE]), sb("OH", [TOK, 2, 4, NE])
        most, best = sb("most", [TOK, 2, 4]), sb("best", [TOK, 2, 4])
        total, gate = sb("total", [TOK, 2, 4]), sb("gate", [TOK, 2, 4])
        OHT = sb("OHT", [NE, 2, 4 * TOK])
        pen = sb("pen", [NE, 2, 4 * TOK], BF16)
        HID = sb("b_HID", [128, 2, NE, 4 * TOK])
        psX, psR = bank("b_psX"), bank("b_psR")
        psL = psH = psR
        psY = [bank("b_psY0"), bank("b_psY1")]
        psE = [bank(f"b_psE{i}") for i in range(4)]

        normed, x_mm, x_copied = sem("b_normed"), sem("b_x_mm"), sem("b_x_copied")
        l_mm = sem("l_mm")
        ROUTE = 7
        route = sem("route")
        sh_made, ex_made, gated, oh_made = sem("sh_made"), sem("b_ex_made"), sem("gated"), sem("b_oh_made")
        oh_mm, pen_made = sem("oh_mm"), sem("pen_made")
        e_mm, e_relu = sem("e_mm"), sem("e_relu")
        y_mm, y_added = sem("y_mm"), sem("y_added")
        h = group_view(mem["h"], 2)
        ident = mem["c"]("ident")
        live = lambda g: not known(g) or 0 <= g < GROUPS

        with nc.Block() as block:
            @block.gpsimd
            def _(pool):
                def step(i, r):
                    if live(2 * i + r):
                        ln.root(pool, 2 * i + r, r % 2)

                skewed(pool, step, GROUPS, 3)

            @block.vector
            def _(dve):
                def own(ins, g, j):
                    ins.then_inc(route, 1)
                    dve.wait_ge(route, ROUTE * g + j)

                def router(g, slot):
                    dve.wait_ge(l_mm, g + 1)
                    own(dve.tensor_tensor(LG[:, slot], psL[0:TOK, 0:4 * NE].rearrange("p (k e) -> p k e", k=4),
                                          W["br"][:].unsqueeze(1).to_broadcast([TOK, 4, NE]), ALU.add), g, 1)
                    own(dve.tensor_reduce(most[:, slot].unsqueeze(2), LG[:, slot], AX.X, ALU.max), g, 2)
                    dve.tensor_tensor(SH[:, slot], LG[:, slot], most[:, slot].unsqueeze(2).to_broadcast([TOK, 4, NE]),
                                      ALU.subtract).then_inc(sh_made, 1)
                    dve.wait_ge(sh_made, g + 1)
                    own(dve.scalar_tensor_tensor(cand[:, slot], SH[:, slot], 0.0,
                                                 mem["c"]("rank8", TOK).unsqueeze(1).to_broadcast([TOK, 4, NE]),
                                                 ALU.is_ge, ALU.mult), g, 3)
                    own(dve.tensor_reduce(best[:, slot].unsqueeze(2), cand[:, slot], AX.X, ALU.max), g, 4)
                    dve.tensor_tensor(OH[:, slot], cand[:, slot], best[:, slot].unsqueeze(2).to_broadcast([TOK, 4, NE]),
                                      ALU.is_equal).then_inc(oh_made, 1)
                    dve.wait_ge(ex_made, g + 1)
                    own(dve.tensor_reduce(total[:, slot].unsqueeze(2), EX[:, slot], AX.X, ALU.add), g, 5)
                    dve.reciprocal(gate[:, slot], total[:, slot]).then_inc(gated, 1)

                def turned(g, slot):
                    dve.wait_ge(oh_mm, g + 1)
                    own(dve.tensor_copy(OHT[:, slot], psH[0:NE, 0:4 * TOK]), g, 6)
                    own(dve.tensor_scalar(pen[:, slot], psH[0:NE, 0:4 * TOK], 1.0, BIG, ALU.subtract, ALU.mult), g, 7)
                    dve.sem_inc(pen_made, 1)

                def step(i, r):
                    s = 2 * i + r
                    if live(s - 2):
                        turned(s - 2, r % 2)
                    if live(s):
                        ln.take(dve, at(h, i, r, 2), s, r % 2)
                    for k in range(4):
                        if live(s - 3):
                            if k == 0:
                                dve.wait_ge(gated, s - 2)
                                stand(dve, mem["passed"]["dve"])
                            dve.wait_ge(y_mm, 4 * (s - 3) + k + 1)
                            x = at(h, i, r - 3, 2)[:, k, :]
                            dve.scalar_tensor_tensor(x, psY[k % 2][0:TOK, 0:D], gate[:, (r - 3) % 2, k:k + 1],
                                                     x, ALU.mult, ALU.add).then_inc(y_added, 1)
                        if k == 0 and live(s):
                            if positive(s - 1):
                                dve.wait_ge(x_mm, s - 1)
                            ln.scale(dve, xn[:, r % 2], at(h, i, r, 2), s, r % 2, normed, last_only=True)
                    if live(s - 1):
                        router(s - 1, (r - 1) % 2)

                skewed(dve, step, GROUPS, 3)

            @block.scalar
            def _(act):
                def step(i, r):
                    s = 2 * i + r
                    if live(s - 1):
                        act.wait_ge(x_mm, s)
                        act.activation(XT[:, (r - 1) % 2], psX[:, 0:4 * TOK], ACT.Copy).then_inc(x_copied, 1)
                    for e in range(NE):
                        if live(s - 2):
                            act.wait_ge(e_mm, NE * (s - 2) + e + 1)
                            act.activation(HID[:, r % 2, e], psE[e % 4][:, 0:4 * TOK], ACT.Relu,
                                           bias=W["b1"][:, e:e + 1]).then_inc(e_relu, 1)
                        if e == 5 and live(s - 1):
                            act.wait_ge(sh_made, s)
                            act.activation(EX[:, (r - 1) % 2], SH[:, (r - 1) % 2], ACT.Exp).then_inc(ex_made, 1)

                skewed(act, step, GROUPS, 3)

            @block.tensor
            def _(pe):
                def second(g, slot, k):
                    if k == 0:
                        pe.wait_ge(e_relu, NE * (g + 1))
                    if positive(4 * g + k - 1):
                        pe.wait_ge(y_added, 4 * g + k - 1)
                    for e in range(NE):
                        pe.matmul(psY[k % 2][0:TOK, 0:D], HID[:, slot, e, k * TOK:(k + 1) * TOK],
                                  W["w2"][:, e, :], start=(e == 0), stop=False)
                    pe.matmul(psY[k % 2][0:TOK, 0:D], OHT[:, slot, k * TOK:(k + 1) * TOK], W["b2"][:],
                              start=False, stop=True).then_inc(y_mm, 1)

                def first(g, slot, e):
                    n = NE * g + e
                    if e == 0:
                        pe.wait_ge(pen_made, g + 1)
                    if positive(n - 3):
                        pe.wait_ge(e_relu, n - 3)
                    pe.matmul(psE[e % 4][:, 0:4 * TOK], W["w1"][:, e, :], XT[:, slot], start=True, stop=False)
                    pe.matmul(psE[e % 4][:, 0:4 * TOK], mem["sel_bf"][:, e, :], pen[:, slot], start=False, stop=True
                              ).then_inc(e_mm, 1)

                def step(i, r):
                    s = 2 * i + r
                    if live(s - 1):
                        if positive(s - 1):
                            pe.wait_ge(x_copied, s - 1)
                        pe.wait_ge(normed, s)
                        for k in range(4):
                            ins = pe.transpose(psX[:, k * TOK:(k + 1) * TOK], xn[:, (r - 1) % 2, k, :],
                                               ident[0:TOK, 0:TOK])
                        ins.then_inc(x_mm, 1)
                    if live(s - 2):
                        pe.wait_ge(oh_made, s - 1)
                        pe.wait_ge(sh_made, s - 1)
                        for k in range(4):
                            ins = pe.transpose(psH[0:NE, k * TOK:(k + 1) * TOK], OH[:, r % 2, k, :],
                                               ident[0:TOK, 0:TOK])
                        ins.then_inc(oh_mm, 1)
                    for k in range(4):
                        if live(s - 3):
                            second(s - 3, (r - 3) % 2, k)
                        if live(s - 2):
                            first(s - 2, r % 2, 2 * k)
                            first(s - 2, r % 2, 2 * k + 1)
                        if k == 1 and live(s - 1):
                            pe.wait_ge(x_copied, s)
                            if positive(s - 1):
                                pe.wait_ge(pen_made, s - 1)
                            for t in range(4):
                                ins = pe.matmul(psL[0:TOK, t * NE:(t + 1) * NE],
                                                XT[:, (r - 1) % 2, t * TOK:(t + 1) * TOK], W["wr"][:],
                                                start=True, stop=True)
                            ins.then_inc(l_mm, 1)

                skewed(pe, step, GROUPS, 3)


LAYERS, HEADS, HD = 3, 4, 32
FB = 4


def retention(nc, ctx, io, mem):
    ITEMS = LAYERS * GROUPS
    COLS = 4 * TOK
    with ExitStack() as here:
        def sb(name, shape, dt=F32):
            return here.enter_context(nc.sbuf_tensor(name, shape, dt))

        def sem(name):
            return here.enter_context(nc.semaphore(name))

        def bank(name):
            return here.enter_context(nc.psum_tensor(name, [128, BANK], F32))

        WA, WC, WD, WB = mem["ret_a"], mem["ret_c"], mem["ret_d"], mem["ret_b2"]
        wa, wc, wd, wb = sb("wa", [D, 6 * D + 2]), sb("wc", [D, 8 + D + 4 * D]), sb("wd", [D, FB * D]), \
            sb("wb", [TOK, D])
        wq, ln1_w, ln1_b = wa[:, 0:6 * D], wa[:, 6 * D:6 * D + 1], wa[:, 6 * D + 1:6 * D + 2]
        gn_w, gn_b, ln2_w, ln2_b, b1 = (wc[:, 0:1], wc[:, 1:2], wc[:, 2:3], wc[:, 3:4], wc[:, 4:8])
        wo, w1 = wc[:, 8:8 + D], wc[:, 8 + D:8 + 5 * D]

        X = mem["X"]
        ln0, ln1, ln2 = Norm(nc, here, "ln_0", mem), Norm(nc, here, "ln_1", mem), Norm(nc, here, "ln_2", mem)
        xn1, xn2 = sb("xn1", [TOK, 2, 4, D]), sb("xn2", [TOK, 2, 4, D])
        XT1, XT3 = sb("XT1", [D, 2, COLS]), sb("XT3", [D, 2, COLS])
        RA, RB = sb("RA", [D, 2, COLS]), sb("RB", [D, 2, COLS])
        QK = sb("QK", [D, 2, 2, COLS])
        TH, SG = sb("TH", [D, 2, COLS]), sb("SG", [D, 2, COLS])
        V = sb("V", [TOK, 2, 4, D])
        AM = sb("AM", [TOK, 2, HEADS, 4, TOK])
        SQ, Yn = sb("SQ", [TOK, 2, 4 * D]), sb("Yn", [TOK, 2, 4, D])
        var, vare, grs = (sb(n, [TOK, 2, 4 * HEADS]) for n in ("gn_var", "gn_vare", "gn_rstd"))
        YA, U = sb("YA", [D, 2, COLS]), sb("U", [D, 2, COLS])
        HID = sb("HID", [128, 2, FB, COLS])
        mean_wv = sb("mean_wv", [D, LAYERS, HEADS])
        wide = [bank(f"wide{j}") for j in range(4)]
        psT, psG, psV, psF = bank("r_psT"), bank("r_psG"), bank("r_psV"), bank("r_psF")

        x0_made, xn1_made, xn2_made = sem("x0_made"), sem("xn1_made"), sem("xn2_made")
        t1_mm, t1_copied = sem("t1_mm"), sem("t1_copied")
        t2_mm, t2_copied = sem("t2_mm"), sem("t2_copied")
        t3_mm, t3_copied = sem("t3_mm"), sem("t3_copied")
        q_mm, rot_mul, rotated = sem("r_q_mm"), sem("rot_mul"), sem("rotated")
        v_mm, v_copied, g_mm, tanhed, sg_made = (sem("r_v_mm"), sem("r_v_copied"), sem("r_g_mm"), sem("tanhed"),
                                                 sem("sg_made"))
        a_mm, masked = sem("a_mm"), sem("masked")
        y_mm, squared, var_made, vare_made, grs_made, yn_made = (
            sem("r_y_mm"), sem("squared"), sem("gvar_made"), sem("gvare_made"), sem("grs_made"), sem("yn_made"))
        gated, wo_mm, wo_added = sem("r_gated"), sem("wo_mm"), sem("wo_added")
        f1_mm, gelued = sem("f1_mm"), sem("gelued")
        f2_mm, f2_added, b2_added = sem("f2_mm"), sem("f2_added"), sem("b2_added")
        centred, took_a, took_c, took_d = sem("centred"), sem("took_a"), sem("took_c"), sem("took_d")
        ident, decay = mem["c"]("ident"), mem["c"]("decay", TOK).rearrange("p (h q) -> p h q", h=HEADS)
        h = group_view(mem["h"], GROUPS)
        live = lambda n: not known(n) or 0 <= n < ITEMS
        group = lambda t, r: t[:].rearrange("p (g k) c -> p g k c", k=4)[:, r % GROUPS]
        per_pos = lambda a: a.rearrange("p (b q) -> p b q", q=NQ)

        with nc.Block() as block:
            @block.gpsimd
            def _(pool):
                def take(dst, src, i, took, waits, part):
                    if not known(i) or i > 0:
                        for sm, v in waits:
                            pool.wait_ge(sm, v)
                        stand(pool, mem["passed"]["pool"])
                    ins = pool.tensor_copy(dst[:], src[:, i, :])
                    if part:
                        ins.then_inc(took, 1)

                def step(i, r):
                    s = 8 * i + r
                    if r == 1 and live(s - 1):
                        take(wa, WA, i, took_a, [(g_mm, 8 * i), (t1_copied, 8 * i)], True)
                    if r == 3 and live(s - 3):
                        take(wc, WC, i, took_c, [(gelued, 32 * i)], False)
                        take(wb, WB, i, took_c, [(b2_added, 8 * i)], True)
                    if known(s) and s + 1 < GROUPS:
                        ln0.root(pool, s + 1, (r + 1) % 2)
                    if live(s):
                        ln1.root(pool, s, r % 2)
                    if r == 3 and live(s - 3):
                        take(wd, WD, i, took_d, [(f2_mm, 8 * i)], True)
                    if live(s - 3):
                        ln2.root(pool, s - 3, (r - 3) % 2)
                    if live(s - 1):
                        for j in range(2):
                            pool.wait_ge(rot_mul, 4 * (s - 1) + 2 * j + 2)
                            pool.tensor_tensor(QK[:, (r - 1) % 2, j], RA[:, j], RB[:, j], ALU.add
                                               ).then_inc(rotated, 1)
                    if live(s - 3):
                        pool.wait_ge(xn2_made, s - 2)
                        if r == 3:
                            pool.wait_ge(took_c, i + 1)
                        x = group(X, r - 3)
                        pool.tensor_tensor(x, x, wb[:].unsqueeze(1).to_broadcast([TOK, 4, D]), ALU.add
                                           ).then_inc(b2_added, 1)
                    if live(s - 2):
                        pool.wait_ge(var_made, s - 1)
                        pool.tensor_tensor(vare[:, r % 2], var[:, r % 2], mem["eps"][0:TOK, :], ALU.add
                                           ).then_inc(vare_made, 1)
                        pool.wait_ge(vare_made, s - 1)
                        pool.tensor_tensor(grs[:, r % 2], vare[:, r % 2], mem["half_neg"][0:TOK, :], ALU.pow
                                           ).then_inc(grs_made, 1)

                ln0.root(pool, 0, 0)
                pool.wait_ge(centred, 3)
                skewed(pool, step, ITEMS, 4, per=8)

            @block.vector
            def _(dve):
                def rest(g):
                    ln0.take(dve, at(h, 0, g, GROUPS), g, g % 2)
                    ln0.scale(dve, group(X, g), at(h, 0, g, GROUPS), g, g % 2, x0_made, last_only=True)

                def step(i, r):
                    s = 8 * i + r
                    a, b, c, d = s - 1, s - 2, s - 3, s - 4
                    if known(s) and s + 1 < GROUPS:
                        rest(s + 1)
                    if live(s):
                        if known(i) and i == 0:
                            dve.wait_ge(x0_made, s + 1)
                        else:
                            dve.wait_ge(f2_added, s - 7)
                        ln1.take(dve, group(X, r), s, r % 2)
                    if live(c):
                        dve.wait_ge(grs_made, c + 1)
                        dve.tensor_tensor(Yn[:, (r - 3) % 2].rearrange("p k (g e) -> p (k g) e", e=HD),
                                          psV[0:TOK, :].rearrange("p (g e) -> p g e", e=HD),
                                          grs[:, (r - 3) % 2].unsqueeze(2).to_broadcast([TOK, 4 * HEADS, HD]), ALU.mult
                                          ).then_inc(yn_made, 1)
                    if live(s):
                        ln1.scale(dve, xn1[:, r % 2], group(X, r), s, r % 2, xn1_made, last_only=True)
                    if live(d):
                        dve.wait_ge(b2_added, d + 1)
                        dve.wait_ge(f2_mm, d + 1)
                        x = group(X, r - 4)
                        dve.tensor_tensor(x, psF[0:TOK, :].rearrange("p (k c) -> p k c", k=4), x, ALU.add
                                          ).then_inc(f2_added, 1)
                    if live(c):
                        dve.wait_ge(t2_copied, c + 1)
                        dve.scalar_tensor_tensor(U[:, (r - 3) % 2], SG[:, (r - 3) % 2], 0.5, YA[:, (r - 3) % 2],
                                                 ALU.mult, ALU.mult).then_inc(gated, 1)
                    if live(b):
                        for j in range(HEADS):
                            dve.wait_ge(a_mm, 4 * b + j + 1)
                            dve.tensor_tensor(AM[:, r % 2, j],
                                              wide[j][0:TOK, 0:COLS].rearrange("p (k q) -> p k q", k=4),
                                              decay[:, j, :].unsqueeze(1).to_broadcast([TOK, 4, TOK]), ALU.mult
                                              ).then_inc(masked, 1)
                    if live(c):
                        dve.wait_ge(wo_mm, c + 1)
                        x = group(X, r - 3)
                        dve.tensor_tensor(x, psG[0:TOK, :].rearrange("p (k c) -> p k c", k=4), x, ALU.add
                                          ).then_inc(wo_added, 1)
                        dve.wait_ge(wo_added, c + 1)
                        ln2.take(dve, x, c, (r - 3) % 2)
                    if live(a):
                        for j in range(4):
                            which, table = j // 2, ("cos" if j % 2 == 0 else "sin") + "qk"[j // 2]
                            if j % 2 == 0:
                                if positive(2 * (a - 1) + which + 1):
                                    dve.wait_ge(rotated, 2 * (a - 1) + which + 1)
                            dve.wait_ge(q_mm, 4 * a + j + 1)
                            dve.tensor_tensor(per_pos((RA, RB)[j % 2][:, which]), per_pos(wide[j][:, 0:COLS]),
                                              mem["c"](table).unsqueeze(1).to_broadcast([D, 8, NQ]), ALU.mult
                                              ).then_inc(rot_mul, 1)
                    if live(c):
                        ln2.scale(dve, xn2[:, (r - 3) % 2], group(X, r - 3), c, (r - 3) % 2, xn2_made, last_only=True)
                    if live(b):
                        dve.wait_ge(squared, b + 1)
                        dve.tensor_reduce(var[:, r % 2].unsqueeze(2),
                                          SQ[:, r % 2].rearrange("p (g e) -> p g e", e=HD), AX.X, ALU.add
                                          ).then_inc(var_made, 1)
                    if live(a):
                        dve.wait_ge(tanhed, a + 1)
                        dve.scalar_tensor_tensor(SG[:, (r - 1) % 2], TH[:, (r - 1) % 2], 1.0, psG[:, 0:COLS],
                                                 ALU.add, ALU.mult).then_inc(sg_made, 1)

                wv = WA[:, :, 4 * D:5 * D].rearrange("p l (h e) -> p l h e", h=HEADS)
                dve.tensor_reduce(mean_wv[:].unsqueeze(3), wv, AX.X, ALU.add).then_inc(centred, 1)
                dve.wait_ge(centred, 1)
                dve.tensor_scalar(mean_wv[:], mean_wv[:], 1.0 / HD, None, ALU.mult).then_inc(centred, 1)
                dve.wait_ge(centred, 2)
                for l in range(LAYERS):
                    ins = dve.tensor_tensor(wv[:, l], wv[:, l],
                                            mean_wv[:, l].unsqueeze(2).to_broadcast([D, HEADS, HD]), ALU.subtract)
                ins.then_inc(centred, 1)
                rest(0)
                skewed(dve, step, ITEMS, 4, per=8)

            @block.scalar
            def _(act):
                def step(i, r):
                    s = 8 * i + r
                    a, b, c = s - 1, s - 2, s - 3
                    if live(a):
                        if r == 1:
                            act.wait_ge(took_a, i + 1)
                        act.wait_ge(t1_mm, a + 1)
                        act.activation(XT1[:, (r - 1) % 2], psT[:, 0:COLS], ACT.Identity, bias=ln1_b, scale=ln1_w
                                       ).then_inc(t1_copied, 1)
                    if live(c):
                        if r == 3:
                            act.wait_ge(took_c, i + 1)
                        act.wait_ge(t2_mm, c + 1)
                        act.activation(YA[:, (r - 3) % 2], psT[:, 0:COLS], ACT.Identity, bias=gn_b, scale=gn_w
                                       ).then_inc(t2_copied, 1)
                    if live(a):
                        act.wait_ge(v_mm, a + 1)
                        act.activation(V[:, (r - 1) % 2].rearrange("p k c -> p (k c)"), psV[0:TOK, :], ACT.Copy
                                       ).then_inc(v_copied, 1)
                    if live(b):
                        act.wait_ge(y_mm, b + 1)
                        act.activation(SQ[:, r % 2], psV[0:TOK, :], ACT.Square, scale=HD ** -0.5
                                       ).then_inc(squared, 1)
                    if live(c):
                        act.wait_ge(t3_mm, c + 1)
                        act.activation(XT3[:, (r - 3) % 2], psT[:, 0:COLS], ACT.Identity, bias=ln2_b, scale=ln2_w
                                       ).then_inc(t3_copied, 1)
                    if live(a):
                        act.wait_ge(g_mm, a + 1)
                        act.activation(TH[:, (r - 1) % 2], psG[:, 0:COLS], ACT.Tanh, scale=0.5).then_inc(tanhed, 1)
                    if live(c):
                        for j in range(FB):
                            act.wait_ge(f1_mm, 4 * c + j + 1)
                            act.activation(HID[:, (r - 3) % 2, j], wide[j][:, 0:COLS], ACT.Gelu, bias=b1[:, j:j + 1]
                                           ).then_inc(gelued, 1)

                skewed(act, step, ITEMS, 4, per=8)

            @block.tensor
            def _(pe):
                def turn(src, slot, done):
                    for k in range(4):
                        ins = pe.transpose(psT[:, k * TOK:(k + 1) * TOK], src[:, slot, k, :], ident[0:TOK, 0:TOK])
                    ins.then_inc(done, 1)

                def step(i, r):
                    s = 8 * i + r
                    a, b, c, d = s - 1, s - 2, s - 3, s - 4
                    if live(a):
                        if positive(c):
                            pe.wait_ge(t3_copied, c)
                        elif positive(a):
                            pe.wait_ge(t1_copied, a)
                        pe.wait_ge(xn1_made, a + 1)
                        turn(xn1, (r - 1) % 2, t1_mm)
                    if live(d):
                        if r == 4:
                            pe.wait_ge(took_d, i + 1)
                        pe.wait_ge(gelued, 4 * d + 4)
                        if positive(d):
                            pe.wait_ge(f2_added, d)
                        for k in range(4):
                            for j in range(FB):
                                ins = pe.matmul(psF[0:TOK, k * D:(k + 1) * D],
                                                HID[:, (r - 4) % 2, j, k * TOK:(k + 1) * TOK],
                                                wd[:, j * D:(j + 1) * D], start=(j == 0), stop=(j == FB - 1))
                        ins.then_inc(f2_mm, 1)
                    if live(c):
                        if live(a):
                            pe.wait_ge(t1_copied, a + 1)
                        elif positive(c):
                            pe.wait_ge(t3_copied, c)
                        pe.wait_ge(yn_made, c + 1)
                        turn(Yn, (r - 3) % 2, t2_mm)
                    if live(b):
                        pe.wait_ge(rotated, 2 * b + 2)
                        for j in range(HEADS):
                            if positive(4 * (c - 1) + j + 1):
                                pe.wait_ge(gelued, 4 * (c - 1) + j + 1)
                            pe.wait_ge(rot_mul, 4 * b + j + 1)
                            rows = slice(j * HD, (j + 1) * HD)
                            for k in range(4):
                                cols = slice(k * TOK, (k + 1) * TOK)
                                ins = pe.matmul(wide[j][0:TOK, cols], QK[rows, r % 2, 1, cols], QK[rows, r % 2, 0, cols],
                                                start=True, stop=True)
                            ins.then_inc(a_mm, 1)
                    if live(c):
                        if r == 3:
                            pe.wait_ge(took_c, i + 1)
                        if live(b):
                            pe.wait_ge(sg_made, b + 1)
                        pe.wait_ge(gated, c + 1)
                        for k in range(4):
                            ins = pe.matmul(psG[0:TOK, k * D:(k + 1) * D], U[:, (r - 3) % 2, k * TOK:(k + 1) * TOK], wo,
                                            start=True, stop=True)
                        ins.then_inc(wo_mm, 1)
                    if live(a):
                        if r == 1:
                            pe.wait_ge(took_a, i + 1)
                        pe.wait_ge(t1_copied, a + 1)
                        if positive(c + 1):
                            pe.wait_ge(yn_made, c + 1)
                        elif positive(a):
                            pe.wait_ge(v_copied, a)
                        for k in range(4):
                            ins = pe.matmul(psV[0:TOK, k * D:(k + 1) * D], XT1[:, (r - 1) % 2, k * TOK:(k + 1) * TOK],
                                            wq[:, 4 * D:5 * D], start=True, stop=True)
                        ins.then_inc(v_mm, 1)
                        for j in range(4):
                            if live(b):
                                pe.wait_ge(masked, 4 * b + j + 1)
                            else:
                                if positive(4 * (a - 1) + j + 1):
                                    pe.wait_ge(rot_mul, 4 * (a - 1) + j + 1)
                            pe.matmul(wide[j][:, 0:COLS], wq[:, j * D:(j + 1) * D], XT1[:, (r - 1) % 2],
                                      start=True, stop=True).then_inc(q_mm, 1)
                    if live(b):
                        pe.wait_ge(masked, 4 * b + 4)
                        if live(a):
                            pe.wait_ge(v_copied, a + 1)
                        elif positive(c + 1):
                            pe.wait_ge(yn_made, c + 1)
                        for k in range(4):
                            for j in range(HEADS):
                                ins = pe.matmul(psV[0:TOK, k * D + j * HD:k * D + (j + 1) * HD],
                                                AM[:, r % 2, j, k, :], V[:, r % 2, k, j * HD:(j + 1) * HD],
                                                start=True, stop=True)
                        ins.then_inc(y_mm, 1)
                    if live(c):
                        pe.wait_ge(t2_copied, c + 1)
                        pe.wait_ge(xn2_made, c + 1)
                        turn(xn2, (r - 3) % 2, t3_mm)
                    if live(a):
                        if live(c):
                            pe.wait_ge(wo_added, c + 1)
                        else:
                            if positive(a):
                                pe.wait_ge(sg_made, a)
                        pe.matmul(psG[:, 0:COLS], wq[:, 5 * D:6 * D], XT1[:, (r - 1) % 2], start=True, stop=True
                                  ).then_inc(g_mm, 1)
                    if live(c):
                        pe.wait_ge(t3_copied, c + 1)
                        for j in range(FB):
                            if live(a):
                                pe.wait_ge(rot_mul, 4 * a + j + 1)
                            elif live(b):
                                pe.wait_ge(masked, 4 * b + j + 1)
                            else:
                                pe.wait_ge(gelued, 4 * (c - 1) + j + 1)
                            pe.matmul(wide[j][:, 0:COLS], w1[:, j * D:(j + 1) * D], XT3[:, (r - 3) % 2],
                                      start=True, stop=True).then_inc(f1_mm, 1)

                skewed(pe, step, ITEMS, 4, per=8)


NR, CAP = 64, 128


def routed_network(nc, ctx, io, mem):
    COLS = 4 * TOK
    with ExitStack() as here:
        def sb(name, shape, dt=F32):
            return here.enter_context(nc.sbuf_tensor(name, shape, dt))

        def sem(name):
            return here.enter_context(nc.semaphore(name))

        def bank(name):
            return here.enter_context(nc.psum_tensor(name, [128, BANK], F32))

        W = mem["w4"]
        ln = Norm(nc, here, "ln_c", mem)
        xn, XT = sb("c_xn", [TOK, 2, 4, D]), sb("c_XT", [D, 2, COLS])
        HID = sb("c_HID", [128, 2, FB, COLS])
        R4 = [TOK, 2, 4, NR]
        LG, SH, EX, C1, C2, OH1, OH2, S2, D2, KE, KX = (
            sb("c_" + n, R4) for n in ("LG", "SH", "EX", "C1", "C2", "OH1", "OH2", "S2", "D2", "KE", "KX"))
        M = sb("c_M", R4, BF16)
        chosen = sb("chosen", [TOK, NR])
        before_all = sb("before_all", [TOK, 2, NR], BF16)
        m1, b1, m2, b2, total, inverse, kept, weight = (
            sb("c_" + n, [TOK, 2, 4]) for n in ("m1", "b1", "m2", "b2", "total", "inverse", "kept", "weight"))
        BH, OUT = sb("BH", [TOK, 4, D]), sb("OUT", [TOK, 2, 4, D])
        psX, psL, psP, psY = bank("c_psX"), bank("c_psL"), bank("c_psP"), bank("c_psY")
        wide = [bank(f"c_wide{j}") for j in range(FB)]

        summed, normed, x_mm, x_copied = sem("summed"), sem("c_normed"), sem("c_x_mm"), sem("c_x_copied")
        l_mm, sh_made, ex_made = sem("c_l_mm"), sem("c_sh_made"), sem("c_ex_made")
        ROUTE = 12
        route = sem("c_route")
        keep = sem("keep")
        m_made, prior_made, p_mm = sem("m_made"), sem("prior_made"), sem("c_p_mm")
        f1_mm, gelued = sem("c_f1_mm"), sem("c_gelued")
        f2_mm, biased, out_made = sem("c_f2_mm"), sem("biased"), sem("out_made")
        stored = mem["stored"]
        h, X = group_view(mem["h"], 2), group_view(mem["X"], 2)
        ident = mem["c"]("ident")
        live = lambda g: not known(g) or 0 <= g < GROUPS
        out = io["out"].rearrange("(i r k a) q d -> i r (a q) k d", r=2, k=4, a=2)

        with nc.Block() as block:
            @block.sync
            def _(sp):
                def step(i, r):
                    s = 2 * i + r
                    if live(s - 2):
                        sp.wait_ge(out_made, s - 1)
                        stand(sp, mem["passed"]["sp"])
                        sp.dma_start(out[i + (r - 2) // 2, r % 2], OUT[:, r % 2]).then_inc(stored[r % 2], 16)

                skewed(sp, step, GROUPS, 2, peel=2)
                for j in range(2):
                    sp.wait_ge(stored[j], 16 * GROUPS // 2)

            @block.gpsimd
            def _(pool):
                def step(i, r):
                    s = 2 * i + r
                    if live(s):
                        x = at(h, i, r, 2)
                        pool.tensor_tensor(x, x, at(X, i, r, 2), ALU.add).then_inc(summed, 1)
                        ln.root(pool, s, r % 2)

                skewed(pool, step, GROUPS, 2, peel=2)

            @block.vector
            def _(dve):
                def own(ins, g, j):
                    ins.then_inc(route, 1)
                    dve.wait_ge(route, ROUTE * g + j)

                def over(a):
                    return a.unsqueeze(2).to_broadcast([TOK, 4, NR])

                def router(g, o):
                    rank = mem["c"]("rank64", TOK).unsqueeze(1).to_broadcast([TOK, 4, NR])
                    dve.wait_ge(l_mm, g + 1)
                    own(dve.tensor_reduce(m1[:, o].unsqueeze(2), psL[0:TOK, 0:4 * NR].rearrange("p (k e) -> p k e", k=4),
                                          AX.X, ALU.max), g, 1)
                    dve.tensor_tensor(SH[:, o], psL[0:TOK, 0:4 * NR].rearrange("p (k e) -> p k e", k=4), over(m1[:, o]),
                                      ALU.subtract).then_inc(sh_made, 1)
                    dve.wait_ge(sh_made, g + 1)
                    own(dve.scalar_tensor_tensor(C1[:, o], SH[:, o], 0.0, rank, ALU.is_ge, ALU.mult), g, 2)
                    own(dve.tensor_reduce(b1[:, o].unsqueeze(2), C1[:, o], AX.X, ALU.max), g, 3)
                    own(dve.tensor_tensor(OH1[:, o], C1[:, o], over(b1[:, o]), ALU.is_equal), g, 4)
                    own(dve.scalar_tensor_tensor(S2[:, o], OH1[:, o], LOWEST, SH[:, o], ALU.mult, ALU.add), g, 5)
                    own(dve.tensor_reduce(m2[:, o].unsqueeze(2), S2[:, o], AX.X, ALU.max), g, 6)
                    own(dve.tensor_tensor(D2[:, o], S2[:, o], over(m2[:, o]), ALU.subtract), g, 7)
                    own(dve.scalar_tensor_tensor(C2[:, o], D2[:, o], 0.0, rank, ALU.is_ge, ALU.mult), g, 8)
                    own(dve.tensor_reduce(b2[:, o].unsqueeze(2), C2[:, o], AX.X, ALU.max), g, 9)
                    own(dve.tensor_tensor(OH2[:, o], C2[:, o], over(b2[:, o]), ALU.is_equal), g, 10)
                    dve.tensor_tensor(M[:, o], OH1[:, o], OH2[:, o], ALU.add).then_inc(m_made, 1)
                    dve.wait_ge(m_made, g + 1)
                    own(dve.tensor_reduce(chosen[:].unsqueeze(2), M[:, o].rearrange("p k e -> p e k"), AX.X, ALU.add),
                        g, 11)
                    dve.tensor_tensor(before_all[:, 1 - o], before_all[:, o], chosen[:], ALU.add).then_inc(prior_made, 1)
                    dve.wait_ge(ex_made, g + 1)
                    own(dve.tensor_reduce(total[:, o].unsqueeze(2), EX[:, o], AX.X, ALU.add), g, 12)
                    dve.reciprocal(inverse[:, o], total[:, o])

                def step(i, r):
                    s = 2 * i + r
                    g, o = s - 2, r % 2
                    if live(g):
                        dve.wait_ge(p_mm, g + 1)
                        dve.scalar_tensor_tensor(KE[:, o], psP[0:TOK, 0:4 * NR].rearrange("p (k e) -> p k e", k=4),
                                                 float(CAP), M[:, o], ALU.is_lt, ALU.mult).then_inc(keep, 1)
                        dve.wait_ge(keep, 5 * g + 1)
                        dve.tensor_tensor(KX[:, o], KE[:, o], EX[:, o], ALU.mult).then_inc(keep, 1)
                        dve.wait_ge(keep, 5 * g + 2)
                        dve.tensor_reduce(kept[:, o].unsqueeze(2), KX[:, o], AX.X, ALU.add).then_inc(keep, 1)
                        dve.wait_ge(keep, 5 * g + 3)
                        dve.tensor_tensor(weight[:, o], kept[:, o], inverse[:, o], ALU.mult).then_inc(keep, 1)
                        dve.wait_ge(keep, 5 * g + 4)
                        stand(dve, mem["passed"]["dve"])
                        x = at(h, i, r - 2, 2)
                        for k in range(4):
                            ins = dve.scalar_tensor_tensor(BH[:, k], W["b2"][:], weight[:, o, k:k + 1], x[:, k, :],
                                                           ALU.mult, ALU.add)
                        ins.then_inc(keep, 1)
                        dve.wait_ge(keep, 5 * g + 5)
                        if positive(16 * (i - 1)):
                            dve.wait_ge(stored[o], 16 * (i - 1))
                        dve.wait_ge(f2_mm, g + 1)
                        for k in range(4):
                            ins = dve.scalar_tensor_tensor(OUT[:, o, k], psY[0:TOK, k * D:(k + 1) * D],
                                                           weight[:, o, k:k + 1], BH[:, k], ALU.mult, ALU.add)
                        ins.then_inc(out_made, 1)
                    if live(s):
                        dve.wait_ge(summed, s + 1)
                        stand(dve, mem["passed"]["dve"])
                        ln.take(dve, at(h, i, r, 2), s, r % 2)
                        if positive(s - 1):
                            dve.wait_ge(x_mm, s - 1)
                        ln.scale(dve, xn[:, r % 2], at(h, i, r, 2), s, r % 2, normed, last_only=True)
                    if live(s - 1):
                        router(s - 1, (r - 1) % 2)

                dve.memset(before_all[:, 0], 0.0).then_inc(prior_made, 1)
                dve.wait_ge(prior_made, 1)
                skewed(dve, step, GROUPS, 2, peel=2)

            @block.scalar
            def _(act):
                def step(i, r):
                    s = 2 * i + r
                    if live(s - 1):
                        o = (r - 1) % 2
                        act.wait_ge(x_mm, s)
                        act.activation(XT[:, o], psX[:, 0:COLS], ACT.Copy).then_inc(x_copied, 1)
                        act.wait_ge(sh_made, s)
                        act.activation(EX[:, o], SH[:, o], ACT.Exp).then_inc(ex_made, 1)
                        for j in range(FB):
                            act.wait_ge(f1_mm, 4 * (s - 1) + j + 1)
                            act.activation(HID[:, o, j], wide[j][:, 0:COLS], ACT.Gelu, bias=W["b1"][:, j:j + 1]
                                           ).then_inc(gelued, 1)

                skewed(act, step, GROUPS, 2, peel=2)

            @block.tensor
            def _(pe):
                def step(i, r):
                    s = 2 * i + r
                    o, a = r % 2, (r - 1) % 2
                    if live(s - 1):
                        if positive(s - 1):
                            pe.wait_ge(x_copied, s - 1)
                        pe.wait_ge(normed, s)
                        for k in range(4):
                            ins = pe.transpose(psX[:, k * TOK:(k + 1) * TOK], xn[:, a, k, :], ident[0:TOK, 0:TOK])
                        ins.then_inc(x_mm, 1)
                    if live(s - 2):
                        g = s - 2
                        pe.wait_ge(m_made, g + 1)
                        pe.wait_ge(prior_made, g + 1)
                        if positive(5 * (g - 1) + 1):
                            pe.wait_ge(keep, 5 * (g - 1) + 1)
                        for k in range(4):
                            parts = [(mem["ones_bf"][:], before_all[:, o])]
                            parts += [(mem["ones_bf"][:], M[:, o, j]) for j in range(k)]
                            parts += [(mem["before_bf"][:], M[:, o, k])]
                            for n, (left, right) in enumerate(parts):
                                ins = pe.matmul(psP[0:TOK, k * NR:(k + 1) * NR], left, right, start=(n == 0),
                                                stop=(n == len(parts) - 1))
                        ins.then_inc(p_mm, 1)
                        pe.wait_ge(gelued, 4 * g + 4)
                        if positive(g):
                            pe.wait_ge(out_made, g)
                        for k in range(4):
                            for j in range(FB):
                                ins = pe.matmul(psY[0:TOK, k * D:(k + 1) * D], HID[:, o, j, k * TOK:(k + 1) * TOK],
                                                W["w2"][:, j, :], start=(j == 0), stop=(j == FB - 1))
                        ins.then_inc(f2_mm, 1)
                    if live(s - 1):
                        pe.wait_ge(x_copied, s)
                        if positive(s - 1):
                            pe.wait_ge(sh_made, s - 1)
                        for k in range(4):
                            ins = pe.matmul(psL[0:TOK, k * NR:(k + 1) * NR], XT[:, a, k * TOK:(k + 1) * TOK], W["wr"][:],
                                            start=True, stop=True)
                        ins.then_inc(l_mm, 1)
                        for j in range(FB):
                            if positive(4 * (s - 2) + j + 1):
                                pe.wait_ge(gelued, 4 * (s - 2) + j + 1)
                            pe.matmul(wide[j][:, 0:COLS], W["w1"][:, j * D:(j + 1) * D], XT[:, a], start=True, stop=True
                                      ).then_inc(f1_mm, 1)

                skewed(pe, step, GROUPS, 2, peel=2)


def store(nc, ctx, io, mem, src):
    with nc.semaphore("stored") as stored, nc.Block() as block:
        @block.sync
        def _(sp):
            sp.dma_start(io["out"].rearrange("(t a) q d -> (a q) t d", a=2), src[:]).then_inc(stored, 16)
            sp.wait_ge(stored, 16)


STAGE = 4


def tower(nc, io):
    with ExitStack() as ctx:
        def sb(name, shape, dt=F32):
            return ctx.enter_context(nc.sbuf_tensor(name, shape, dt))

        mem = {"h": sb("h", [TOK, TILES, D]), "consts": sb("consts", [128, CONST_ARRAY.shape[1]]),
               "ones_bf": sb("ones_bf", [TOK, TOK], BF16), "before_bf": sb("before_bf", [TOK, TOK], BF16),
               "half_neg": sb("half_neg", [128, 16]), "eps": sb("eps", [128, 16])}

        def c(name, parts=128):
            a, b = CONSTS[name]
            return mem["consts"][0:parts, a:b]

        mem["c"] = c
        mem["bias_in"] = ctx.enter_context(nc.semaphore("bias_in"))
        mem["passed"] = {k: ctx.enter_context(nc.semaphore("passed_" + k)) for k in ("dve", "sp", "pool", "act")}
        mem["stored"] = [ctx.enter_context(nc.semaphore(f"stored{i}")) for i in range(2)]
        mem["ones_set"] = ctx.enter_context(nc.semaphore("ones_set"))
        mem["w1"] = {"qkv": sb("w1_qkv", [D, 3, 512]), "o": sb("w1_o", [128, 4, D])}
        mem["X"] = sb("X", [TOK, TILES, D])
        mem["w2"] = {"wr": sb("w2_wr", [D, NE]), "br": sb("w2_br", [TOK, NE]), "w1": sb("w2_w1", [D, NE, D]),
                     "b1": sb("w2_b1", [D, NE]), "w2": sb("w2_w2", [D, NE, D]), "b2": sb("w2_b2", [NE, D])}
        mem["ret_a"] = sb("ret_a", [D, LAYERS, 6 * D + 2])
        mem["ret_c"] = sb("ret_c", [D, LAYERS, 8 + 5 * D])
        mem["ret_d"] = sb("ret_d", [D, LAYERS, FB * D])
        mem["ret_b2"] = sb("ret_b2", [TOK, LAYERS, D])
        mem["w4"] = {"wr": sb("w4_wr", [D, NR]), "w1": sb("w4_w1", [D, FB * D]), "b1": sb("w4_b1", [D, FB]),
                     "w2": sb("w4_w2", [D, FB, D]), "b2": sb("w4_b2", [TOK, D])}
        mem["sel_bf"] = sb("sel_bf", [NE, NE, D], BF16)
        mem["later_in"] = ctx.enter_context(nc.semaphore("later_in"))
        mem["xT_in"], mem["xtok_in"] = [[ctx.enter_context(nc.semaphore(f"{n}{j}")) for j in range(2)]
                                        for n in ("xT_in", "xtok_in")]
        with ExitStack() as first:
            def sb1(name, shape):
                return first.enter_context(nc.sbuf_tensor(name, shape, F32))

            mem.update(WpT=sb1("WpT", [128, 6, D]), VT=sb1("VT", [128, H0, VD + 1]), BT=sb1("BT", [AUG, H0, AUG]),
                       bias=sb1("bias", [TOK, PAIRS, N]),
                       bias3=first.enter_context(nc.sbuf_tensor("bias3", [TOK, 3 * PAIRS, N], BF16)), xtok=sb1("xtok", [HALF, 2, 4, 2, AUG]),
                       xT=sb1("xT", [AUG, 2, 4, N]), proj_c=sb1("proj_c", [TOK, D]), half=sb1("half", [TOK, 1]))
            setup(nc, ctx, io, mem)
            token_attention(nc, ctx, io, mem)
        if STAGE >= 1:
            head_attention(nc, ctx, io, mem)
        if STAGE >= 2:
            top1_experts(nc, ctx, io, mem)
        if STAGE >= 3:
            retention(nc, ctx, io, mem)
        if STAGE >= 4:
            routed_network(nc, ctx, io, mem)
        else:
            store(nc, ctx, io, mem, mem["X"] if STAGE == 3 else mem["h"])


def kernel(**inputs):
    import numpy as _np
    import concourse.bacc as _bacc
    from concourse import mybir as _mybir
    from concourse.bass_utils import run_bass_kernel_spmd as _run

    a = {k: _np.asarray(v) for k, v in inputs.items()}
    halves = lambda v: v.reshape(v.shape[:-1] + (HALF, 2)).swapaxes(-1, -2)
    laid = {
        "x": a["x"],
        "xT": halves(a["x"].transpose(2, 0, 1)).reshape(D_IN, B, N),
        "kv_w": a["L0_tok_kv_w"], "q_w": a["L0_tok_q_w"], "projT": a["L0_tok_proj_w"].T,
        "ab": a["L0_tok_attention_biases"].T, "idx": halves(a["L0_tok_bias_idxs"]),
        "consts": CONST_ARRAY,
    }
    for w in "qkv":
        laid["a_" + w] = a[f"L0_attn_W_{w.upper()}"].transpose(2, 0, 1).reshape(D, 512)
    laid["b_wr"], laid["b_br"], laid["b_b2"] = a["L0_ffn_Wr"], a["L0_ffn_br"], a["L0_ffn_b2"]
    laid["b_w1"] = a["L0_ffn_W1"].transpose(1, 0, 2)
    laid["b_w2"] = a["L0_ffn_W2"].transpose(1, 0, 2)
    laid["b_b1"] = a["L0_ffn_b1"].T
    r = {k[8:]: v for k, v in a.items() if k.startswith("L1_attn_")}
    flat = lambda v: v.transpose(2, 0, 1, 3).reshape(D, LAYERS, D)
    swap = lambda v: v.reshape(v.shape[:-1] + (-1, 2))[..., ::-1].reshape(v.shape)
    laid["r_wq"], laid["r_wk"], laid["r_wv"] = flat(r["WQ"]), flat(r["WK"]), flat(r["WV"])
    laid["r_wqs"], laid["r_wks"] = swap(laid["r_wq"]), swap(laid["r_wk"])
    laid["r_wg"], laid["r_wo"] = r["WG"].transpose(1, 0, 2), r["WO"].transpose(1, 0, 2)
    laid["r_ln1"] = _np.stack([r["ln1_w"], r["ln1_b"]], -1).transpose(1, 0, 2)
    laid["r_small"] = _np.concatenate(
        [_np.stack([r["gn_w"], r["gn_b"], r["ln2_w"], r["ln2_b"]], -1).transpose(1, 0, 2),
         r["ffn_b1"].reshape(LAYERS, FB, D).transpose(2, 0, 1)], -1)
    laid["r_w1"] = r["ffn_w1"].transpose(1, 0, 2)
    laid["r_w2"] = r["ffn_w2"].reshape(LAYERS, FB, D, D).transpose(2, 0, 1, 3).reshape(D, LAYERS, FB * D)
    laid["r_b2"] = r["ffn_b2"]
    laid["c_wr"], laid["c_w1"] = a["L1_ffn_router_w"].T, a["L1_ffn_w1"].T
    laid["c_b1"] = a["L1_ffn_b1"].reshape(FB, D).T
    laid["c_w2"] = a["L1_ffn_w2"].T.reshape(FB, D, D).transpose(1, 0, 2)
    laid["c_b2"] = a["L1_ffn_b2"]
    laid["a_o"] = a["L0_attn_W_O"].T
    for w in ("kv", "q", "proj"):
        four = _np.stack([a[f"L0_tok_{w}_{k}"] for k in "gbmv"])
        laid[w + "_bn"] = four.T if w == "proj" else four.reshape(4, H0, -1).transpose(2, 0, 1)
    nc = _bacc.Bacc("TRN2", target_bir_lowering=False, num_devices=1)
    io, arrays = {}, {}
    for name, v in laid.items():
        v = _np.ascontiguousarray(v)
        arrays["in_" + name] = v
        io[name] = nc.dram_tensor("in_" + name, v.shape, _mybir.dt.from_np(v.dtype), kind="ExternalInput").ap()
    io["out"] = nc.dram_tensor("out", (B, NQ, D), F32, kind="ExternalOutput").ap()
    tower(nc, io)
    r = _run(nc, [arrays], core_ids=[0])
    return r.results[0]["out"]
```

```python
from contextlib import ExitStack

import concourse.bass as bass
from concourse import mybir
import numpy as np

F32 = mybir.dt.float32
F32R = mybir.dt.float32r
BF16 = mybir.dt.bfloat16
I32 = mybir.dt.int32
ALU = mybir.AluOpType
ACT = mybir.ActivationFunctionType
AX = mybir.AxisListType

B, N, NQ = 64, 196, 49
D_IN, D = 96, 128
H0, KD, VD = 12, 32, 64
HALF = N // 2
TOK = 2 * NQ
TILES = B * NQ // TOK
AUG = D_IN + 1
OFFS = 196
PAIRS = H0 // 2
EPS = 1e-5
LOWEST = -3.0e38
BANK = 512

CONSTS = {}


def _constants():
    p = np.arange(128)
    parts = []

    def put(name, a):
        full = np.zeros((128,) + a.shape[1:], np.float32)
        full[:a.shape[0]] = a
        full = full.reshape(128, -1)
        at = sum(x.shape[1] for x in parts)
        CONSTS[name] = (at, at + full.shape[1])
        parts.append(full)

    put("entry", np.stack([p, p + HALF], 1).astype(np.float32))
    put("ident", np.eye(128, dtype=np.float32))
    t = np.arange(TOK)
    same = (t[:, None] // NQ) == (t[None, :] // NQ)
    put("after", (same & (t[:, None] > t[None, :])).astype(np.float32))
    put("before", (t[:, None] < t[None, :]).astype(np.float32))
    later = (NQ - 1 - t % NQ).astype(np.float32)
    put("later", later[:, None])
    put("floor", np.where(later > 0, 0.0, LOWEST).astype(np.float32)[:, None])
    put("rank8", np.tile(8.0 - np.arange(8), (TOK, 1)))
    put("rank64", np.tile(64.0 - np.arange(64), (TOK, 1)))
    put("sel", np.repeat(np.eye(8)[:, :, None], D, 2))
    heads, hd = 4, 32
    gam = (1.0 - np.exp(np.linspace(np.log(1.0 / 32.0), np.log(1.0 / 512.0), heads))).astype(np.float32)
    nm = t[None, :] - t[:, None]
    dec = np.where((same & (nm >= 0))[:, None, :],
                   gam.astype(np.float64)[None, :, None] ** np.maximum(nm, 0)[:, None, :], 0.0)
    put("decay", dec.astype(np.float32))
    half = hd // 2
    s = (np.arange(half) + 0.4 * hd) / (1.4 * hd)
    pos = np.arange(NQ)
    scale = s[:, None] ** (pos[None, :] / 512.0)
    ang = pos[None, :] / 10000.0 ** (np.arange(half)[:, None] / half)
    for name, sc in (("q", scale), ("k", 1.0 / scale)):
        cos = np.repeat(np.cos(ang) * sc, 2, 0)
        sin = np.repeat(np.sin(ang) * sc, 2, 0)
        sin[0::2] *= -1.0
        put("cos" + name, np.tile(cos, (heads, 1)).astype(np.float32))
        put("sin" + name, np.tile(sin, (heads, 1)).astype(np.float32))
    return np.ascontiguousarray(np.concatenate(parts, 1))


CONST_ARRAY = _constants()


def known(v):
    return isinstance(v, (int, float))


def positive(count):
    return not known(count) or count > 0


def stand(eng, passed):
    eng.sem_inc(passed, 1)


def product(pe, out, left, right):
    pe.matmul(out, left[0], right[0], start=True, stop=False)
    pe.matmul(out, left[1], right[0], start=False, stop=False)
    return pe.matmul(out, left[0], right[1], start=False, stop=True)


def load_features(sp, io, mem, i, par):
    x = io["xT"].rearrange("d (i q b) k -> i q d b k", q=2, b=4)
    sp.dma_start(mem["xT"][0:D_IN, par, :, :], x[i, par]).then_inc(mem["xT_in"][par], 16)


def load_tokens(sp, io, mem, i, par):
    x = io["x"].rearrange("(i q b) (p t) d -> i q b p t d", q=2, b=4, t=2)
    for b in range(4):
        sp.dma_start(mem["xtok"][:, par, b, :, 0:D_IN], x[i, par, b]).then_inc(mem["xtok_in"][par], 16)


def start_loads(sp, loads, loaded):
    for dst, src in loads:
        sp.dma_start(dst, src).then_inc(loaded, 16)
    return 16 * len(loads)


def first_weights(io, mem):
    loads = [(mem["w1"]["qkv"][:, j, :], io[f"a_{w}"]) for j, w in enumerate("qkv")]
    loads.append((mem["w1"]["o"][:], io["a_o"].rearrange("(k p) o -> p k o", p=128)))
    w = mem["w2"]
    loads += [(w["wr"][:], io["b_wr"]), (w["br"][:], io["b_br"].unsqueeze(0).to_broadcast([TOK, NE])),
              (w["w1"][:], io["b_w1"]), (w["b1"][:], io["b_b1"]), (w["w2"][:], io["b_w2"]), (w["b2"][:], io["b_b2"])]
    return loads


def last_weights(io, mem):
    a, c, d = mem["ret_a"], mem["ret_c"], mem["ret_d"]
    loads = [(a[:, :, j * D:(j + 1) * D], io["r_" + n]) for j, n in enumerate(("wq", "wqs", "wk", "wks", "wv", "wg"))]
    loads += [(a[:, :, 6 * D:], io["r_ln1"]), (c[:, :, 0:8], io["r_small"]), (c[:, :, 8:8 + D], io["r_wo"]),
              (c[:, :, 8 + D:], io["r_w1"]), (d[:], io["r_w2"]),
              (mem["ret_b2"][:], io["r_b2"].unsqueeze(0).to_broadcast([TOK, LAYERS, D]))]
    w = mem["w4"]
    loads += [(w["wr"][:], io["c_wr"]), (w["w1"][:], io["c_w1"]), (w["b1"][:], io["c_b1"]), (w["w2"][:], io["c_w2"]),
              (w["b2"][:], io["c_b2"].unsqueeze(0).to_broadcast([TOK, D]))]
    return loads


def setup(nc, ctx, io, mem):
    NCH = 7
    CH = NQ * N // NCH
    BLK = CH // 4
    LOADS = (0, 1, 4, NCH)
    with ExitStack() as here:
        def sb(name, shape, dt=F32):
            return here.enter_context(nc.sbuf_tensor(name, shape, dt))

        def sem(name):
            return here.enter_context(nc.semaphore(name))

        table = sb("table", [HALF, 2, H0])
        rest1 = sb("rest1", [HALF, 2, H0])
        rest2 = sb("rest2", [HALF, 2, H0])
        parts = sb("parts", [HALF, 2, 3, H0], BF16)
        idx = sb("idx", [HALF, NCH, CH], I32)
        onehot = sb("onehot", [HALF, 2, 2, CH], BF16)
        gathered = sb("gathered", [3 * H0, NCH * CH], BF16)
        kw = sb("kw", [KD, H0, AUG])
        qw = sb("qw", [KD, H0, AUG])
        vw = sb("vw", [VD, H0, AUG])
        bn = {k: sb("bn_" + k, shape) for k, shape in
              (("k", [KD, 4, H0]), ("q", [KD, 4, H0]), ("v", [VD, 4, H0]), ("p", [D, 4, 1]))}
        rs = {k: sb("rs_" + k, list(bn[k].shape)[:1] + list(bn[k].shape)[2:]) for k in bn}
        wide_p = sb("wide_p", [D, 2, D])
        epsb = sb("epsb", [D, H0])
        expo = sb("expo", [D, H0])
        scratch = nc.dram_tensor("bias_scratch", (3 * H0, NQ * N), BF16, kind="Internal").ap()

        bank = [here.enter_context(nc.psum_tensor(f"setup_bank{i}", [128, BANK], F32)) for i in range(8)]

        table_in = sem("table_in")
        idx_in = [sem(f"idx_in{n}") for n in range(3)]
        bn_in, w_in = sem("bn_in"), sem("w_in")
        split = sem("split")
        oh_made = sem("oh_made")
        g_mm = sem("g_mm")
        g_copied = sem("g_copied")
        g_out = sem("g_out")
        fills = sem("fills")
        var_eps = sem("var_eps")
        rstd = sem("rstd")
        folded = sem("folded")
        bt_mm, bt_high = sem("bt_mm"), sem("bt_high")
        done = sem("setup_done")
        bias_in = mem["bias_in"]
        consts, WpT, VT, BT = mem["consts"], mem["WpT"], mem["VT"], mem["BT"]
        ident = mem["c"]("ident")
        entry = mem["c"]("entry", HALF)
        idx_flat = io["idx"].rearrange("a b c -> (a b c)")

        with nc.Block() as block:
            @block.sync
            def _(sp):
                sp.dma_start(table[:], io["ab"].rearrange("(t p) h -> p t h", t=2)).then_inc(table_in, 16)
                sp.dma_start(entry, io["consts"][0:HALF, 0:2]).then_inc(table_in, 16)
                for n, (c, end) in enumerate(zip(LOADS, LOADS[1:])):
                    sp.dma_start(idx[:, c:end, :].rearrange("p n c -> p (n c)"),
                                 idx_flat[c * CH:end * CH].unsqueeze(0).to_broadcast([HALF, (end - c) * CH])
                                 ).then_inc(idx_in[n], 16)
                sp.wait_ge(mem["ones_set"], 1)
                for par in range(2):
                    load_features(sp, io, mem, 0, par)
                    load_tokens(sp, io, mem, 0, par)
                for c, n in ((0, 4), (4, NCH - 4)):
                    sp.wait_ge(g_copied, c + n)
                    sp.dma_start(scratch[:, c * CH:(c + n) * CH], gathered[:, c * CH:(c + n) * CH]
                                 ).then_inc(g_out, 16)
                sp.wait_ge(g_out, 32)
                for par in range(2):
                    sp.dma_start(mem["bias3"][par * NQ:(par + 1) * NQ, :, :],
                                 scratch.rearrange("(s r) (q k) -> r q s k", r=2, q=NQ)[par]
                                 ).then_inc(bias_in, 16)

            @block.scalar
            def _(act):
                act.dma_start(bn["k"][:], io["kv_bn"][0:KD]).then_inc(bn_in, 16)
                act.dma_start(bn["q"][:], io["q_bn"]).then_inc(bn_in, 16)
                act.dma_start(bn["v"][:], io["kv_bn"][KD:KD + VD]).then_inc(bn_in, 16)
                act.dma_start(bn["p"][:], io["proj_bn"].unsqueeze(2)).then_inc(bn_in, 16)
                kv = io["kv_w"].rearrange("(h e) d -> e h d", h=H0)
                act.dma_start(kw[:, :, 0:D_IN], kv[0:KD]).then_inc(w_in, 16)
                act.dma_start(qw[:, :, 0:D_IN], io["q_w"].rearrange("(h e) d -> e h d", h=H0)).then_inc(w_in, 16)
                act.dma_start(vw[:, :, 0:D_IN], kv[KD:KD + VD]).then_inc(w_in, 16)
                act.dma_start(WpT[:], io["projT"].rearrange("(k p) o -> p k o", p=D)).then_inc(w_in, 16)
                act.dma_start(consts[:, 2:], io["consts"][:, 2:]).then_inc(w_in, 16)
                for c in range(NCH):
                    act.wait_ge(g_mm, c + 1)
                    for j in range(4):
                        at = c * CH + j * BLK
                        ins = act.activation(gathered[:, at:at + BLK], bank[(c % 2) * 4 + j][0:3 * H0, 0:BLK],
                                             ACT.Copy)
                    ins.then_inc(g_copied, 1)
                act.wait_ge(bt_mm, 1)
                for j in range(3):
                    ins = act.activation(BT[0][:, 4 * j:4 * j + 4, :],
                                         bank[j][0:AUG, 0:4 * AUG].rearrange("p (a b) -> p a b", a=4), ACT.Copy)
                ins.then_inc(bt_high, 1)
                for j in range(2):
                    ins = act.activation(VT[0:AUG, 6 * j:6 * j + 6, 0:VD],
                                         bank[3 + j][0:AUG, 0:6 * VD].rearrange("p (a b) -> p a b", a=6), ACT.Copy)
                ins.then_inc(done, 1)

            @block.gpsimd
            def _(pool):
                pool.memset(epsb[:], EPS)
                pool.memset(expo[:], -0.5)
                pool.memset(mem["ones_bf"][:], 1.0)
                pool.memset(mem["half_neg"][:], -0.5)
                pool.memset(mem["eps"][:], EPS)
                pool.memset(mem["half"][:], 0.5)
                pool.memset(mem["xtok"][:], 1.0)
                pool.memset(VT[:], 0.0).then_inc(fills, 1)
                pool.wait_ge(fills, 1)
                pool.memset(VT[D_IN:AUG, :, VD:VD + 1], 1.0).then_inc(fills, 1)
                pool.wait_ge(fills, 2)
                pool.memset(mem["xT"][D_IN:AUG, :, :, :], 1.0).then_inc(mem["ones_set"], 1)
                pool.wait_ge(mem["ones_set"], 1)
                pool.wait_ge(bn_in, 16 * 4)
                for k in "kqvp":
                    v = bn[k][:, 3, :]
                    e, w = v.shape
                    ins = pool.tensor_tensor(rs[k][:], v, epsb[0:e, 0:w], ALU.add)
                ins.then_inc(var_eps, 1)
                pool.wait_ge(var_eps, 1)
                for k in "kqvp":
                    e, w = rs[k].shape
                    ins = pool.tensor_tensor(rs[k][:], rs[k][:], expo[0:e, 0:w], ALU.pow)
                ins.then_inc(rstd, 1)

            @block.vector
            def _(dve):
                steps = [0]

                def link(ins):
                    steps[0] += 1
                    ins.then_inc(split, 1)
                    dve.wait_ge(split, steps[0])

                dve.wait_ge(table_in, 32)
                link(dve.tensor_copy(parts[:, :, 0], table[:]))
                link(dve.tensor_tensor(rest1[:], table[:], parts[:, :, 0], ALU.subtract))
                link(dve.tensor_copy(parts[:, :, 1], rest1[:]))
                link(dve.tensor_tensor(rest2[:], rest1[:], parts[:, :, 1], ALU.subtract))
                link(dve.tensor_copy(parts[:, :, 2], rest2[:]))
                for c in range(NCH):
                    if c in LOADS:
                        dve.wait_ge(idx_in[LOADS.index(c)], 16)
                    if c >= 2:
                        dve.wait_ge(g_mm, c - 1)
                    for t in range(2):
                        dve.tensor_scalar(onehot[:, c % 2, t, :], idx[:, c, :], entry[:, t:t + 1], None,
                                          ALU.is_equal).then_inc(oh_made, 1)
                dve.wait_ge(rstd, 1)
                dve.wait_ge(w_in, 16 * 5)
                for k, w in (("k", kw), ("q", qw), ("v", vw), ("p", None)):
                    link(dve.tensor_tensor(rs[k][:], rs[k][:], bn[k][:, 0, :], ALU.mult))
                    link(dve.tensor_tensor(bn[k][:, 2, :], bn[k][:, 2, :], rs[k][:], ALU.mult))
                    link(dve.tensor_tensor(bn[k][:, 1, :], bn[k][:, 1, :], bn[k][:, 2, :], ALU.subtract))
                    if k == "q":
                        link(dve.tensor_scalar(rs[k][:], rs[k][:], KD ** -0.5, None, ALU.mult))
                        link(dve.tensor_scalar(bn[k][:, 1, :], bn[k][:, 1, :], KD ** -0.5, None, ALU.mult))
                    if w is not None:
                        e = w.shape[0]
                        link(dve.tensor_tensor(w[:, :, 0:D_IN], w[:, :, 0:D_IN],
                                               rs[k][:].unsqueeze(2).to_broadcast([e, H0, D_IN]), ALU.mult))
                        dve.tensor_copy(w[:, :, D_IN:AUG], bn[k][:, 1, :].unsqueeze(2)).then_inc(folded, 1)
                    else:
                        dve.tensor_copy(wide_p[:, 0], rs[k][:].to_broadcast([D, D]))
                        dve.tensor_copy(wide_p[:, 1], bn[k][:, 1].to_broadcast([D, D])).then_inc(folded, 1)
                dve.tensor_copy(mem["before_bf"][:], mem["c"]("before", TOK))
                dve.tensor_copy(mem["sel_bf"][:].rearrange("p e f -> p (e f)"), mem["c"]("sel", 8))
                dve.wait_ge(bt_mm, 1)
                dve.tensor_copy(mem["proj_c"][:], bank[5][0:TOK, D:2 * D])
                dve.wait_ge(bt_high, 1)
                for j in range(3):
                    dve.tensor_tensor(BT[1][:, 4 * j:4 * j + 4, :],
                                      bank[j][0:AUG, 0:4 * AUG].rearrange("p (a b) -> p a b", a=4),
                                      BT[0][:, 4 * j:4 * j + 4, :], ALU.subtract)
                dve.tensor_tensor(WpT[:], WpT[:], bank[5][:, 0:D].unsqueeze(1).to_broadcast([D, 6, D]), ALU.mult)

            @block.tensor
            def _(pe):
                for c in range(NCH):
                    pe.wait_ge(oh_made, 2 * (c + 1))
                    if c >= 2:
                        pe.wait_ge(g_copied, c - 1)
                    for j in range(4):
                        for m in range(2):
                            ins = pe.matmul(bank[(c % 2) * 4 + j][0:3 * H0, 0:BLK],
                                            parts[:, m].rearrange("p s h -> p (s h)"),
                                            onehot[:, c % 2, m, j * BLK:(j + 1) * BLK],
                                            start=(m == 0), stop=(m == 1))
                    ins.then_inc(g_mm, 1)
                pe.wait_ge(folded, 2)
                pe.wait_ge(g_copied, NCH)
                for h in range(H0):
                    pe.matmul(bank[h // 4][0:AUG, (h % 4) * AUG:(h % 4 + 1) * AUG], qw[:, h, :], kw[:, h, :],
                              start=True, stop=True)
                pe.wait_ge(folded, 4)
                for h in range(H0):
                    pe.transpose(bank[3 + h // 6][0:AUG, (h % 6) * VD:(h % 6 + 1) * VD], vw[:, h, :],
                                 ident[0:VD, 0:VD])
                for j in range(2):
                    ins = pe.transpose(bank[5][:, j * D:(j + 1) * D], wide_p[:, j], ident)
                ins.then_inc(bt_mm, 1)


def token_attention(nc, ctx, io, mem):
    QUADS = B // 4
    with ExitStack() as here:
        def sb(name, shape, dt=F32):
            return here.enter_context(nc.sbuf_tensor(name, shape, dt))

        def sem(name):
            return here.enter_context(nc.semaphore(name))

        xtok, xT = mem["xtok"], mem["xT"]
        XQ = [sb(f"XQ_{part}", [AUG, 2, 4, 7, 7], F32R) for part in ("high", "low")]
        XS = [sb(f"XS_{part}", [AUG, 2, 4, N], F32R) for part in ("high", "low")]
        QT = [sb(f"QT_{part}", [AUG, 2, 4, H0 * NQ], F32R) for part in ("high", "low")]
        QF = sb("QF", [AUG, 3, 2, 4, NQ])
        T = sb("T", [TOK, 2, PAIRS, N])
        mx = sb("mx", [TOK, 2, PAIRS])
        EF = sb("EF", [HALF, 2, H0 * NQ])
        E = [sb(f"E_{part}", [HALF, 2, 2, H0 * NQ], F32R) for part in ("high", "low")]
        XT = [sb(f"XT_{part}", [HALF, 2, 4, 2, AUG], F32R) for part in ("high", "low")]
        EX = sb("EX", [AUG, 2, H0, TOK])
        rc = sb("rc", [TOK, 2, H0])
        O = sb("O", [TOK, 2, H0 * VD])
        HS = sb("HS", [TOK, 2, H0 * VD])
        HST = sb("HST", [128, 6, TOK])
        psS = here.enter_context(nc.psum_tensor("psS", [128, 3, BANK], F32))
        psT = here.enter_context(nc.psum_tensor("psT", [128, 2, BANK], F32))
        psX = here.enter_context(nc.psum_tensor("psX", [128, 2, BANK], F32))
        psM = here.enter_context(nc.psum_tensor("psM", [128, BANK], F32))

        xtok_in, xT_in = mem["xtok_in"], mem["xT_in"]
        x_split, tok_split = sem("x_split"), sem("tok_split")
        q_mm, q_copied, q_high, q_made = sem("q_mm"), sem("q_copied"), sem("q_high"), sem("q_made")
        s_mm, s_added = sem("s_mm"), sem("s_added")
        shifted = sem("shifted")
        t_mm, e_made = sem("t_mm"), sem("e_made")
        exped = sem("exped")
        x_mm = [sem("x_mm0"), sem("x_mm1")]
        x_copied = [sem("x_copied0"), sem("x_copied1")]
        v_mm, v_inverse, v_scaled = sem("v_mm"), sem("v_inverse"), sem("v_scaled")
        swished = sem("swished")
        bias_made = sem("bias_made")
        hst_mm, hst_copied = sem("hst_mm"), sem("hst_copied")
        projected = sem("projected")

        ident = mem["c"]("ident")
        first_banks = [psM, psX[:, 0], psX[:, 1], psT[:, 0], psT[:, 1], psS[:, 0]]
        bias, BT, VT, WpT = mem["bias"], mem["BT"], mem["VT"], mem["WpT"]
        h = mem["h"][:].rearrange("p (i k) c -> p i k c", k=4)

        def steps(emit):
            for r in range(8):
                emit(0, r)
            with emit.eng.Fori(1, QUADS // 2 - 1) as i:
                for r in range(8):
                    emit(i, r)
            for r in range(8, 20):
                emit(QUADS // 2 - 2, r)

        class Steps:

            def __init__(self, eng, step):
                self.eng, self.step = eng, step

            def __call__(self, i, r):
                if known(i):
                    i, r = i + r // 8, r % 8
                self.step(i, r)

        def queried(par):
            return xT[:, par, :, 0:HALF].rearrange("p b (y x) -> p b y x", x=14)[:, :, 0:7, 0:7]

        def live(n, last=B):
            return not known(n) or 0 <= n < last

        with nc.Block() as block:
            @block.sync
            def _(sp):
                later = start_loads(sp, first_weights(io, mem), mem["later_in"])
                with sp.Fori(1, QUADS // 2) as i:
                    for par in range(2):
                        q = 2 * i + par
                        sp.wait_ge(x_split, 2 * (q - 1))
                        stand(sp, mem["passed"]["sp"])
                        load_features(sp, io, mem, i, par)
                        sp.wait_ge(tok_split, 2 * (q - 1))
                        stand(sp, mem["passed"]["sp"])
                        load_tokens(sp, io, mem, i, par)
                sp.wait_ge(mem["later_in"], later)

            @block.gpsimd
            def _(pool):
                def low_features(i, par):
                    q = 2 * i + par
                    pool.wait_ge(x_split, 2 * q + 1)
                    pool.tensor_tensor(XQ[1][:, par], queried(par), XQ[0][:, par], ALU.subtract)
                    pool.tensor_tensor(XS[1][:, par], xT[:, par], XS[0][:, par], ALU.subtract).then_inc(x_split, 1)

                def low_tokens(i, par):
                    q = 2 * i + par
                    pool.wait_ge(tok_split, 2 * q + 1)
                    pool.tensor_tensor(XT[1][:, par], xtok[:, par], XT[0][:, par], ALU.subtract).then_inc(tok_split, 1)

                def low_e(n, t, slot):
                    pool.wait_ge(exped, 4 * n + 2 * t + 2)
                    pool.tensor_tensor(E[1][:, slot, t, :], EF[:, t, :], E[0][:, slot, t, :], ALU.subtract
                                       ).then_inc(e_made, 1)

                def low_q(i, par, j):
                    q = 2 * i + par
                    pool.wait_ge(q_high, 6 * q + j + 1)
                    for u in range(2):
                        at = slice((2 * j + u) * NQ, (2 * j + u + 1) * NQ)
                        ins = pool.tensor_tensor(QT[1][:, par, :, at], QF[:, j % 3, u], QT[0][:, par, :, at],
                                                 ALU.subtract)
                    ins.then_inc(q_made, 1)

                def step(i, r):
                    n = 8 * i + r
                    ahead = live(2 * i + r // 4 + 1, QUADS)
                    ni, npar = i + (r // 4 + 1) // 2, (r // 4 + 1) % 2

                    def chunk(j):
                        if ahead:
                            low_q(ni, npar, j)

                    if r % 4 == 0 and ahead:
                        low_features(ni, npar)
                    if r % 4 == 2:
                        chunk(1)
                    if live(n - 1):
                        low_e(n - 1, 0, (r - 1) % 2)
                    if r % 4 == 2:
                        chunk(2)
                    if r % 4 == 3:
                        chunk(5)
                    if live(n - 1):
                        low_e(n - 1, 1, (r - 1) % 2)
                    if r % 4 == 1:
                        chunk(0)
                    if r % 4 == 2:
                        chunk(3)
                    if r % 4 == 2:
                        chunk(4)
                    if r % 4 == 1 and live(2 * i + r // 4, QUADS):
                        low_tokens(i, r // 4)

                low_features(0, 0)
                for j in range(6):
                    low_q(0, 0, j)
                steps(Steps(pool, step))

            @block.tensor
            def _(pe):
                def q_chunk(i, par, j):
                    q = 2 * i + par
                    first = known(q) and q == 0
                    if j == 0:
                        pe.wait_ge(x_split, 2 * q + 2)
                    if not first:
                        pe.wait_ge(q_copied, 6 * q + j)
                    out = first_banks[j] if first else psM
                    src = [x[:, par].rearrange("p b y x -> p (b y x)") for x in XQ]
                    for u in range(2):
                        ins = product(pe, out[0:AUG, u * 4 * NQ:(u + 1) * 4 * NQ], [w[:, 2 * j + u, :] for w in BT], src)
                    ins.then_inc(q_mm, 1)

                def scores(i, r, n):
                    q, par, b = 2 * i + r // 4, r // 4, r % 4
                    pe.wait_ge(q_made, 6 * (q + 1))
                    for j in range(3):
                        if positive(3 * (n - 1) + j + 1):
                            pe.wait_ge(s_added, 3 * (n - 1) + j + 1)
                        for u in range(2):
                            at = (2 * j + u) * TOK
                            ins = product(pe, psS[0:TOK, j, u * N:(u + 1) * N], [q[:, par, b, at:at + TOK] for q in QT],
                                          [x[:, par, b, :] for x in XS])
                        ins.then_inc(s_mm, 1)

                def turn(n, t, slot):
                    pe.wait_ge(shifted, n + 1)
                    if positive(4 * n + 2 * t - 1):
                        pe.wait_ge(exped, 4 * n + 2 * t - 1)
                    for j in range(PAIRS):
                        ins = pe.transpose(psT[0:HALF, j // 3, (j % 3) * TOK:(j % 3 + 1) * TOK],
                                           T[:, slot, j, t * HALF:(t + 1) * HALF], ident[0:TOK, 0:TOK])
                    ins.then_inc(t_mm, 1)

                def weigh(n, c, slot, par, b, i):
                    if c == 0:
                        pe.wait_ge(tok_split, 4 * i + 2 * par + 2)
                    pe.wait_ge(exped, 4 * n + 4)
                    if positive(n):
                        pe.wait_ge(x_copied[c], n)
                    if slot == 0:
                        if positive(n - 1 + c):
                            pe.wait_ge(v_scaled, n - 1 + c)
                    for j, (x, e) in enumerate(((0, 0), (1, 0), (0, 1))):
                        if e == 1:
                            pe.wait_ge(e_made, 2 * n + 2)
                        for t in range(2):
                            ins = pe.matmul(psX[0:AUG, c, 0:6 * NQ], XT[x][:, par, b, t, :],
                                            E[e][:, slot, t, c * 6 * NQ:(c + 1) * 6 * NQ],
                                            start=(t == 0 and j == 0), stop=(t == 1 and j == 2))
                    ins.then_inc(x_mm[c], 1)

                def values(p, slot):
                    for c in range(2):
                        for k in range(2):
                            pe.wait_ge(x_copied[k], 2 * p + 2)
                        for j in range(6):
                            hh = 6 * c + j
                            ins = pe.matmul(psX[0:TOK, c, j * (VD + 1):(j + 1) * (VD + 1)], EX[:, slot, hh, :],
                                            VT[0:AUG, hh, :], start=True, stop=True)
                        ins.then_inc(v_mm, 1)

                def swish_turn(p, c, slot, q_count):
                    if c == 0:
                        pe.wait_ge(swished, 2 * p + 2)
                        if positive(q_count):
                            pe.wait_ge(q_copied, q_count)
                        if positive(p):
                            pe.wait_ge(projected, 2 * p)
                    else:
                        pe.wait_ge(hst_copied, 2 * p + 1)
                    for j in range(3):
                        k = 3 * c + j
                        ins = pe.transpose(psM[:, j * TOK:(j + 1) * TOK], HS[:, slot, k * 128:(k + 1) * 128],
                                           ident[0:TOK, 0:TOK])
                    ins.then_inc(hst_mm, 1)

                def project(p, q_count):
                    pe.wait_ge(hst_copied, 2 * p + 2)
                    if positive(q_count):
                        pe.wait_ge(q_copied, q_count)
                    for k in range(6):
                        ins = pe.matmul(psM[0:TOK, 0:D], HST[:, k, :], WpT[:, k, :], start=(k == 0), stop=(k == 5))
                    ins.then_inc(projected, 1)

                def step(i, r):
                    n = 8 * i + r
                    q = 2 * i + r // 4
                    ahead = live(q + 1, QUADS)
                    ni, npar = i + (r // 4 + 1) // 2, (r // 4 + 1) % 2
                    made = 6 * (q + 1)

                    def chunk(j):
                        if ahead:
                            if j == 1:
                                if positive(4 * i + r // 2 - 2):
                                    pe.wait_ge(projected, 2 * (4 * i + r // 2 - 2))
                            if j in (0, 5):
                                if positive(2 * (4 * i + (r - 5) // 2) + 2):
                                    pe.wait_ge(hst_copied, 2 * (4 * i + (r - 5) // 2) + 2)
                            q_chunk(ni, npar, j)

                    p = 4 * i + (r - 4) // 2 if r % 2 == 0 else 4 * i + (r - 5) // 2
                    pair = live(p, TILES)
                    slot = (p % 2) if known(p) else ((r - 4) // 2) % 2 if r % 2 == 0 else ((r - 5) // 2) % 2
                    if r % 2 == 0 and pair:
                        values(p, slot)
                    if live(n):
                        scores(i, r, n)
                    if r % 4 == 2:
                        chunk(1)
                    if r % 2 == 1 and pair:
                        swish_turn(p, 0, slot, made + 5 if ahead and r % 4 == 3 else 0)
                    if live(n - 1):
                        turn(n - 1, 0, (r - 1) % 2)
                    if r % 4 == 2:
                        chunk(2)
                    if r % 2 == 1 and pair:
                        swish_turn(p, 1, slot, 0)
                    m = n - 2
                    mi, mr = i + (r - 2) // 8, (r - 2) % 8
                    if live(m):
                        weigh(m, 0, mr % 2, mr // 4, mr % 4, mi)
                    if r % 4 > 0:
                        chunk({1: 0, 2: 3, 3: 5}[r % 4])
                    if live(n - 1):
                        turn(n - 1, 1, (r - 1) % 2)
                    if live(m):
                        weigh(m, 1, mr % 2, mr // 4, mr % 4, mi)
                    if r % 4 == 2:
                        chunk(4)
                    if r % 2 == 1 and pair:
                        project(p, (made + (1 if r % 4 == 1 else 6)) if ahead else 0)

                for j in range(6):
                    q_chunk(0, 0, j)
                steps(Steps(pe, step))

            @block.vector
            def _(dve):
                def add_max(n, r):
                    slot = r % 2
                    for j in range(PAIRS):
                        if j % 2 == 0:
                            dve.wait_ge(s_mm, 3 * n + j // 2 + 1)
                            stand(dve, mem["passed"]["dve"])
                        ins = dve.tensor_tensor_reduce(
                            T[:, slot, j, :], psS[0:TOK, j // 2, (j % 2) * N:(j % 2 + 1) * N], bias[:, j, :],
                            1.0, LOWEST, ALU.add, ALU.max, mx[:, slot, j:j + 1])
                        if j % 2:
                            ins.then_inc(s_added, 1)

                def shift(n, r):
                    slot = r % 2
                    dve.wait_ge(s_added, 3 * n + 3)
                    dve.tensor_tensor(T[:, slot], T[:, slot],
                                      mx[:, slot].unsqueeze(2).to_broadcast([TOK, PAIRS, N]),
                                      ALU.subtract).then_inc(shifted, 1)

                def copy_x(n, slot, odd):
                    dve.wait_ge(x_mm[0], n + 1)
                    dve.tensor_copy(EX[:, slot, 0:6, odd * NQ:(odd + 1) * NQ],
                                    psX[0:AUG, 0, 0:6 * NQ].rearrange("p (h q) -> p h q", h=6)
                                    ).then_inc(x_copied[0], 1)

                def scale_values(p, slot):
                    for c in range(2):
                        v = psX[0:TOK, c, 0:6 * (VD + 1)].rearrange("p (h e) -> p h e", h=6)
                        dve.wait_ge(v_mm, 2 * p + c + 1)
                        dve.reciprocal(rc[:, slot, 6 * c:6 * c + 6].unsqueeze(2), v[:, :, VD:VD + 1]
                                       ).then_inc(v_inverse, 1)
                        dve.wait_ge(v_inverse, 2 * p + c + 1)
                        dve.tensor_tensor(O[:, slot, c * 6 * VD:(c + 1) * 6 * VD].rearrange("p (h e) -> p h e", h=6),
                                          v[:, :, 0:VD],
                                          rc[:, slot, 6 * c:6 * c + 6].unsqueeze(2).to_broadcast([TOK, 6, VD]),
                                          ALU.mult).then_inc(v_scaled, 1)

                def swish(p, slot):
                    dve.wait_ge(swished, 2 * p + 1)
                    dve.scalar_tensor_tensor(HS[:, slot], HS[:, slot], 1.0, O[:, slot], ALU.min, ALU.mult
                                             ).then_inc(swished, 1)

                def add_proj(p, i, k):
                    dve.wait_ge(projected, 2 * p + 1)
                    dve.tensor_tensor(h[:, i + k // 4, k % 4, :], psM[0:TOK, 0:D], mem["proj_c"][:], ALU.add
                                      ).then_inc(projected, 1)

                def step(i, r):
                    n = 8 * i + r
                    k = (r - 4) // 2 if r % 2 == 0 else (r - 5) // 2
                    p = 4 * i + k
                    pair = live(p, TILES)
                    slot = k % 2
                    if r % 2 == 0 and pair:
                        scale_values(p, slot)
                    if live(n):
                        add_max(n, r)
                    if live(n - 2):
                        copy_x(n - 2, ((r - 2) // 2) % 2, r % 2)
                    if live(n):
                        shift(n, r)
                    if r % 2 == 0 and pair:
                        swish(p, slot)
                    if r % 2 == 1 and pair:
                        add_proj(p, i, k)

                dve.wait_ge(mem["bias_in"], 32)
                part = lambda n: mem["bias3"][:, n * PAIRS:(n + 1) * PAIRS, :]
                dve.tensor_tensor(bias[:], part(0), part(1), ALU.add).then_inc(bias_made, 1)
                dve.wait_ge(bias_made, 1)
                dve.tensor_tensor(bias[:], bias[:], part(2), ALU.add).then_inc(bias_made, 1)
                dve.wait_ge(bias_made, 2)
                steps(Steps(dve, step))

            @block.scalar
            def _(act):
                def copy_q(i, par, j):
                    q = 2 * i + par
                    n = 6 * q + j
                    src = first_banks[j] if known(q) and q == 0 else psM
                    act.wait_ge(q_mm, n + 1)
                    if positive(n - 2):
                        act.wait_ge(q_made, n - 2)
                    act.activation(QF[:, j % 3], src[0:AUG, 0:8 * NQ].rearrange("p (u b q) -> p u b q", u=2, b=4),
                                   ACT.Copy).then_inc(q_copied, 1)

                def round_q(i, par, j):
                    act.wait_ge(q_copied, 6 * (2 * i + par) + j + 1)
                    act.activation(QT[0][:, par, :, 2 * j * NQ:(2 * j + 2) * NQ].rearrange("p b (u q) -> p u b q", u=2),
                                   QF[:, j % 3], ACT.Copy).then_inc(q_high, 1)

                def high_features(i, par):
                    q = 2 * i + par
                    act.wait_ge(xT_in[par], 16 * (i + 1))
                    if positive(12 * (q - 1)):
                        act.wait_ge(s_mm, 12 * (q - 1))
                    act.activation(XQ[0][:, par], queried(par), ACT.Copy)
                    act.activation(XS[0][:, par], xT[:, par], ACT.Copy).then_inc(x_split, 1)

                def high_tokens(i, par):
                    q = 2 * i + par
                    act.wait_ge(xtok_in[par], 64 * (i + 1))
                    if positive(4 * (q - 1)):
                        act.wait_ge(x_mm[1], 4 * (q - 1))
                    act.activation(XT[0][:, par], xtok[:, par], ACT.Copy).then_inc(tok_split, 1)

                def exp(n, t, slot):
                    if positive(2 * n + t - 1):
                        act.wait_ge(e_made, 2 * n + t - 1)
                    act.wait_ge(t_mm, 2 * n + t + 1)
                    act.activation(EF[:, t, :].rearrange("p (c x) -> p c x", c=2), psT[0:HALF, :, 0:6 * NQ],
                                   ACT.Exp).then_inc(exped, 1)

                def round_e(n, t, slot):
                    act.wait_ge(exped, 4 * n + 2 * t + 1)
                    act.activation(E[0][:, slot, t, :], EF[:, t, :], ACT.Copy).then_inc(exped, 1)

                def copy_x(n, slot, odd):
                    act.wait_ge(x_mm[1], n + 1)
                    act.activation(EX[:, slot, 6:12, odd * NQ:(odd + 1) * NQ],
                                   psX[0:AUG, 1, 0:6 * NQ].rearrange("p (h q) -> p h q", h=6), ACT.Copy
                                   ).then_inc(x_copied[1], 1)

                def relu(p, slot):
                    act.wait_ge(v_scaled, 2 * p + 2)
                    act.activation(HS[:, slot], O[:, slot], ACT.Relu, bias=mem["half"][:, 0:1], scale=1.0 / 6.0
                                   ).then_inc(swished, 1)

                def copy_hst(p, c):
                    act.wait_ge(hst_mm, 2 * p + c + 1)
                    act.activation(HST[:, 3 * c:3 * c + 3, :],
                                   psM[:, 0:3 * TOK].rearrange("p (k q) -> p k q", k=3), ACT.Copy
                                   ).then_inc(hst_copied, 1)

                def step(i, r):
                    n = 8 * i + r
                    q = 2 * i + r // 4
                    ahead = live(q + 1, QUADS)
                    ni, npar = i + (r // 4 + 1) // 2, (r // 4 + 1) % 2

                    def chunk(j, stage):
                        if ahead:
                            stage(ni, npar, j)

                    k = (r - 4) // 2 if r % 2 == 0 else (r - 5) // 2
                    p = 4 * i + k
                    pair = live(p, TILES)
                    slot = k % 2
                    if r % 4 == 0 and ahead:
                        high_features(ni, npar)
                    if r % 4 == 2:
                        chunk(1, copy_q)
                    if r % 2 == 1 and pair:
                        copy_hst(p, 0)
                    if live(n - 1):
                        exp(n - 1, 0, (r - 1) % 2)
                    if r % 4 == 2:
                        chunk(1, round_q)
                        chunk(2, copy_q)
                    if r % 2 == 1 and pair:
                        copy_hst(p, 1)
                    if r % 4 == 3:
                        chunk(4, round_q)
                    if live(n - 1):
                        round_e(n - 1, 0, (r - 1) % 2)
                    if r % 2 == 0 and pair:
                        relu(p, slot)
                    middle = {1: 0, 2: 3, 3: 5}
                    if r % 4 > 0:
                        chunk(middle[r % 4], copy_q)
                    if r % 4 == 2:
                        chunk(2, round_q)
                    if live(n - 1):
                        exp(n - 1, 1, (r - 1) % 2)
                    if r % 4 == 2:
                        chunk(4, copy_q)
                    if r % 4 == 3:
                        chunk(5, round_q)
                    if r % 2 == 1 and live(n - 2):
                        copy_x(n - 2, ((r - 2) // 2) % 2, r % 2)
                    if live(n - 1):
                        round_e(n - 1, 1, (r - 1) % 2)
                    if r % 2 == 0 and live(n - 2):
                        copy_x(n - 2, ((r - 2) // 2) % 2, r % 2)
                    if r % 4 in (1, 2):
                        chunk(middle[r % 4], round_q)
                    if r % 4 == 1 and live(2 * i + r // 4, QUADS):
                        high_tokens(i, r // 4)

                high_features(0, 0)
                for j in range(6):
                    copy_q(0, 0, j)
                    round_q(0, 0, j)
                steps(Steps(act, step))


class Norm:

    def __init__(self, nc, here, name, mem):
        self.mem, self.name = mem, name
        self.stats = here.enter_context(nc.sbuf_tensor(name + "_stats", [TOK, 2, 4, 6], F32))
        self.mv = here.enter_context(nc.sbuf_tensor(name + "_mv", [TOK, 2, 4, 2], F32))
        self.var = here.enter_context(nc.sbuf_tensor(name + "_var", [TOK, 2, 4], F32))
        self.rstd = here.enter_context(nc.sbuf_tensor(name + "_rstd", [TOK, 2, 4], F32))
        self.moments = here.enter_context(nc.semaphore(name + "_moments"))
        self.roots = here.enter_context(nc.semaphore(name + "_roots"))

    def take(self, dve, x, g, slot):
        for k in range(4):
            ins = dve.bn_stats(self.stats[:, slot, k, :], x[:, k, :])
        ins.then_inc(self.moments, 1)
        dve.wait_ge(self.moments, 2 * g + 1)
        stand(dve, self.mem["passed"]["dve"])
        for k in range(4):
            ins = dve.bn_aggr(self.mv[:, slot, k, :], self.stats[:, slot, k, :])
        ins.then_inc(self.moments, 1)

    def root(self, pool, g, slot):
        pool.wait_ge(self.moments, 2 * g + 2)
        pool.tensor_tensor(self.var[:, slot, :].unsqueeze(2), self.mv[:, slot, :, 1:2],
                           self.mem["eps"][0:TOK, 0:4].unsqueeze(2), ALU.add).then_inc(self.roots, 1)
        pool.wait_ge(self.roots, 2 * g + 1)
        pool.tensor_tensor(self.rstd[:, slot, :], self.var[:, slot, :], self.mem["half_neg"][0:TOK, 0:4],
                           ALU.pow).then_inc(self.roots, 1)

    def scale(self, eng, out, x, g, slot, done, last_only=False, passed="dve"):
        eng.wait_ge(self.roots, 2 * g + 2)
        stand(eng, self.mem["passed"][passed])
        for k in range(4):
            ins = eng.tensor_scalar(out[:, k, :], x[:, k, :], self.mv[:, slot, k, 0:1],
                                    self.rstd[:, slot, k:k + 1], ALU.subtract, ALU.mult)
            if not last_only or k == 3:
                ins.then_inc(done, 1)


def group_view(t, per):
    return t[:].rearrange("p (i r k) c -> p i r k c", r=per, k=4)


def at(view, i, r, per):
    return view[:, i + r // per, r % per]


def skewed(eng, step, groups, lag, per=2, peel=0):
    first = -(-(lag + peel) // per)
    whole = groups // per
    for n in range(first * per):
        step(n // per, n % per)
    with eng.Fori(first, whole) as i:
        for r in range(per):
            step(i, r)
    for n in range(whole * per, groups + lag):
        step(n // per, n % per)


GROUPS = TILES // 4
H1, D1 = 8, 64


def head_attention(nc, ctx, io, mem):
    with ExitStack() as here:
        def sb(name, shape, dt=F32):
            return here.enter_context(nc.sbuf_tensor(name, shape, dt))

        def sem(name):
            return here.enter_context(nc.semaphore(name))

        def bank(name):
            return here.enter_context(nc.psum_tensor(name, [128, BANK], F32))

        W = mem["w1"]
        ln = Norm(nc, here, "ln_a", mem)
        xn = sb("xn", [TOK, 2, 4, D])
        XT = sb("XT", [D, 2, 4, 2 * TOK])
        KS = sb("KS", [TOK, 2, 512])
        VS = sb("VS", [TOK, 2, 4, 2, 512])
        PR = sb("PR", [TOK, 2, 512])
        dots = sb("dots", [TOK, 2, 4, H1])
        top = sb("top", [TOK, 2, 4, H1])
        arg = sb("arg", [TOK, 2, 2, 4, H1])
        wts = sb("wts", [TOK, 2, 2, 4, H1])
        den = sb("den", [TOK, 2, 4, H1])
        coef = sb("coef", [TOK, 2, 2, 4, H1])
        ZA, ZB, Z = sb("ZA", [TOK, 2, 512]), sb("ZB", [TOK, 2, 512]), sb("Z", [TOK, 2, 512])
        ZT = sb("ZT", [128, 2, 4 * TOK])
        ps = [bank(n) for n in ("psQ", "psK", "psV", "psL")]
        psZ, psO = bank("psZ"), bank("psO")
        psX = [bank("psX0"), bank("psX1")]

        normed = sem("normed")
        x_mm, x_copied = sem("a_x_mm"), sem("a_x_copied")
        qkvl_mm, kvl_copied = sem("qkvl_mm"), sem("kvl_copied")
        multiplied, dotted = sem("multiplied"), sem("dotted")
        soft = sem("soft")
        arg_made, wts_made, coef_made = sem("arg_made"), sem("wts_made"), sem("coef_made")
        z_parts, z_made = sem("z_parts"), sem("z_made")
        z_mm, z_copied, o_mm, o_added = sem("z_mm"), sem("z_copied"), sem("o_mm"), sem("o_added")
        h = group_view(mem["h"], 2)
        ident, after = mem["c"]("ident"), mem["c"]("after", TOK)
        live = lambda g: not known(g) or 0 <= g < GROUPS

        def behind(s, r, k, tiles):
            return (s - 3, r - 3, k + 4 - tiles) if k + 4 >= tiles else (s - 4, r - 4, k + 8 - tiles)

        with nc.Block() as block:
            @block.sync
            def _(sp):
                before = 16 * len(first_weights(io, mem))
                sp.wait_ge(mem["later_in"], before + start_loads(sp, last_weights(io, mem), mem["later_in"]))

            @block.gpsimd
            def _(pool):
                def step(i, r):
                    s = 2 * i + r
                    for k in range(4):
                        g, gr, kz = behind(s, r, k, 5)
                        if live(g):
                            t = 4 * g + kz
                            if positive(t - 1):
                                pool.wait_ge(z_mm, t - 1)
                            pool.wait_ge(z_parts, t + 1)
                            pool.tensor_tensor(Z[:, kz % 2], ZA[:, kz % 2], ZB[:, kz % 2], ALU.add
                                               ).then_inc(z_made, 1)
                        if k == 1 and live(s):
                            ln.root(pool, s, r % 2)

                skewed(pool, step, GROUPS, 4)

            @block.vector
            def _(dve):
                def z_tile(g, slot, k):
                    t = 4 * g + k
                    if k == 0:
                        dve.wait_ge(coef_made, g + 1)
                    if positive(t - 1):
                        dve.wait_ge(z_made, t - 1)
                    for j, out in ((0, ZA), (1, ZB)):
                        ins = dve.tensor_tensor(out[:, k % 2].rearrange("p (h d) -> p h d", h=H1),
                                                VS[:, slot, k, j].rearrange("p (h d) -> p h d", h=H1),
                                                coef[:, slot, j, k].unsqueeze(2).to_broadcast([TOK, H1, D1]),
                                                ALU.mult)
                    ins.then_inc(z_parts, 1)

                def dot(g, slot, k):
                    t = 4 * g + k
                    dve.wait_ge(qkvl_mm, 4 * t + 1)
                    dve.wait_ge(kvl_copied, 3 * t + 1)
                    dve.tensor_tensor(PR[:, k % 2], ps[0][0:TOK, :], KS[:, k % 2], ALU.mult).then_inc(multiplied, 1)
                    dve.wait_ge(multiplied, t + 1)
                    dve.tensor_reduce(dots[:, slot, k, :].unsqueeze(2),
                                      PR[:, k % 2].rearrange("p (h d) -> p h d", h=H1), AX.X, ALU.add
                                      ).then_inc(dotted, 1)

                def softmax_args(g, slot):
                    d = dots[:, slot]
                    dve.wait_ge(dotted, 4 * g + 4)
                    dve.tensor_scalar(top[:, slot], d, D1 ** -0.5, mem["c"]("floor", TOK), ALU.mult, ALU.max
                                      ).then_inc(soft, 1)
                    dve.wait_ge(soft, 3 * g + 1)
                    dve.scalar_tensor_tensor(arg[:, slot, 0], d, D1 ** -0.5, top[:, slot], ALU.mult, ALU.subtract)
                    dve.tensor_scalar(arg[:, slot, 1], top[:, slot], -1.0, 0.0, ALU.mult, ALU.min
                                      ).then_inc(arg_made, 1)

                def softmax_ends(g, slot):
                    dve.wait_ge(wts_made, g + 1)
                    dve.scalar_tensor_tensor(den[:, slot], wts[:, slot, 1], mem["c"]("later", TOK), wts[:, slot, 0],
                                             ALU.mult, ALU.add).then_inc(soft, 1)
                    dve.wait_ge(soft, 3 * g + 2)
                    dve.reciprocal(den[:, slot], den[:, slot]).then_inc(soft, 1)
                    dve.wait_ge(soft, 3 * g + 3)
                    dve.tensor_tensor(coef[:, slot].rearrange("p j k h -> p j (k h)"),
                                      wts[:, slot].rearrange("p j k h -> p j (k h)"),
                                      den[:, slot].rearrange("p k h -> p (k h)").unsqueeze(1)
                                      .to_broadcast([TOK, 2, 4 * H1]), ALU.mult).then_inc(coef_made, 1)

                def step(i, r):
                    s = 2 * i + r
                    for k in range(4):
                        if live(s - 2):
                            dot(s - 2, r % 2, k)
                        if k == 0 and live(s - 3):
                            softmax_ends(s - 3, (r - 3) % 2)
                        g, gr, kz = behind(s, r, k, 5)
                        if live(g):
                            z_tile(g, gr % 2, kz)
                        if k == 1 and live(s):
                            ln.take(dve, at(h, i, r, 2), s, r % 2)
                        if k == 3 and live(s - 2):
                            softmax_args(s - 2, r % 2)
                        if k == 3 and live(s):
                            if positive(4 * (s - 1)):
                                dve.wait_ge(x_mm, 4 * (s - 1))
                            ln.scale(dve, xn[:, r % 2], at(h, i, r, 2), s, r % 2, normed)
                        g, gr, kz = behind(s, r, k, 6)
                        if live(g):
                            dve.wait_ge(o_mm, 4 * g + kz + 1)
                            x = at(h, i, gr, 2)[:, kz, :]
                            dve.tensor_tensor(x, psO[0:TOK, 0:D], x, ALU.add).then_inc(o_added, 1)

                skewed(dve, step, GROUPS, 4)

            @block.scalar
            def _(act):
                def step(i, r):
                    s = 2 * i + r
                    for k in range(4):
                        t = 4 * (s - 2) + k
                        if live(s - 2):
                            if positive(t - 1):
                                act.wait_ge(multiplied, t - 1)
                            act.wait_ge(qkvl_mm, 4 * t + 2)
                            act.activation(KS[:, k % 2], ps[1][0:TOK, :], ACT.Copy).then_inc(kvl_copied, 1)
                        if k == 0 and live(s - 3):
                            act.wait_ge(arg_made, s - 2)
                            act.activation(wts[:, (r - 3) % 2], arg[:, (r - 3) % 2], ACT.Exp).then_inc(wts_made, 1)
                        g, gr, kz = behind(s, r, k, 6)
                        if live(g):
                            act.wait_ge(z_mm, 4 * g + kz + 1)
                            act.activation(ZT[:, kz % 2], psZ[:, 0:4 * TOK], ACT.Copy).then_inc(z_copied, 1)
                        if live(s - 2):
                            for j in range(2):
                                act.wait_ge(qkvl_mm, 4 * t + 3 + j)
                                act.activation(VS[:, r % 2, k, j], ps[2 + j][0:TOK, :], ACT.Copy
                                               ).then_inc(kvl_copied, 1)
                        if live(s - 1):
                            act.wait_ge(x_mm, 4 * (s - 1) + k + 1)
                            act.activation(XT[:, (r - 1) % 2, k, :], psX[k % 2][:, 0:2 * TOK], ACT.Copy
                                           ).then_inc(x_copied, 1)

                skewed(act, step, GROUPS, 4)

            @block.tensor
            def _(pe):
                def project(g, slot, k, j):
                    t = 4 * g + k
                    if j == 0:
                        pe.wait_ge(x_copied, t + 1)
                        if positive(t):
                            pe.wait_ge(multiplied, t)
                    else:
                        if positive(3 * (t - 1) + j):
                            pe.wait_ge(kvl_copied, 3 * (t - 1) + j)
                    src = XT[:, slot, k, TOK:2 * TOK] if j == 3 else XT[:, slot, k, 0:TOK]
                    pe.matmul(ps[j][0:TOK, :], src, W["qkv"][:, min(j, 2), :], start=True, stop=True
                              ).then_inc(qkvl_mm, 1)

                def step(i, r):
                    s = 2 * i + r
                    for k in range(4):
                        gz, gr, kz = behind(s, r, k, 6)
                        g = 4 * gz + kz
                        if live(s - 2):
                            project(s - 2, r % 2, k, 0)
                            project(s - 2, r % 2, k, 1)
                        if live(gz):
                            if positive(g):
                                pe.wait_ge(z_copied, g)
                            pe.wait_ge(z_made, g + 1)
                            for j in range(4):
                                ins = pe.transpose(psZ[:, j * TOK:(j + 1) * TOK], Z[:, kz % 2, j * 128:(j + 1) * 128],
                                                   ident[0:TOK, 0:TOK])
                            ins.then_inc(z_mm, 1)
                        if live(s - 2):
                            project(s - 2, r % 2, k, 2)
                            project(s - 2, r % 2, k, 3)
                        if live(gz):
                            if positive(g):
                                pe.wait_ge(o_added, g)
                            pe.wait_ge(z_copied, g + 1)
                            for j in range(4):
                                ins = pe.matmul(psO[0:TOK, 0:D], ZT[:, kz % 2, j * TOK:(j + 1) * TOK],
                                                W["o"][:, j, :], start=(j == 0), stop=(j == 3))
                            ins.then_inc(o_mm, 1)
                        if live(s - 1):
                            t = 4 * (s - 1) + k
                            if positive(t - 1):
                                pe.wait_ge(x_copied, t - 1)
                            pe.wait_ge(normed, t + 1)
                            pe.transpose(psX[k % 2][:, 0:TOK], xn[:, (r - 1) % 2, k, :], ident[0:TOK, 0:TOK])
                            pe.matmul(psX[k % 2][:, TOK:2 * TOK], xn[:, (r - 1) % 2, k, :], after,
                                      start=True, stop=True).then_inc(x_mm, 1)

                skewed(pe, step, GROUPS, 4)


LAYERS, HEADS, HD = 3, 4, 32
FB = 4
EARLY = 6
SUMMED, AHEAD = 7, 2
NE = 8
BIG = 1.0e30


def top1_experts(nc, ctx, io, mem):
    with ExitStack() as here:
        def sb(name, shape, dt=F32):
            return here.enter_context(nc.sbuf_tensor(name, shape, dt))

        def sem(name):
            return here.enter_context(nc.semaphore(name))

        def bank(name):
            return here.enter_context(nc.psum_tensor(name, [128, BANK], F32))

        W = mem["w2"]
        ln = Norm(nc, here, "ln_b", mem)
        xn = sb("b_xn", [TOK, 2, 4, D])
        XT = sb("b_XT", [D, 2, 4 * TOK])
        LG, SH, EX = sb("LG", [TOK, 2, 4, NE]), sb("SH", [TOK, 2, 4, NE]), sb("b_EX", [TOK, 2, 4, NE])
        cand, OH = sb("cand", [TOK, 2, 4, NE]), sb("OH", [TOK, 2, 4, NE])
        most, best = sb("most", [TOK, 2, 4]), sb("best", [TOK, 2, 4])
        total, gate = sb("total", [TOK, 2, 4]), sb("gate", [TOK, 2, 4])
        OHT = sb("OHT", [NE, 2, 4 * TOK])
        pen = sb("pen", [NE, 2, 4 * TOK], BF16)
        HID = sb("b_HID", [128, 2, NE, 4 * TOK])
        psX, psR = bank("b_psX"), bank("b_psR")
        psL = psH = psR
        psY = [bank("b_psY0"), bank("b_psY1")]
        psE = [bank(f"b_psE{i}") for i in range(4)]

        normed, x_mm, x_copied = sem("b_normed"), sem("b_x_mm"), sem("b_x_copied")
        l_mm = sem("l_mm")
        ROUTE = 7
        route = sem("route")
        sh_made, ex_made, gated, oh_made = sem("sh_made"), sem("b_ex_made"), sem("gated"), sem("b_oh_made")
        oh_mm, pen_made = sem("oh_mm"), sem("pen_made")
        e_mm, e_relu = sem("e_mm"), sem("e_relu")
        y_mm, y_added = sem("y_mm"), sem("y_added")
        h = group_view(mem["h"], 2)
        ident = mem["c"]("ident")
        X = group_view(mem["X"], 2)
        ln0, x0_made, centred = mem["ln0"], mem["x0_made"], sem("centred")
        mean_wv = sb("mean_wv", [D, LAYERS, HEADS])
        live = lambda g: not known(g) or 0 <= g < GROUPS
        early = lambda g: not known(g) or 0 <= g < EARLY

        with nc.Block() as block:
            @block.gpsimd
            def _(pool):
                def step(i, r):
                    s = 2 * i + r
                    if live(s):
                        ln.root(pool, s, r % 2)
                    if early(s - 4):
                        ln0.root(pool, s - 4, r % 2)
                    if known(s) and s == 3:
                        pool.wait_ge(centred, 3)
                        for work, layers in mem["work"]:
                            pool.tensor_copy(work[:], layers[:, 0, :])

                skewed(pool, step, GROUPS, 3)

            @block.vector
            def _(dve):
                def own(ins, g, j):
                    ins.then_inc(route, 1)
                    dve.wait_ge(route, ROUTE * g + j)

                def router(g, slot):
                    dve.wait_ge(l_mm, g + 1)
                    own(dve.tensor_tensor(LG[:, slot], psL[0:TOK, 0:4 * NE].rearrange("p (k e) -> p k e", k=4),
                                          W["br"][:].unsqueeze(1).to_broadcast([TOK, 4, NE]), ALU.add), g, 1)
                    own(dve.tensor_reduce(most[:, slot].unsqueeze(2), LG[:, slot], AX.X, ALU.max), g, 2)
                    dve.tensor_tensor(SH[:, slot], LG[:, slot], most[:, slot].unsqueeze(2).to_broadcast([TOK, 4, NE]),
                                      ALU.subtract).then_inc(sh_made, 1)
                    dve.wait_ge(sh_made, g + 1)
                    own(dve.scalar_tensor_tensor(cand[:, slot], SH[:, slot], 0.0,
                                                 mem["c"]("rank8", TOK).unsqueeze(1).to_broadcast([TOK, 4, NE]),
                                                 ALU.is_ge, ALU.mult), g, 3)
                    own(dve.tensor_reduce(best[:, slot].unsqueeze(2), cand[:, slot], AX.X, ALU.max), g, 4)
                    dve.tensor_tensor(OH[:, slot], cand[:, slot], best[:, slot].unsqueeze(2).to_broadcast([TOK, 4, NE]),
                                      ALU.is_equal).then_inc(oh_made, 1)
                    dve.wait_ge(ex_made, g + 1)
                    own(dve.tensor_reduce(total[:, slot].unsqueeze(2), EX[:, slot], AX.X, ALU.add), g, 5)
                    dve.reciprocal(gate[:, slot], total[:, slot]).then_inc(gated, 1)

                def turned(g, slot):
                    dve.wait_ge(oh_mm, g + 1)
                    own(dve.tensor_copy(OHT[:, slot], psH[0:NE, 0:4 * TOK]), g, 6)
                    own(dve.tensor_scalar(pen[:, slot], psH[0:NE, 0:4 * TOK], 1.0, BIG, ALU.subtract, ALU.mult), g, 7)
                    dve.sem_inc(pen_made, 1)

                def centre():
                    wv = mem["ret_a"][:, :, 4 * D:5 * D].rearrange("p l (h e) -> p l h e", h=HEADS)
                    dve.tensor_reduce(mean_wv[:].unsqueeze(3), wv, AX.X, ALU.add).then_inc(centred, 1)
                    dve.wait_ge(centred, 1)
                    dve.tensor_scalar(mean_wv[:], mean_wv[:], 1.0 / HD, None, ALU.mult).then_inc(centred, 1)
                    dve.wait_ge(centred, 2)
                    for l in range(LAYERS):
                        ins = dve.tensor_tensor(wv[:, l], wv[:, l], mean_wv[:, l].unsqueeze(2).to_broadcast([D, HEADS, HD]),
                                                ALU.subtract)
                    ins.then_inc(centred, 1)

                def step(i, r):
                    s = 2 * i + r
                    if live(s - 2):
                        turned(s - 2, r % 2)
                    if live(s):
                        ln.take(dve, at(h, i, r, 2), s, r % 2)
                    for k in range(4):
                        if live(s - 3):
                            if k == 0:
                                dve.wait_ge(gated, s - 2)
                                stand(dve, mem["passed"]["dve"])
                            dve.wait_ge(y_mm, 4 * (s - 3) + k + 1)
                            x = at(h, i, r - 3, 2)[:, k, :]
                            dve.scalar_tensor_tensor(x, psY[k % 2][0:TOK, 0:D], gate[:, (r - 3) % 2, k:k + 1],
                                                     x, ALU.mult, ALU.add).then_inc(y_added, 1)
                        if k == 0 and live(s):
                            if positive(s - 1):
                                dve.wait_ge(x_mm, s - 1)
                            ln.scale(dve, xn[:, r % 2], at(h, i, r, 2), s, r % 2, normed, last_only=True)
                        if k == 1 and early(s - 4):
                            ln0.take(dve, at(h, i, r - 4, 2), s - 4, r % 2)
                        if k == 2 and early(s - 4):
                            ln0.scale(dve, at(X, i, r - 4, 2), at(h, i, r - 4, 2), s - 4, r % 2, x0_made,
                                      last_only=True)
                    if known(s) and s == 3:
                        centre()
                    if live(s - 1):
                        router(s - 1, (r - 1) % 2)

                skewed(dve, step, GROUPS, 3)

            @block.scalar
            def _(act):
                def step(i, r):
                    s = 2 * i + r
                    if live(s - 1):
                        act.wait_ge(x_mm, s)
                        act.activation(XT[:, (r - 1) % 2], psX[:, 0:4 * TOK], ACT.Copy).then_inc(x_copied, 1)
                    for e in range(NE):
                        if live(s - 2):
                            act.wait_ge(e_mm, NE * (s - 2) + e + 1)
                            act.activation(HID[:, r % 2, e], psE[e % 4][:, 0:4 * TOK], ACT.Relu,
                                           bias=W["b1"][:, e:e + 1]).then_inc(e_relu, 1)
                        if e == 5 and live(s - 1):
                            act.wait_ge(sh_made, s)
                            act.activation(EX[:, (r - 1) % 2], SH[:, (r - 1) % 2], ACT.Exp).then_inc(ex_made, 1)

                skewed(act, step, GROUPS, 3)

            @block.tensor
            def _(pe):
                def second(g, slot, k):
                    if k == 0:
                        pe.wait_ge(e_relu, NE * (g + 1))
                    if positive(4 * g + k - 1):
                        pe.wait_ge(y_added, 4 * g + k - 1)
                    for e in range(NE):
                        pe.matmul(psY[k % 2][0:TOK, 0:D], HID[:, slot, e, k * TOK:(k + 1) * TOK],
                                  W["w2"][:, e, :], start=(e == 0), stop=False)
                    pe.matmul(psY[k % 2][0:TOK, 0:D], OHT[:, slot, k * TOK:(k + 1) * TOK], W["b2"][:],
                              start=False, stop=True).then_inc(y_mm, 1)

                def first(g, slot, e):
                    n = NE * g + e
                    if e == 0:
                        pe.wait_ge(pen_made, g + 1)
                    if positive(n - 3):
                        pe.wait_ge(e_relu, n - 3)
                    pe.matmul(psE[e % 4][:, 0:4 * TOK], W["w1"][:, e, :], XT[:, slot], start=True, stop=False)
                    pe.matmul(psE[e % 4][:, 0:4 * TOK], mem["sel_bf"][:, e, :], pen[:, slot], start=False, stop=True
                              ).then_inc(e_mm, 1)

                def step(i, r):
                    s = 2 * i + r
                    if live(s - 1):
                        if positive(s - 1):
                            pe.wait_ge(x_copied, s - 1)
                        pe.wait_ge(normed, s)
                        for k in range(4):
                            ins = pe.transpose(psX[:, k * TOK:(k + 1) * TOK], xn[:, (r - 1) % 2, k, :],
                                               ident[0:TOK, 0:TOK])
                        ins.then_inc(x_mm, 1)
                    if live(s - 2):
                        pe.wait_ge(oh_made, s - 1)
                        pe.wait_ge(sh_made, s - 1)
                        for k in range(4):
                            ins = pe.transpose(psH[0:NE, k * TOK:(k + 1) * TOK], OH[:, r % 2, k, :],
                                               ident[0:TOK, 0:TOK])
                        ins.then_inc(oh_mm, 1)
                    for k in range(4):
                        if live(s - 3):
                            second(s - 3, (r - 3) % 2, k)
                        if live(s - 2):
                            first(s - 2, r % 2, 2 * k)
                            first(s - 2, r % 2, 2 * k + 1)
                        if k == 1 and live(s - 1):
                            pe.wait_ge(x_copied, s)
                            if positive(s - 1):
                                pe.wait_ge(pen_made, s - 1)
                            for t in range(4):
                                ins = pe.matmul(psL[0:TOK, t * NE:(t + 1) * NE],
                                                XT[:, (r - 1) % 2, t * TOK:(t + 1) * TOK], W["wr"][:],
                                                start=True, stop=True)
                            ins.then_inc(l_mm, 1)

                skewed(pe, step, GROUPS, 3)


def retention(nc, ctx, io, mem):
    ITEMS = LAYERS * GROUPS
    COLS = 4 * TOK
    with ExitStack() as here:
        def sb(name, shape, dt=F32):
            return here.enter_context(nc.sbuf_tensor(name, shape, dt))

        def sem(name):
            return here.enter_context(nc.semaphore(name))

        def bank(name):
            return here.enter_context(nc.psum_tensor(name, [128, BANK], F32))

        (wa, WA), (wc, WC), (wd, WD), (wb, WB) = mem["work"]
        wq, ln1_w, ln1_b = wa[:, 0:6 * D], wa[:, 6 * D:6 * D + 1], wa[:, 6 * D + 1:6 * D + 2]
        gn_w, gn_b, ln2_w, ln2_b, b1 = (wc[:, 0:1], wc[:, 1:2], wc[:, 2:3], wc[:, 3:4], wc[:, 4:8])
        wo, w1 = wc[:, 8:8 + D], wc[:, 8 + D:8 + 5 * D]

        X = mem["X"]
        ln0, x0_made = mem["ln0"], mem["x0_made"]
        ln1, ln2 = Norm(nc, here, "ln_1", mem), Norm(nc, here, "ln_2", mem)
        xn1, xn2 = sb("xn1", [TOK, 2, 4, D]), sb("xn2", [TOK, 2, 4, D])
        XT1, XT3 = sb("XT1", [D, 2, COLS]), sb("XT3", [D, 2, COLS])
        RA, RB = sb("RA", [D, 2, COLS]), sb("RB", [D, 2, COLS])
        QK = sb("QK", [D, 2, 2, COLS])
        TH, SG = sb("TH", [D, 2, COLS]), sb("SG", [D, 2, COLS])
        V = sb("V", [TOK, 2, 4, D])
        AM = sb("AM", [TOK, 2, HEADS, 4, TOK])
        SQ, Yn = sb("SQ", [TOK, 2, 4 * D]), sb("Yn", [TOK, 2, 4, D])
        var, vare, grs = (sb(n, [TOK, 2, 4 * HEADS]) for n in ("gn_var", "gn_vare", "gn_rstd"))
        YA, U = sb("YA", [D, 2, COLS]), sb("U", [D, 2, COLS])
        HID = sb("HID", [128, 2, FB, COLS])
        wide = [bank(f"wide{j}") for j in range(4)]
        psT, psG, psV, psF = bank("r_psT"), bank("r_psG"), bank("r_psV"), bank("r_psF")

        xn1_made, xn2_made = sem("xn1_made"), sem("xn2_made")
        t1_mm, t1_copied = sem("t1_mm"), sem("t1_copied")
        t2_mm, t2_copied = sem("t2_mm"), sem("t2_copied")
        t3_mm, t3_copied = sem("t3_mm"), sem("t3_copied")
        q_mm, rot_mul, rotated = sem("r_q_mm"), sem("rot_mul"), sem("rotated")
        v_mm, v_copied, g_mm, tanhed, sg_made = (sem("r_v_mm"), sem("r_v_copied"), sem("r_g_mm"), sem("tanhed"),
                                                 sem("sg_made"))
        a_mm, masked = sem("a_mm"), sem("masked")
        y_mm, squared, var_made, vare_made, grs_made, yn_made = (
            sem("r_y_mm"), sem("squared"), sem("gvar_made"), sem("gvare_made"), sem("grs_made"), sem("yn_made"))
        gated, wo_mm, wo_added = sem("r_gated"), sem("wo_mm"), sem("wo_added")
        f1_mm, gelued = sem("f1_mm"), sem("gelued")
        f2_mm, f2_added, b2_added = sem("f2_mm"), sem("f2_added"), sem("b2_added")
        took_a, took_c, took_d = sem("took_a"), sem("took_c"), sem("took_d")
        ident, decay = mem["c"]("ident"), mem["c"]("decay", TOK).rearrange("p (h q) -> p h q", h=HEADS)
        h = group_view(mem["h"], GROUPS)
        live = lambda n: not known(n) or 0 <= n < ITEMS
        group = lambda t, r: t[:].rearrange("p (g k) c -> p g k c", k=4)[:, r % GROUPS]
        per_pos = lambda a: a.rearrange("p (b q) -> p b q", q=NQ)

        with nc.Block() as block:
            @block.gpsimd
            def _(pool):
                def step(i, r):
                    s = 8 * i + r
                    if known(s) and s >= ITEMS:
                        for g in (2 * (s - ITEMS), 2 * (s - ITEMS) + 1):
                            if g < SUMMED:
                                pool.wait_ge(f2_added, ITEMS - GROUPS + g + 1)
                                x = group(mem["h"], g)
                                pool.tensor_tensor(x, x, group(X, g), ALU.add).then_inc(mem["summed"], 1)
                    new = not known(i) or i > 0
                    if new and r == 1 and live(s - 1):
                        pool.wait_ge(g_mm, 8 * i)
                        pool.wait_ge(t1_copied, 8 * i)
                        stand(pool, mem["passed"]["pool"])
                        pool.tensor_copy(wa[:], WA[:, i, :]).then_inc(took_a, 1)
                    if new and r == 3 and live(s - 3):
                        pool.wait_ge(gelued, 32 * i)
                        stand(pool, mem["passed"]["pool"])
                        pool.tensor_copy(wc[:], WC[:, i, :])
                        pool.tensor_copy(wb[:], WB[:, i, :]).then_inc(took_c, 1)
                    if known(s) and EARLY <= s + 1 < GROUPS:
                        ln0.root(pool, s + 1, (r + 1) % 2)
                    if live(s):
                        ln1.root(pool, s, r % 2)
                    if new and r == 3 and live(s - 3):
                        pool.wait_ge(f2_mm, 8 * i)
                        stand(pool, mem["passed"]["pool"])
                        pool.tensor_copy(wd[:], WD[:, i, :]).then_inc(took_d, 1)
                    if live(s - 3):
                        ln2.root(pool, s - 3, (r - 3) % 2)
                    if live(s - 1):
                        for j in range(2):
                            pool.wait_ge(rot_mul, 4 * (s - 1) + 2 * j + 2)
                            pool.tensor_tensor(QK[:, (r - 1) % 2, j], RA[:, j], RB[:, j], ALU.add
                                               ).then_inc(rotated, 1)
                    if live(s - 3):
                        pool.wait_ge(xn2_made, s - 2)
                        if new and r == 3:
                            pool.wait_ge(took_c, i)
                        x = group(X, r - 3)
                        pool.tensor_tensor(x, x, wb[:].unsqueeze(1).to_broadcast([TOK, 4, D]), ALU.add
                                           ).then_inc(b2_added, 1)
                    if live(s - 2):
                        pool.wait_ge(var_made, s - 1)
                        pool.tensor_tensor(vare[:, r % 2], var[:, r % 2], mem["eps"][0:TOK, :], ALU.add
                                           ).then_inc(vare_made, 1)
                        pool.wait_ge(vare_made, s - 1)
                        pool.tensor_tensor(grs[:, r % 2], vare[:, r % 2], mem["half_neg"][0:TOK, :], ALU.pow
                                           ).then_inc(grs_made, 1)
                    if known(s) and s >= ITEMS:
                        n = s - ITEMS
                        if n <= AHEAD:
                            mem["ln4"].root(pool, n, n % 2)
                        if n < AHEAD:
                            mem["ln4"].scale(pool, mem["xn4"][:, n], group(mem["h"], n), n, n, mem["normed4"],
                                             last_only=True, passed="pool")

                skewed(pool, step, ITEMS, 4, per=8)

            @block.vector
            def _(dve):
                def rest(g):
                    ln0.take(dve, at(h, 0, g, GROUPS), g, g % 2)
                    ln0.scale(dve, group(X, g), at(h, 0, g, GROUPS), g, g % 2, x0_made, last_only=True)

                def add_second(r, d):
                    dve.wait_ge(b2_added, d + 1)
                    dve.wait_ge(f2_mm, d + 1)
                    x = group(X, r - 4)
                    dve.tensor_tensor(x, psF[0:TOK, :].rearrange("p (k c) -> p k c", k=4), x, ALU.add
                                      ).then_inc(f2_added, 1)

                def step(i, r):
                    s = 8 * i + r
                    a, b, c, d = s - 1, s - 2, s - 3, s - 4
                    if known(s) and EARLY <= s + 1 < GROUPS:
                        rest(s + 1)
                    if live(s):
                        if known(i) and i == 0:
                            dve.wait_ge(x0_made, s + 1)
                        else:
                            dve.wait_ge(f2_added, s - 7)
                        ln1.take(dve, group(X, r), s, r % 2)
                    if live(c):
                        dve.wait_ge(grs_made, c + 1)
                        dve.tensor_tensor(Yn[:, (r - 3) % 2].rearrange("p k (g e) -> p (k g) e", e=HD),
                                          psV[0:TOK, :].rearrange("p (g e) -> p g e", e=HD),
                                          grs[:, (r - 3) % 2].unsqueeze(2).to_broadcast([TOK, 4 * HEADS, HD]), ALU.mult
                                          ).then_inc(yn_made, 1)
                    if live(s):
                        ln1.scale(dve, xn1[:, r % 2], group(X, r), s, r % 2, xn1_made, last_only=True)
                    draining = known(s) and s > ITEMS
                    if live(d) and not draining:
                        add_second(r, d)
                    if live(c):
                        dve.wait_ge(t2_copied, c + 1)
                        dve.scalar_tensor_tensor(U[:, (r - 3) % 2], SG[:, (r - 3) % 2], 0.5, YA[:, (r - 3) % 2],
                                                 ALU.mult, ALU.mult).then_inc(gated, 1)
                    if live(b):
                        for j in range(HEADS):
                            dve.wait_ge(a_mm, 4 * b + j + 1)
                            dve.tensor_tensor(AM[:, r % 2, j],
                                              wide[j][0:TOK, 0:COLS].rearrange("p (k q) -> p k q", k=4),
                                              decay[:, j, :].unsqueeze(1).to_broadcast([TOK, 4, TOK]), ALU.mult
                                              ).then_inc(masked, 1)
                    if live(c):
                        dve.wait_ge(wo_mm, c + 1)
                        x = group(X, r - 3)
                        dve.tensor_tensor(x, psG[0:TOK, :].rearrange("p (k c) -> p k c", k=4), x, ALU.add
                                          ).then_inc(wo_added, 1)
                        dve.wait_ge(wo_added, c + 1)
                        ln2.take(dve, x, c, (r - 3) % 2)
                    for j in range(4):
                        if j == 3 and live(c):
                            ln2.scale(dve, xn2[:, (r - 3) % 2], group(X, r - 3), c, (r - 3) % 2, xn2_made,
                                      last_only=True)
                        if live(a):
                            which, table = j // 2, ("cos" if j % 2 == 0 else "sin") + "qk"[j // 2]
                            if j % 2 == 0:
                                if positive(2 * (a - 1) + which + 1):
                                    dve.wait_ge(rotated, 2 * (a - 1) + which + 1)
                            dve.wait_ge(q_mm, 4 * a + j + 1)
                            dve.tensor_tensor(per_pos((RA, RB)[j % 2][:, which]), per_pos(wide[j][:, 0:COLS]),
                                              mem["c"](table).unsqueeze(1).to_broadcast([D, 8, NQ]), ALU.mult
                                              ).then_inc(rot_mul, 1)
                    if live(d) and draining:
                        add_second(r, d)
                    if known(s) and ITEMS <= s <= ITEMS + AHEAD:
                        n = s - ITEMS
                        dve.wait_ge(mem["summed"], n + 1)
                        if n > 1:
                            dve.wait_ge(mem["normed4"], n - 1)
                        mem["ln4"].take(dve, group(mem["h"], n), n, n % 2)
                    if live(b):
                        dve.wait_ge(squared, b + 1)
                        dve.tensor_reduce(var[:, r % 2].unsqueeze(2),
                                          SQ[:, r % 2].rearrange("p (g e) -> p g e", e=HD), AX.X, ALU.add
                                          ).then_inc(var_made, 1)
                    if live(a):
                        dve.wait_ge(tanhed, a + 1)
                        dve.scalar_tensor_tensor(SG[:, (r - 1) % 2], TH[:, (r - 1) % 2], 1.0, psG[:, 0:COLS],
                                                 ALU.add, ALU.mult).then_inc(sg_made, 1)

                skewed(dve, step, ITEMS, 4, per=8)

            @block.scalar
            def _(act):
                def step(i, r):
                    s = 8 * i + r
                    a, b, c = s - 1, s - 2, s - 3
                    if live(a):
                        if r == 1 and (not known(i) or i > 0):
                            act.wait_ge(took_a, i)
                        act.wait_ge(t1_mm, a + 1)
                        act.activation(XT1[:, (r - 1) % 2], psT[:, 0:COLS], ACT.Identity, bias=ln1_b, scale=ln1_w
                                       ).then_inc(t1_copied, 1)
                    if live(c):
                        if r == 3 and (not known(i) or i > 0):
                            act.wait_ge(took_c, i)
                        act.wait_ge(t2_mm, c + 1)
                        act.activation(YA[:, (r - 3) % 2], psT[:, 0:COLS], ACT.Identity, bias=gn_b, scale=gn_w
                                       ).then_inc(t2_copied, 1)
                    if live(a):
                        act.wait_ge(v_mm, a + 1)
                        act.activation(V[:, (r - 1) % 2].rearrange("p k c -> p (k c)"), psV[0:TOK, :], ACT.Copy
                                       ).then_inc(v_copied, 1)
                    if live(c):
                        act.wait_ge(t3_mm, c + 1)
                        act.activation(XT3[:, (r - 3) % 2], psT[:, 0:COLS], ACT.Identity, bias=ln2_b, scale=ln2_w
                                       ).then_inc(t3_copied, 1)
                    if live(b):
                        act.wait_ge(y_mm, b + 1)
                        act.activation(SQ[:, r % 2], psV[0:TOK, :], ACT.Square, scale=HD ** -0.5
                                       ).then_inc(squared, 1)
                    if live(a):
                        act.wait_ge(g_mm, a + 1)
                        act.activation(TH[:, (r - 1) % 2], psG[:, 0:COLS], ACT.Tanh, scale=0.5).then_inc(tanhed, 1)
                    if live(c):
                        for j in range(FB):
                            act.wait_ge(f1_mm, 4 * c + j + 1)
                            act.activation(HID[:, (r - 3) % 2, j], wide[j][:, 0:COLS], ACT.Gelu, bias=b1[:, j:j + 1]
                                           ).then_inc(gelued, 1)

                skewed(act, step, ITEMS, 4, per=8)

            @block.tensor
            def _(pe):
                def turn(src, slot, done):
                    for k in range(4):
                        ins = pe.transpose(psT[:, k * TOK:(k + 1) * TOK], src[:, slot, k, :], ident[0:TOK, 0:TOK])
                    ins.then_inc(done, 1)

                def second(i, r, d):
                    if r == 4 and (not known(i) or i > 0):
                        pe.wait_ge(took_d, i)
                    pe.wait_ge(gelued, 4 * d + 4)
                    if positive(d):
                        pe.wait_ge(f2_added, d)
                    for k in range(4):
                        for j in range(FB):
                            ins = pe.matmul(psF[0:TOK, k * D:(k + 1) * D],
                                            HID[:, (r - 4) % 2, j, k * TOK:(k + 1) * TOK],
                                            wd[:, j * D:(j + 1) * D], start=(j == 0), stop=(j == FB - 1))
                    ins.then_inc(f2_mm, 1)

                def weigh_values(r, tiles):
                    for k in tiles:
                        for j in range(HEADS):
                            ins = pe.matmul(psV[0:TOK, k * D + j * HD:k * D + (j + 1) * HD],
                                            AM[:, r % 2, j, k, :], V[:, r % 2, k, j * HD:(j + 1) * HD],
                                            start=True, stop=True)
                    return ins

                def step(i, r):
                    s = 8 * i + r
                    a, b, c, d = s - 1, s - 2, s - 3, s - 4
                    if live(a):
                        if positive(c):
                            pe.wait_ge(t3_copied, c)
                        elif positive(a):
                            pe.wait_ge(t1_copied, a)
                        pe.wait_ge(xn1_made, a + 1)
                        turn(xn1, (r - 1) % 2, t1_mm)
                    draining = known(s) and s > ITEMS
                    if live(d) and not draining:
                        second(i, r, d)
                    if live(c):
                        if live(a):
                            pe.wait_ge(t1_copied, a + 1)
                        elif positive(c):
                            pe.wait_ge(t3_copied, c)
                        pe.wait_ge(yn_made, c + 1)
                        turn(Yn, (r - 3) % 2, t2_mm)
                    if live(b):
                        pe.wait_ge(rotated, 2 * b + 2)
                        for j in range(HEADS):
                            if positive(4 * (c - 1) + j + 1):
                                pe.wait_ge(gelued, 4 * (c - 1) + j + 1)
                            pe.wait_ge(rot_mul, 4 * b + j + 1)
                            rows = slice(j * HD, (j + 1) * HD)
                            for k in range(4):
                                cols = slice(k * TOK, (k + 1) * TOK)
                                ins = pe.matmul(wide[j][0:TOK, cols], QK[rows, r % 2, 1, cols], QK[rows, r % 2, 0, cols],
                                                start=True, stop=True)
                            ins.then_inc(a_mm, 1)
                    if live(c):
                        if r == 3 and (not known(i) or i > 0):
                            pe.wait_ge(took_c, i)
                        if live(b):
                            pe.wait_ge(sg_made, b + 1)
                        pe.wait_ge(gated, c + 1)
                        for k in range(4):
                            ins = pe.matmul(psG[0:TOK, k * D:(k + 1) * D], U[:, (r - 3) % 2, k * TOK:(k + 1) * TOK], wo,
                                            start=True, stop=True)
                        ins.then_inc(wo_mm, 1)
                    if live(d) and draining:
                        second(i, r, d)
                    if live(a):
                        if r == 1 and (not known(i) or i > 0):
                            pe.wait_ge(took_a, i)
                        pe.wait_ge(t1_copied, a + 1)
                        if positive(c + 1):
                            pe.wait_ge(yn_made, c + 1)
                        elif positive(a):
                            pe.wait_ge(v_copied, a)
                        for k in range(4):
                            ins = pe.matmul(psV[0:TOK, k * D:(k + 1) * D], XT1[:, (r - 1) % 2, k * TOK:(k + 1) * TOK],
                                            wq[:, 4 * D:5 * D], start=True, stop=True)
                        ins.then_inc(v_mm, 1)
                        for j in range(4):
                            if live(b):
                                pe.wait_ge(masked, 4 * b + j + 1)
                            else:
                                if positive(4 * (a - 1) + j + 1):
                                    pe.wait_ge(rot_mul, 4 * (a - 1) + j + 1)
                            pe.matmul(wide[j][:, 0:COLS], wq[:, j * D:(j + 1) * D], XT1[:, (r - 1) % 2],
                                      start=True, stop=True).then_inc(q_mm, 1)
                    if live(b):
                        pe.wait_ge(masked, 4 * b + 4)
                        if live(a):
                            pe.wait_ge(v_copied, a + 1)
                        elif positive(c + 1):
                            pe.wait_ge(yn_made, c + 1)
                        weigh_values(r, (0, 1, 2))
                    if live(c):
                        pe.wait_ge(t2_copied, c + 1)
                        pe.wait_ge(xn2_made, c + 1)
                        turn(xn2, (r - 3) % 2, t3_mm)
                    if live(b):
                        weigh_values(r, (3,)).then_inc(y_mm, 1)
                    if live(a):
                        if live(c):
                            pe.wait_ge(wo_added, c + 1)
                        else:
                            if positive(a):
                                pe.wait_ge(sg_made, a)
                        pe.matmul(psG[:, 0:COLS], wq[:, 5 * D:6 * D], XT1[:, (r - 1) % 2], start=True, stop=True
                                  ).then_inc(g_mm, 1)
                    if live(c):
                        pe.wait_ge(t3_copied, c + 1)
                        for j in range(FB):
                            if live(a):
                                pe.wait_ge(rot_mul, 4 * a + j + 1)
                            elif live(b):
                                pe.wait_ge(masked, 4 * b + j + 1)
                            else:
                                pe.wait_ge(gelued, 4 * (c - 1) + j + 1)
                            pe.matmul(wide[j][:, 0:COLS], w1[:, j * D:(j + 1) * D], XT3[:, (r - 3) % 2],
                                      start=True, stop=True).then_inc(f1_mm, 1)

                skewed(pe, step, ITEMS, 4, per=8)


NR, CAP = 64, 128


def routed_network(nc, ctx, io, mem):
    COLS = 4 * TOK
    with ExitStack() as here:
        def sb(name, shape, dt=F32):
            return here.enter_context(nc.sbuf_tensor(name, shape, dt))

        def sem(name):
            return here.enter_context(nc.semaphore(name))

        def bank(name):
            return here.enter_context(nc.psum_tensor(name, [128, BANK], F32))

        W = mem["w4"]
        ln, xn, XT = mem["ln4"], mem["xn4"], sb("c_XT", [D, 2, COLS])
        HID = sb("c_HID", [128, 2, FB, COLS])
        R4 = [TOK, 2, 4, NR]
        LG, SH, EX, C1, C2, OH1, OH2, S2, D2, KE, KX = (
            sb("c_" + n, R4) for n in ("LG", "SH", "EX", "C1", "C2", "OH1", "OH2", "S2", "D2", "KE", "KX"))
        M = sb("c_M", R4, BF16)
        chosen = sb("chosen", [TOK, NR])
        before_all = sb("before_all", [TOK, 2, NR], BF16)
        m1, b1, m2, b2, total, inverse, kept, weight = (
            sb("c_" + n, [TOK, 2, 4]) for n in ("m1", "b1", "m2", "b2", "total", "inverse", "kept", "weight"))
        YW, OUT = sb("YW", [TOK, 2, 4, D]), sb("OUT", [TOK, 2, 4, D])
        psX, psL, psP, psY = bank("c_psX"), bank("c_psL"), bank("c_psP"), bank("c_psY")
        wide = [bank(f"c_wide{j}") for j in range(FB)]

        summed, normed, x_mm, x_copied = mem["summed"], mem["normed4"], sem("c_x_mm"), sem("c_x_copied")
        l_mm, sh_made, ex_made = sem("c_l_mm"), sem("c_sh_made"), sem("c_ex_made")
        ROUTE = 12
        route = sem("c_route")
        keep, kx_made = sem("keep"), sem("kx_made")
        m_made, prior_made, p_mm = sem("m_made"), sem("prior_made"), sem("c_p_mm")
        f1_mm, gelued = sem("c_f1_mm"), sem("c_gelued")
        f2_mm, y_scaled, out_made = sem("c_f2_mm"), sem("y_scaled"), sem("out_made")
        stored = mem["stored"]
        h, X = group_view(mem["h"], 2), group_view(mem["X"], 2)
        ident = mem["c"]("ident")
        one = mem["c"]("sel", 1)[:, 0:TOK]
        live = lambda g: not known(g) or 0 <= g < GROUPS
        out = io["out"].rearrange("(i r k a) q d -> i r (a q) k d", r=2, k=4, a=2)

        with nc.Block() as block:
            @block.sync
            def _(sp):
                def step(i, r):
                    s = 2 * i + r
                    if live(s - 3):
                        sp.wait_ge(out_made, s - 2)
                        stand(sp, mem["passed"]["sp"])
                        sp.dma_start(out[i + (r - 3) // 2, (r - 3) % 2], OUT[:, (r - 3) % 2]
                                     ).then_inc(stored[(r - 3) % 2], 16)

                skewed(sp, step, GROUPS, 3, peel=2)
                for j in range(2):
                    sp.wait_ge(stored[j], 16 * GROUPS // 2)

            @block.gpsimd
            def _(pool):
                def step(i, r):
                    s = 2 * i + r
                    if live(s - 2):
                        o = r % 2
                        pool.wait_ge(keep, 3 * (s - 2) + 1)
                        pool.tensor_tensor(KX[:, o], KE[:, o], EX[:, o], ALU.mult).then_inc(kx_made, 1)
                    if live(s - 3):
                        o = (r - 3) % 2
                        if positive(16 * (i + (r - 3) // 2)):
                            pool.wait_ge(stored[o], 16 * (i + (r - 3) // 2))
                        pool.wait_ge(y_scaled, s - 2)
                        pool.tensor_tensor(OUT[:, o], YW[:, o], at(h, i, r - 3, 2), ALU.add).then_inc(out_made, 1)
                    if live(s) and not (known(s) and s < AHEAD):
                        pool.wait_ge(x_mm, s - 1)
                        ln.scale(pool, xn[:, r % 2], at(h, i, r, 2), s, r % 2, normed, last_only=True, passed="pool")
                    if live(s - 1):
                        o = (r - 1) % 2
                        pool.wait_ge(route, ROUTE * (s - 1) + 10)
                        pool.tensor_tensor(M[:, o], OH1[:, o], OH2[:, o], ALU.add).then_inc(m_made, 1)
                    if live(s + 1) and not (known(s) and s < AHEAD):
                        ln.root(pool, s + 1, (r + 1) % 2)

                x = at(h, 0, SUMMED, 2)
                pool.tensor_tensor(x, x, at(X, 0, SUMMED, 2), ALU.add).then_inc(summed, 1)
                skewed(pool, step, GROUPS, 3, peel=2)

            @block.vector
            def _(dve):
                def own(ins, g, j):
                    ins.then_inc(route, 1)
                    dve.wait_ge(route, ROUTE * g + j)

                def over(a):
                    return a.unsqueeze(2).to_broadcast([TOK, 4, NR])

                def shifted(g, o):
                    dve.wait_ge(l_mm, g + 1)
                    own(dve.tensor_reduce(m1[:, o].unsqueeze(2), psL[0:TOK, 0:4 * NR].rearrange("p (k e) -> p k e", k=4),
                                          AX.X, ALU.max), g, 1)
                    dve.tensor_tensor(SH[:, o], psL[0:TOK, 0:4 * NR].rearrange("p (k e) -> p k e", k=4), over(m1[:, o]),
                                      ALU.subtract).then_inc(sh_made, 1)

                def choose(g, o):
                    rank = mem["c"]("rank64", TOK).unsqueeze(1).to_broadcast([TOK, 4, NR])
                    dve.wait_ge(sh_made, g + 1)
                    own(dve.scalar_tensor_tensor(C1[:, o], SH[:, o], 0.0, rank, ALU.is_ge, ALU.mult), g, 2)
                    own(dve.tensor_reduce(b1[:, o].unsqueeze(2), C1[:, o], AX.X, ALU.max), g, 3)
                    own(dve.tensor_tensor(OH1[:, o], C1[:, o], over(b1[:, o]), ALU.is_equal), g, 4)
                    own(dve.scalar_tensor_tensor(S2[:, o], OH1[:, o], LOWEST, SH[:, o], ALU.mult, ALU.add), g, 5)
                    own(dve.tensor_reduce(m2[:, o].unsqueeze(2), S2[:, o], AX.X, ALU.max), g, 6)
                    own(dve.tensor_tensor(D2[:, o], S2[:, o], over(m2[:, o]), ALU.subtract), g, 7)
                    own(dve.scalar_tensor_tensor(C2[:, o], D2[:, o], 0.0, rank, ALU.is_ge, ALU.mult), g, 8)
                    own(dve.tensor_reduce(b2[:, o].unsqueeze(2), C2[:, o], AX.X, ALU.max), g, 9)
                    dve.tensor_tensor(OH2[:, o], C2[:, o], over(b2[:, o]), ALU.is_equal).then_inc(route, 1)

                def count(g, o):
                    dve.wait_ge(ex_made, g + 1)
                    own(dve.tensor_reduce(total[:, o].unsqueeze(2), EX[:, o], AX.X, ALU.add), g, 11)
                    dve.reciprocal(inverse[:, o], total[:, o])
                    dve.wait_ge(m_made, g + 1)
                    own(dve.tensor_reduce(chosen[:].unsqueeze(2), M[:, o].rearrange("p k e -> p e k"), AX.X, ALU.add),
                        g, 12)
                    dve.tensor_tensor(before_all[:, 1 - o], before_all[:, o], chosen[:], ALU.add).then_inc(prior_made, 1)

                def step(i, r):
                    s = 2 * i + r
                    g, o = s - 2, r % 2
                    if live(g):
                        dve.wait_ge(p_mm, g + 1)
                        dve.scalar_tensor_tensor(KE[:, o], psP[0:TOK, 0:4 * NR].rearrange("p (k e) -> p k e", k=4),
                                                 float(CAP), M[:, o], ALU.is_lt, ALU.mult).then_inc(keep, 1)
                    if live(s - 1):
                        shifted(s - 1, (r - 1) % 2)
                    if live(s + 1) and not (known(s) and s < AHEAD):
                        dve.wait_ge(summed, s + 2)
                        dve.wait_ge(normed, s)
                        stand(dve, mem["passed"]["dve"])
                        ln.take(dve, at(h, i, r + 1, 2), s + 1, (r + 1) % 2)
                    if live(g):
                        dve.wait_ge(kx_made, g + 1)
                        dve.tensor_reduce(kept[:, o].unsqueeze(2), KX[:, o], AX.X, ALU.add).then_inc(keep, 1)
                        dve.wait_ge(keep, 3 * g + 2)
                        dve.tensor_tensor(weight[:, o], kept[:, o], inverse[:, o], ALU.mult).then_inc(keep, 1)
                    if live(s - 1):
                        choose(s - 1, (r - 1) % 2)
                        count(s - 1, (r - 1) % 2)

                dve.memset(before_all[:, 0], 0.0).then_inc(prior_made, 1)
                dve.wait_ge(prior_made, 1)
                skewed(dve, step, GROUPS, 3, peel=2)

            @block.scalar
            def _(act):
                def step(i, r):
                    s = 2 * i + r
                    if live(s - 1):
                        o = (r - 1) % 2
                        act.wait_ge(x_mm, s)
                        act.activation(XT[:, o], psX[:, 0:COLS], ACT.Copy).then_inc(x_copied, 1)
                    if live(s - 3):
                        g, w = s - 3, (r - 3) % 2
                        act.wait_ge(keep, 3 * g + 3)
                        act.wait_ge(f2_mm, g + 1)
                        for k in range(4):
                            ins = act.activation(YW[:, w, k], psY[0:TOK, k * D:(k + 1) * D], ACT.Copy,
                                                 scale=weight[:, w, k:k + 1])
                        ins.then_inc(y_scaled, 1)
                    if live(s - 1):
                        act.wait_ge(sh_made, s)
                        act.activation(EX[:, o], SH[:, o], ACT.Exp).then_inc(ex_made, 1)
                        for j in range(FB):
                            act.wait_ge(f1_mm, 4 * (s - 1) + j + 1)
                            act.activation(HID[:, o, j], wide[j][:, 0:COLS], ACT.Gelu, bias=W["b1"][:, j:j + 1]
                                           ).then_inc(gelued, 1)

                skewed(act, step, GROUPS, 3, peel=2)

            @block.tensor
            def _(pe):
                def step(i, r):
                    s = 2 * i + r
                    o, a, g = r % 2, (r - 1) % 2, s - 2
                    if live(s - 1):
                        if positive(s - 1):
                            pe.wait_ge(x_copied, s - 1)
                        pe.wait_ge(normed, s)
                        for k in range(4):
                            ins = pe.transpose(psX[:, k * TOK:(k + 1) * TOK], xn[:, a, k, :], ident[0:TOK, 0:TOK])
                        ins.then_inc(x_mm, 1)
                    if live(g):
                        pe.wait_ge(m_made, g + 1)
                        pe.wait_ge(prior_made, g + 1)
                        if positive(3 * (g - 1) + 1):
                            pe.wait_ge(keep, 3 * (g - 1) + 1)
                        for k in range(4):
                            parts = [(mem["ones_bf"][:], before_all[:, o])]
                            parts += [(mem["ones_bf"][:], M[:, o, j]) for j in range(k)]
                            parts += [(mem["before_bf"][:], M[:, o, k])]
                            for n, (left, right) in enumerate(parts):
                                ins = pe.matmul(psP[0:TOK, k * NR:(k + 1) * NR], left, right, start=(n == 0),
                                                stop=(n == len(parts) - 1))
                        ins.then_inc(p_mm, 1)
                    if live(s - 1):
                        pe.wait_ge(x_copied, s)
                        if positive(s - 1):
                            pe.wait_ge(sh_made, s - 1)
                        for k in range(4):
                            ins = pe.matmul(psL[0:TOK, k * NR:(k + 1) * NR], XT[:, a, k * TOK:(k + 1) * TOK], W["wr"][:],
                                            start=True, stop=True)
                        ins.then_inc(l_mm, 1)
                        for j in range(FB):
                            if positive(4 * (s - 2) + j + 1):
                                pe.wait_ge(gelued, 4 * (s - 2) + j + 1)
                            pe.matmul(wide[j][:, 0:COLS], W["w1"][:, j * D:(j + 1) * D], XT[:, a], start=True, stop=True
                                      ).then_inc(f1_mm, 1)
                    if live(g):
                        pe.wait_ge(gelued, 4 * g + 4)
                        if positive(g):
                            pe.wait_ge(y_scaled, g)
                        for k in range(4):
                            for j in range(FB):
                                pe.matmul(psY[0:TOK, k * D:(k + 1) * D], HID[:, o, j, k * TOK:(k + 1) * TOK],
                                          W["w2"][:, j, :], start=(j == 0), stop=False)
                            ins = pe.matmul(psY[0:TOK, k * D:(k + 1) * D], one, W["b2"][0:1, :], start=False, stop=True)
                        ins.then_inc(f2_mm, 1)

                skewed(pe, step, GROUPS, 3, peel=2)


def store(nc, ctx, io, mem, src):
    with nc.semaphore("stored") as stored, nc.Block() as block:
        @block.sync
        def _(sp):
            sp.dma_start(io["out"].rearrange("(t a) q d -> (a q) t d", a=2), src[:]).then_inc(stored, 16)
            sp.wait_ge(stored, 16)


STAGE = 4


def tower(nc, io):
    with ExitStack() as ctx:
        def sb(name, shape, dt=F32):
            return ctx.enter_context(nc.sbuf_tensor(name, shape, dt))

        mem = {"h": sb("h", [TOK, TILES, D]), "consts": sb("consts", [128, CONST_ARRAY.shape[1]]),
               "ones_bf": sb("ones_bf", [TOK, TOK], BF16), "before_bf": sb("before_bf", [TOK, TOK], BF16),
               "half_neg": sb("half_neg", [128, 16]), "eps": sb("eps", [128, 16])}

        def c(name, parts=128):
            a, b = CONSTS[name]
            return mem["consts"][0:parts, a:b]

        mem["c"] = c
        mem["bias_in"] = ctx.enter_context(nc.semaphore("bias_in"))
        mem["passed"] = {k: ctx.enter_context(nc.semaphore("passed_" + k)) for k in ("dve", "sp", "pool", "act")}
        mem["stored"] = [ctx.enter_context(nc.semaphore(f"stored{i}")) for i in range(2)]
        mem["ones_set"] = ctx.enter_context(nc.semaphore("ones_set"))
        mem["w1"] = {"qkv": sb("w1_qkv", [D, 3, 512]), "o": sb("w1_o", [128, 4, D])}
        mem["w2"] = {"wr": sb("w2_wr", [D, NE]), "br": sb("w2_br", [TOK, NE]), "w1": sb("w2_w1", [D, NE, D]),
                     "b1": sb("w2_b1", [D, NE]), "w2": sb("w2_w2", [D, NE, D]), "b2": sb("w2_b2", [NE, D])}
        mem["sel_bf"] = sb("sel_bf", [NE, NE, D], BF16)
        mem["later_in"] = ctx.enter_context(nc.semaphore("later_in"))
        mem["xT_in"], mem["xtok_in"] = [[ctx.enter_context(nc.semaphore(f"{n}{j}")) for j in range(2)]
                                        for n in ("xT_in", "xtok_in")]
        with ExitStack() as first:
            def sb1(name, shape):
                return first.enter_context(nc.sbuf_tensor(name, shape, F32))

            mem.update(WpT=sb1("WpT", [128, 6, D]), VT=sb1("VT", [128, H0, VD + 1]),
                       BT=[first.enter_context(nc.sbuf_tensor(f"BT_{part}", [AUG, H0, AUG], F32R))
                           for part in ("high", "low")],
                       bias=sb1("bias", [TOK, PAIRS, N]),
                       bias3=first.enter_context(nc.sbuf_tensor("bias3", [TOK, 3 * PAIRS, N], BF16)),
                       xtok=sb1("xtok", [HALF, 2, 4, 2, AUG]),
                       xT=sb1("xT", [AUG, 2, 4, N]), proj_c=sb1("proj_c", [TOK, D]), half=sb1("half", [TOK, 1]))
            setup(nc, ctx, io, mem)
            token_attention(nc, ctx, io, mem)
        mem["ret_a"] = sb("ret_a", [D, LAYERS, 6 * D + 2])
        mem["ret_c"] = sb("ret_c", [D, LAYERS, 8 + 5 * D])
        mem["ret_d"] = sb("ret_d", [D, LAYERS, FB * D])
        mem["ret_b2"] = sb("ret_b2", [TOK, LAYERS, D])
        mem["w4"] = {"wr": sb("w4_wr", [D, NR]), "w1": sb("w4_w1", [D, FB * D]), "b1": sb("w4_b1", [D, FB]),
                     "w2": sb("w4_w2", [D, FB, D]), "b2": sb("w4_b2", [TOK, D])}
        if STAGE >= 1:
            head_attention(nc, ctx, io, mem)
        mem["X"] = sb("X", [TOK, TILES, D])
        mem["ln0"] = Norm(nc, ctx, "ln_0", mem)
        mem["x0_made"] = ctx.enter_context(nc.semaphore("x0_made"))
        mem["work"] = [(sb("wa", [D, 6 * D + 2]), mem["ret_a"]), (sb("wc", [D, 8 + D + 4 * D]), mem["ret_c"]),
                       (sb("wd", [D, FB * D]), mem["ret_d"]), (sb("wb", [TOK, D]), mem["ret_b2"])]
        mem["ln4"], mem["xn4"] = Norm(nc, ctx, "ln_c", mem), sb("c_xn", [TOK, 2, 4, D])
        mem["summed"], mem["normed4"] = [ctx.enter_context(nc.semaphore(n)) for n in ("summed", "c_normed")]
        if STAGE >= 2:
            top1_experts(nc, ctx, io, mem)
        if STAGE >= 3:
            retention(nc, ctx, io, mem)
        if STAGE >= 4:
            routed_network(nc, ctx, io, mem)
        else:
            store(nc, ctx, io, mem, mem["X"] if STAGE == 3 else mem["h"])


def kernel(**inputs):
    import numpy as _np
    import concourse.bacc as _bacc
    from concourse import mybir as _mybir
    from concourse.bass_utils import run_bass_kernel_spmd as _run

    a = {k: _np.asarray(v) for k, v in inputs.items()}
    halves = lambda v: v.reshape(v.shape[:-1] + (HALF, 2)).swapaxes(-1, -2)
    laid = {
        "x": a["x"],
        "xT": halves(a["x"].transpose(2, 0, 1)).reshape(D_IN, B, N),
        "kv_w": a["L0_tok_kv_w"], "q_w": a["L0_tok_q_w"], "projT": a["L0_tok_proj_w"].T,
        "ab": a["L0_tok_attention_biases"].T, "idx": halves(a["L0_tok_bias_idxs"]),
        "consts": CONST_ARRAY,
    }
    for w in "qkv":
        laid["a_" + w] = a[f"L0_attn_W_{w.upper()}"].transpose(2, 0, 1).reshape(D, 512)
    laid["b_wr"], laid["b_br"], laid["b_b2"] = a["L0_ffn_Wr"], a["L0_ffn_br"], a["L0_ffn_b2"]
    laid["b_w1"] = a["L0_ffn_W1"].transpose(1, 0, 2)
    laid["b_w2"] = a["L0_ffn_W2"].transpose(1, 0, 2)
    laid["b_b1"] = a["L0_ffn_b1"].T
    r = {k[8:]: v for k, v in a.items() if k.startswith("L1_attn_")}
    flat = lambda v: v.transpose(2, 0, 1, 3).reshape(D, LAYERS, D)
    swap = lambda v: v.reshape(v.shape[:-1] + (-1, 2))[..., ::-1].reshape(v.shape)
    laid["r_wq"], laid["r_wk"], laid["r_wv"] = flat(r["WQ"]), flat(r["WK"]), flat(r["WV"])
    laid["r_wqs"], laid["r_wks"] = swap(laid["r_wq"]), swap(laid["r_wk"])
    laid["r_wg"], laid["r_wo"] = r["WG"].transpose(1, 0, 2), r["WO"].transpose(1, 0, 2)
    laid["r_ln1"] = _np.stack([r["ln1_w"], r["ln1_b"]], -1).transpose(1, 0, 2)
    laid["r_small"] = _np.concatenate(
        [_np.stack([r["gn_w"], r["gn_b"], r["ln2_w"], r["ln2_b"]], -1).transpose(1, 0, 2),
         r["ffn_b1"].reshape(LAYERS, FB, D).transpose(2, 0, 1)], -1)
    laid["r_w1"] = r["ffn_w1"].transpose(1, 0, 2)
    laid["r_w2"] = r["ffn_w2"].reshape(LAYERS, FB, D, D).transpose(2, 0, 1, 3).reshape(D, LAYERS, FB * D)
    laid["r_b2"] = r["ffn_b2"]
    laid["c_wr"], laid["c_w1"] = a["L1_ffn_router_w"].T, a["L1_ffn_w1"].T
    laid["c_b1"] = a["L1_ffn_b1"].reshape(FB, D).T
    laid["c_w2"] = a["L1_ffn_w2"].T.reshape(FB, D, D).transpose(1, 0, 2)
    laid["c_b2"] = a["L1_ffn_b2"]
    laid["a_o"] = a["L0_attn_W_O"].T
    for w in ("kv", "q", "proj"):
        four = _np.stack([a[f"L0_tok_{w}_{k}"] for k in "gbmv"])
        laid[w + "_bn"] = four.T if w == "proj" else four.reshape(4, H0, -1).transpose(2, 0, 1)
    nc = _bacc.Bacc("TRN2", target_bir_lowering=False, num_devices=1)
    io, arrays = {}, {}
    for name, v in laid.items():
        v = _np.ascontiguousarray(v)
        arrays["in_" + name] = v
        io[name] = nc.dram_tensor("in_" + name, v.shape, _mybir.dt.from_np(v.dtype), kind="ExternalInput").ap()
    io["out"] = nc.dram_tensor("out", (B, NQ, D), F32, kind="ExternalOutput").ap()
    tower(nc, io)
    r = _run(nc, [arrays], core_ids=[0])
    return r.results[0]["out"]
```
